# Optimizing a Trainium2 kernel written in Bass

```python
import numpy as np
import jax
import jax.numpy as jnp

def _softmax(x, axis=-1):
    return jax.nn.softmax(x, axis=axis)

def _gelu(x):
    return jax.nn.gelu(x, approximate=True)

def _silu(x):
    return jax.nn.silu(x)

def _sigmoid(x):
    return jax.nn.sigmoid(x)

def _layernorm(x, axis=-1, eps=1e-05):
    m = jnp.mean(x, axis=axis, keepdims=True)
    v = jnp.var(x, axis=axis, keepdims=True)
    return (x - m) / jnp.sqrt(v + eps)

def _scatter_add(tgt, idx, src, axis=0):
    return tgt.at[idx].add(src)

def _segment_sum(src, seg, n):
    return jax.ops.segment_sum(src, seg, n)
kernel_name = 'mk_decoder_preln_d4_seqx_r8_226936'

def setup_inputs(seed: int=0):
    np.random.seed(seed)
    _w = jnp.asarray

    def _rec_inputs():
        import jax
        import jax.numpy as jnp
        _rk = jax.random.key(seed)
        x = 0.0002417 + 0.9998 * jax.random.normal(jax.random.fold_in(_rk, 1), (32, 128, 128), jnp.float32)
        _lenS = 128 - jax.random.randint(jax.random.fold_in(_rk, 7), (32,), 0, max(1, 128 // 4) + 1, jnp.int32)
        _lenS2 = 77 - jax.random.randint(jax.random.fold_in(_rk, 8), (32,), 0, max(1, 77 // 4) + 1, jnp.int32)
        _ctx_1024P = jax.random.normal(jax.random.fold_in(_rk, 11), (32, 16, 128), jnp.float32)
        _ctx_1024c = jax.random.dirichlet(jax.random.fold_in(_rk, 511), 0.3 * jnp.ones((16,), jnp.float32), (32, 77))
        _ctx_1024t = jnp.einsum('bsk,bkd->bsd', _ctx_1024c, _ctx_1024P)
        _ctx_1024t = _ctx_1024t * jax.lax.rsqrt(jnp.mean(jnp.square(_ctx_1024t)) + 1e-12) * 0.953939
        ctx_1024 = 7.22013e-05 + 1.00017 * (_ctx_1024t + 0.3 * jax.random.normal(jax.random.fold_in(_rk, 611), (32, 77, 128), jnp.float32))
        _validS = jnp.arange(128)[None, :] < _lenS[:, None]
        _validS2 = jnp.arange(77)[None, :] < _lenS2[:, None]
        _causal = jnp.tril(jnp.ones((128, 128), dtype=bool))
        mask_BxS2_bk0 = jnp.logical_not(jnp.broadcast_to(_validS2[:, :], (32, 77)))
        return (x, ctx_1024, mask_BxS2_bk0)
    x, ctx_1024, mask_BxS2_bk0 = _rec_inputs()

    def _L0_attn_setup():
        import jax, jax.numpy as jnp
        import numpy as np
        D_MODEL = 128
        N_HEADS = 16
        D_HEAD = D_MODEL // N_HEADS
        EPS = 1e-06

        def _phi(x):
            return jax.nn.elu(x) + 1.0
        key = jax.random.key(seed)
        k1, k2, k3 = jax.random.split(key, 3)
        x = jax.random.normal(k1, (4, 512, D_MODEL), dtype=jnp.float32)
        s = 1.0 / np.sqrt(D_MODEL)
        w_qkv = jax.random.uniform(k2, (3 * D_MODEL, D_MODEL), minval=-s, maxval=s, dtype=jnp.float32)
        w_out = jax.random.uniform(k3, (D_MODEL, D_MODEL), minval=-s, maxval=s, dtype=jnp.float32)
        return {'x': x, 'w_qkv': w_qkv, 'w_out': w_out}
    _L0_attn_all = _L0_attn_setup()
    _L0_attn_in = {k: v for k, v in _L0_attn_all.items() if k in ('w_qkv', 'w_out')}
    del _L0_attn_all

    def _L0_xattn_setup():
        import jax, jax.numpy as jnp
        import numpy as np
        D_MODEL = 128
        B, S = (4, 256)
        key = jax.random.key(seed)
        ks = jax.random.split(key, 10)
        s = 1.0 / np.sqrt(D_MODEL)
        return {'k': jax.random.normal(ks[0], (B, S, D_MODEL), jnp.float32), 'v': jax.random.normal(ks[1], (B, S, D_MODEL), jnp.float32), 'q': jax.random.normal(ks[2], (B, S, D_MODEL), jnp.float32), 'Wk': jax.random.normal(ks[3], (D_MODEL, D_MODEL), jnp.float32) * s, 'Wv': jax.random.normal(ks[4], (D_MODEL, D_MODEL), jnp.float32) * s, 'bv': jnp.zeros((D_MODEL,), jnp.float32), 'Wq': jax.random.normal(ks[5], (D_MODEL, D_MODEL), jnp.float32) * s, 'bq': jnp.zeros((D_MODEL,), jnp.float32), 'Wo': jax.random.normal(ks[6], (D_MODEL, D_MODEL), jnp.float32) * s, 'bo': jnp.zeros((D_MODEL,), jnp.float32)}
    _L0_xattn_all = _L0_xattn_setup()
    _L0_xattn_in = {k: v for k, v in _L0_xattn_all.items() if k in ('Wk', 'Wv', 'bv', 'Wq', 'bq', 'Wo', 'bo')}
    del _L0_xattn_all

    def _L0_ffn_setup():
        import jax, jax.numpy as jnp
        import numpy as np
        TOP_K = 2
        key = jax.random.key(seed)
        k1, k2, k3, k4, k5 = jax.random.split(key, 5)
        B, S, D, F, E = (2, 128, 128, 256, 8)
        return {'x': jax.random.normal(k1, (B, S, D), dtype=jnp.float32), 'router_kernel_DE': jax.random.normal(k2, (D, E), dtype=jnp.float32) * 0.02, 'kernel_gating_EDF': jax.random.normal(k3, (E, D, F), dtype=jnp.float32) * 0.02, 'kernel_up_EDF': jax.random.normal(k4, (E, D, F), dtype=jnp.float32) * 0.02, 'kernel_down_EFD': jax.random.normal(k5, (E, F, D), dtype=jnp.float32) * 0.02}
    _L0_ffn_all = _L0_ffn_setup()
    _L0_ffn_in = {k: v for k, v in _L0_ffn_all.items() if k in ('router_kernel_DE', 'kernel_gating_EDF', 'kernel_up_EDF', 'kernel_down_EFD')}
    del _L0_ffn_all

    def _L1_attn_setup():
        import jax, jax.numpy as jnp
        import numpy as np
        B, M, D, H, K, V = (4, 256, 128, 16, 64, 64)
        key = jax.random.key(seed)
        ks = jax.random.split(key, 5)
        return {'x': jax.random.normal(ks[0], (B, M, D), dtype=jnp.float32), 'P_q': jax.random.normal(ks[1], (H, D, K), dtype=jnp.float32) * 0.02, 'P_k': jax.random.normal(ks[2], (H, D, K), dtype=jnp.float32) * 0.02, 'P_v': jax.random.normal(ks[3], (H, D, V), dtype=jnp.float32) * 0.02, 'P_o': jax.random.normal(ks[4], (H, D, V), dtype=jnp.float32) * 0.02}
    _L1_attn_all = _L1_attn_setup()
    _L1_attn_in = {k: v for k, v in _L1_attn_all.items() if k in ('P_q', 'P_k', 'P_v', 'P_o')}
    del _L1_attn_all

    def _L1_xattn_setup():
        import math
        import jax, jax.numpy as jnp
        import numpy as np
        B, S, D, H = (2, 256, 128, 16)
        DH = D // H
        key = jax.random.key(seed)
        ks = jax.random.split(key, 12)
        s = 1.0 / math.sqrt(D)
        return {'x_q': jax.random.normal(ks[0], (B, S, D), jnp.float32), 'x_k': jax.random.normal(ks[1], (B, S, D), jnp.float32), 'x_v': jax.random.normal(ks[2], (B, S, D), jnp.float32), 'mask': jax.random.randint(ks[3], (B, S), 0, 2) > 0, 'Wq': jax.random.normal(ks[4], (D, D), jnp.float32) * s, 'bq': jnp.zeros((D,), jnp.float32), 'Wk': jax.random.normal(ks[5], (D, D), jnp.float32) * s, 'bk': jnp.zeros((D,), jnp.float32), 'Wv': jax.random.normal(ks[6], (D, D), jnp.float32) * s, 'bv': jnp.zeros((D,), jnp.float32), 'Wo': jax.random.normal(ks[7], (D, D), jnp.float32) * s, 'bo': jnp.zeros((D,), jnp.float32)}
    _L1_xattn_all = _L1_xattn_setup()
    _L1_xattn_in = {k: v for k, v in _L1_xattn_all.items() if k in ('Wq', 'bq', 'Wk', 'bk', 'Wv', 'bv', 'Wo', 'bo')}
    del _L1_xattn_all

    def _L1_ffn_setup():
        import jax, jax.numpy as jnp
        import numpy as np
        B, L, D, H, E, TOP_K = (4, 256, 128, 512, 8, 2)
        LN_EPS = 1e-05
        key = jax.random.key(seed)
        ks = jax.random.split(key, 8)
        x = jax.random.normal(ks[0], (B, L, D), dtype=jnp.float32)
        gate_w = jax.random.normal(ks[1], (D, E), dtype=jnp.float32) / np.sqrt(D)
        w1 = jax.random.normal(ks[2], (E, D, H), dtype=jnp.float32) / np.sqrt(D)
        b1 = jnp.zeros((E, H), dtype=jnp.float32)
        w2 = jax.random.normal(ks[3], (E, H, D), dtype=jnp.float32) / np.sqrt(H)
        b2 = jnp.zeros((E, D), dtype=jnp.float32)
        gamma = jnp.ones((D,), dtype=jnp.float32)
        beta = jnp.zeros((D,), dtype=jnp.float32)
        return {'x': x, 'gate_w': gate_w, 'w1': w1, 'b1': b1, 'w2': w2, 'b2': b2, 'gamma': gamma, 'beta': beta}
    _L1_ffn_all = _L1_ffn_setup()
    _L1_ffn_in = {k: v for k, v in _L1_ffn_all.items() if k in ('gate_w', 'w1', 'b1', 'w2', 'b2', 'gamma', 'beta')}
    del _L1_ffn_all

    def _L2_attn_setup():
        import jax, jax.numpy as jnp
        import numpy as np
        from jax import lax
        H = 128
        DI = 256
        N = 16
        DC = 4
        DTR = 64
        B, L = (2, 256)
        EPS = 1e-05

        def _selective_scan(u, delta, A, Bm, Cm, D):

            def step(h, inp):
                d, b, c, ut = inp
                dA = jnp.exp(d[:, :, None] * A)
                h = dA * h + (d * ut)[:, :, None] * b[:, None, :]
                y = jnp.einsum('bdn,bn->bd', h, c)
                return (h, y)
            h0 = jnp.zeros((u.shape[0], A.shape[0], A.shape[1]), u.dtype)
            xs = (delta.transpose(1, 0, 2), Bm.transpose(1, 0, 2), Cm.transpose(1, 0, 2), u.transpose(1, 0, 2))
            _, ys = lax.scan(step, h0, xs)
            return ys.transpose(1, 0, 2) + u * D

        def _mamba(x, in_proj_w, conv_w, conv_b, x_proj_w, dt_proj_w, dt_proj_b, A_log, D, out_proj_w):
            xz = x @ in_proj_w.T
            xi, z = (xz[..., :DI], xz[..., DI:])
            xc = lax.conv_general_dilated(xi.transpose(0, 2, 1), conv_w, window_strides=(1,), padding=[(DC - 1, 0)], feature_group_count=DI) + conv_b[None, :, None]
            xi = jax.nn.silu(xc.transpose(0, 2, 1))
            dbc = xi @ x_proj_w.T
            dt, Bm, Cm = (dbc[..., :DTR], dbc[..., DTR:DTR + N], dbc[..., DTR + N:])
            delta = jax.nn.softplus(dt @ dt_proj_w.T + dt_proj_b)
            A = -jnp.exp(A_log)
            y = _selective_scan(xi, delta, A, Bm, Cm, D)
            y = y * jax.nn.silu(z)
            return y @ out_proj_w.T
        key = jax.random.key(seed)
        ks = jax.random.split(key, 12)
        rn = lambda k, shp, sc=0.02: jax.random.normal(k, shp, jnp.float32) * sc
        return {'x': jax.random.normal(ks[0], (B, L, H), jnp.float32), 'ln_g': jnp.ones((H,), jnp.float32), 'ln_b': jnp.zeros((H,), jnp.float32), 'in_proj_w': rn(ks[1], (2 * DI, H)), 'conv_w': rn(ks[2], (DI, 1, DC), 0.2), 'conv_b': jnp.zeros((DI,), jnp.float32), 'x_proj_w': rn(ks[3], (DTR + 2 * N, DI)), 'dt_proj_w': rn(ks[4], (DI, DTR), 0.1), 'dt_proj_b': jax.random.uniform(ks[5], (DI,), jnp.float32, -4.0, -2.0), 'A_log': jnp.tile(jnp.log(jnp.arange(1, N + 1, dtype=jnp.float32))[None, :], (DI, 1)), 'D': jnp.ones((DI,), jnp.float32), 'out_proj_w': rn(ks[6], (H, DI)), 'dim_reduce_w': rn(ks[7], (H, 2 * H)), 'dim_reduce_b': jnp.zeros((H,), jnp.float32), 'glu_w': rn(ks[8], (2 * H, H)), 'glu_b': jnp.zeros((2 * H,), jnp.float32)}
    _L2_attn_all = _L2_attn_setup()
    _L2_attn_in = {k: v for k, v in _L2_attn_all.items() if k in ('ln_g', 'ln_b', 'in_proj_w', 'conv_w', 'conv_b', 'x_proj_w', 'dt_proj_w', 'dt_proj_b', 'A_log', 'D', 'out_proj_w', 'dim_reduce_w', 'dim_reduce_b', 'glu_w', 'glu_b')}
    del _L2_attn_all

    def _L2_xattn_setup():
        import jax, jax.numpy as jnp
        import numpy as np
        N_HEAD = 16
        D_MODEL = 128
        D_K = D_MODEL // N_HEAD
        key = jax.random.key(seed)
        ks = jax.random.split(key, 11)
        B, S = (4, 256)
        s = 1.0 / np.sqrt(D_MODEL)
        return {'q': jax.random.normal(ks[0], (B, S, D_MODEL), jnp.float32), 'k': jax.random.normal(ks[1], (B, S, D_MODEL), jnp.float32), 'v': jax.random.normal(ks[2], (B, S, D_MODEL), jnp.float32), 'wq': jax.random.normal(ks[3], (D_MODEL, D_MODEL), jnp.float32) * s, 'bq': jax.random.normal(ks[4], (D_MODEL,), jnp.float32) * s, 'wk': jax.random.normal(ks[5], (D_MODEL, D_MODEL), jnp.float32) * s, 'bk': jax.random.normal(ks[6], (D_MODEL,), jnp.float32) * s, 'wv': jax.random.normal(ks[7], (D_MODEL, D_MODEL), jnp.float32) * s, 'bv': jax.random.normal(ks[8], (D_MODEL,), jnp.float32) * s, 'wo': jax.random.normal(ks[9], (D_MODEL, D_MODEL), jnp.float32) * s, 'bo': jax.random.normal(ks[10], (D_MODEL,), jnp.float32) * s}
    _L2_xattn_all = _L2_xattn_setup()
    _L2_xattn_in = {k: v for k, v in _L2_xattn_all.items() if k in ('wq', 'bq', 'wk', 'bk', 'wv', 'bv', 'wo', 'bo')}
    del _L2_xattn_all

    def _L2_ffn_setup():
        import jax, jax.numpy as jnp
        import numpy as np
        B, S, D, E = (4, 512, 128, 8)
        key = jax.random.key(seed)
        ks = jax.random.split(key, 6)
        scale = 1.0 / np.sqrt(D)
        return {'tokens': jax.random.normal(ks[0], (B, S, D), dtype=jnp.float32), 'gate_w': jax.random.normal(ks[1], (D, E), dtype=jnp.float32) * scale, 'w0': jax.random.normal(ks[2], (D, D), dtype=jnp.float32) * scale, 'b0': jax.random.normal(ks[3], (D,), dtype=jnp.float32) * 0.01, 'w1': jax.random.normal(ks[4], (D, D), dtype=jnp.float32) * scale, 'b1': jax.random.normal(ks[5], (D,), dtype=jnp.float32) * 0.01}
    _L2_ffn_all = _L2_ffn_setup()
    _L2_ffn_in = {k: v for k, v in _L2_ffn_all.items() if k in ('gate_w', 'w0', 'b0', 'w1', 'b1')}
    del _L2_ffn_all

    def _L3_attn_setup():
        import jax, jax.numpy as jnp
        import numpy as np
        EMBED_DIM = 128
        NUM_HEADS = 16
        HEAD_DIM = EMBED_DIM // NUM_HEADS

        def apply_rope(x):
            B, T, H, D = x.shape
            half = D // 2
            theta = 10000.0 ** (-jnp.arange(half, dtype=x.dtype) / half)
            freqs = jnp.arange(T, dtype=x.dtype)[:, None] * theta[None, :]
            cos = freqs.reshape(1, T, 1, half)
            sin = jnp.sin(freqs).reshape(1, T, 1, half)
            cos = jnp.cos(freqs).reshape(1, T, 1, half)
            x1, x2 = (x[..., :half], x[..., half:])
            return jnp.concatenate([x1 * cos - x2 * sin, x1 * sin + x2 * cos], axis=-1)
        key = jax.random.key(seed)
        ks = jax.random.split(key, 9)
        s = 1.0 / np.sqrt(EMBED_DIM)
        inp = {'x': jax.random.normal(ks[0], (4, 256, EMBED_DIM), dtype=jnp.float32), 'Wq': jax.random.uniform(ks[1], (EMBED_DIM, EMBED_DIM), jnp.float32, -s, s), 'bq': jnp.zeros((EMBED_DIM,), jnp.float32), 'Wk': jax.random.uniform(ks[2], (EMBED_DIM, EMBED_DIM), jnp.float32, -s, s), 'bk': jnp.zeros((EMBED_DIM,), jnp.float32), 'Wv': jax.random.uniform(ks[3], (EMBED_DIM, EMBED_DIM), jnp.float32, -s, s), 'bv': jnp.zeros((EMBED_DIM,), jnp.float32), 'Wo': jax.random.uniform(ks[4], (EMBED_DIM, EMBED_DIM), jnp.float32, -s, s), 'bo': jnp.zeros((EMBED_DIM,), jnp.float32)}
        return inp
    _L3_attn_all = _L3_attn_setup()
    _L3_attn_in = {k: v for k, v in _L3_attn_all.items() if k in ('Wq', 'bq', 'Wk', 'bk', 'Wv', 'bv', 'Wo', 'bo')}
    del _L3_attn_all

    def _L3_xattn_setup():
        import jax, jax.numpy as jnp
        import numpy as np
        HIDDEN = 128
        NUM_HEADS = 16
        HEAD_DIM = HIDDEN // NUM_HEADS
        key = jax.random.key(seed)
        k1, k2, k3, k4, k5, k6 = jax.random.split(key, 6)
        B, SQ, SKV = (4, 128, 256)
        s = HIDDEN ** (-0.5)
        return {'xq': jax.random.normal(k1, (B, SQ, HIDDEN), jnp.float32), 'xkv': jax.random.normal(k2, (B, SKV, HIDDEN), jnp.float32), 'Wq': jax.random.normal(k3, (HIDDEN, HIDDEN), jnp.float32) * s, 'Wkv': jax.random.normal(k4, (2 * HIDDEN, HIDDEN), jnp.float32) * s, 'Wout': jax.random.normal(k5, (HIDDEN, HIDDEN), jnp.float32) * s, 'bout': jax.random.normal(k6, (HIDDEN,), jnp.float32) * 0.01}
    _L3_xattn_all = _L3_xattn_setup()
    _L3_xattn_in = {k: v for k, v in _L3_xattn_all.items() if k in ('Wq', 'Wkv', 'Wout', 'bout')}
    del _L3_xattn_all

    def _L3_ffn_setup():
        import jax, jax.numpy as jnp
        import numpy as np
        B, S, D_MODEL, D_HIDDEN = (4, 256, 128, 512)

        def act_quant(x):
            scale = 127.0 / jnp.clip(jnp.max(jnp.abs(x), axis=-1, keepdims=True), 1e-05)
            return jnp.clip(jnp.round(x * scale), -128, 127) / scale

        def weight_quant(w):
            scale = 1.0 / jnp.clip(jnp.mean(jnp.abs(w)), 1e-05)
            return jnp.clip(jnp.round(w * scale), -1, 1) / scale

        def bit_linear(x, w):
            xq = x + jax.lax.stop_gradient(act_quant(x) - x)
            wq = w + jax.lax.stop_gradient(weight_quant(w) - w)
            return jnp.einsum('bsd,hd->bsh', xq, wq)

        def depthwise_conv1d(x_bcl, w, b):
            y = jax.lax.conv_general_dilated(x_bcl, w, window_strides=(1,), padding=[(1, 1)], dimension_numbers=('NCH', 'OIH', 'NCH'), feature_group_count=x_bcl.shape[1])
            return y + b[None, :, None]
        key = jax.random.key(seed)
        ks = jax.random.split(key, 5)
        lim1 = 1.0 / np.sqrt(D_MODEL)
        lim2 = 1.0 / np.sqrt(D_HIDDEN)
        limc = 1.0 / np.sqrt(3.0)
        return {'x': jax.random.normal(ks[0], (B, S, D_MODEL), dtype=jnp.float32), 'w1': jax.random.uniform(ks[1], (D_HIDDEN, D_MODEL), jnp.float32, -lim1, lim1), 'conv_w': jax.random.uniform(ks[2], (D_HIDDEN, 1, 3), jnp.float32, -limc, limc), 'conv_b': jax.random.uniform(ks[3], (D_HIDDEN,), jnp.float32, -limc, limc), 'w2': jax.random.uniform(ks[4], (D_MODEL, D_HIDDEN), jnp.float32, -lim2, lim2)}
    _L3_ffn_all = _L3_ffn_setup()
    _L3_ffn_in = {k: v for k, v in _L3_ffn_all.items() if k in ('w1', 'conv_w', 'conv_b', 'w2')}
    del _L3_ffn_all
    return {'x': x, 'ctx_1024': ctx_1024, 'mask_BxS2_bk0': mask_BxS2_bk0, 'L0_attn_w_qkv': _L0_attn_in['w_qkv'], 'L0_attn_w_out': _L0_attn_in['w_out'], 'L0_xattn_Wk': _L0_xattn_in['Wk'], 'L0_xattn_Wv': _L0_xattn_in['Wv'], 'L0_xattn_bv': _L0_xattn_in['bv'], 'L0_xattn_Wq': _L0_xattn_in['Wq'], 'L0_xattn_bq': _L0_xattn_in['bq'], 'L0_xattn_Wo': _L0_xattn_in['Wo'], 'L0_xattn_bo': _L0_xattn_in['bo'], 'L0_ffn_router_kernel_DE': _L0_ffn_in['router_kernel_DE'], 'L0_ffn_kernel_gating_EDF': _L0_ffn_in['kernel_gating_EDF'], 'L0_ffn_kernel_up_EDF': _L0_ffn_in['kernel_up_EDF'], 'L0_ffn_kernel_down_EFD': _L0_ffn_in['kernel_down_EFD'], 'L1_attn_P_q': _L1_attn_in['P_q'], 'L1_attn_P_k': _L1_attn_in['P_k'], 'L1_attn_P_v': _L1_attn_in['P_v'], 'L1_attn_P_o': _L1_attn_in['P_o'], 'L1_xattn_Wq': _L1_xattn_in['Wq'], 'L1_xattn_bq': _L1_xattn_in['bq'], 'L1_xattn_Wk': _L1_xattn_in['Wk'], 'L1_xattn_bk': _L1_xattn_in['bk'], 'L1_xattn_Wv': _L1_xattn_in['Wv'], 'L1_xattn_bv': _L1_xattn_in['bv'], 'L1_xattn_Wo': _L1_xattn_in['Wo'], 'L1_xattn_bo': _L1_xattn_in['bo'], 'L1_ffn_gate_w': _L1_ffn_in['gate_w'], 'L1_ffn_w1': _L1_ffn_in['w1'], 'L1_ffn_b1': _L1_ffn_in['b1'], 'L1_ffn_w2': _L1_ffn_in['w2'], 'L1_ffn_b2': _L1_ffn_in['b2'], 'L1_ffn_gamma': _L1_ffn_in['gamma'], 'L1_ffn_beta': _L1_ffn_in['beta'], 'L2_attn_ln_g': _L2_attn_in['ln_g'], 'L2_attn_ln_b': _L2_attn_in['ln_b'], 'L2_attn_in_proj_w': _L2_attn_in['in_proj_w'], 'L2_attn_conv_w': _L2_attn_in['conv_w'], 'L2_attn_conv_b': _L2_attn_in['conv_b'], 'L2_attn_x_proj_w': _L2_attn_in['x_proj_w'], 'L2_attn_dt_proj_w': _L2_attn_in['dt_proj_w'], 'L2_attn_dt_proj_b': _L2_attn_in['dt_proj_b'], 'L2_attn_A_log': _L2_attn_in['A_log'], 'L2_attn_D': _L2_attn_in['D'], 'L2_attn_out_proj_w': _L2_attn_in['out_proj_w'], 'L2_attn_dim_reduce_w': _L2_attn_in['dim_reduce_w'], 'L2_attn_dim_reduce_b': _L2_attn_in['dim_reduce_b'], 'L2_attn_glu_w': _L2_attn_in['glu_w'], 'L2_attn_glu_b': _L2_attn_in['glu_b'], 'L2_xattn_wq': _L2_xattn_in['wq'], 'L2_xattn_bq': _L2_xattn_in['bq'], 'L2_xattn_wk': _L2_xattn_in['wk'], 'L2_xattn_bk': _L2_xattn_in['bk'], 'L2_xattn_wv': _L2_xattn_in['wv'], 'L2_xattn_bv': _L2_xattn_in['bv'], 'L2_xattn_wo': _L2_xattn_in['wo'], 'L2_xattn_bo': _L2_xattn_in['bo'], 'L2_ffn_gate_w': _L2_ffn_in['gate_w'], 'L2_ffn_w0': _L2_ffn_in['w0'], 'L2_ffn_b0': _L2_ffn_in['b0'], 'L2_ffn_w1': _L2_ffn_in['w1'], 'L2_ffn_b1': _L2_ffn_in['b1'], 'L3_attn_Wq': _L3_attn_in['Wq'], 'L3_attn_bq': _L3_attn_in['bq'], 'L3_attn_Wk': _L3_attn_in['Wk'], 'L3_attn_bk': _L3_attn_in['bk'], 'L3_attn_Wv': _L3_attn_in['Wv'], 'L3_attn_bv': _L3_attn_in['bv'], 'L3_attn_Wo': _L3_attn_in['Wo'], 'L3_attn_bo': _L3_attn_in['bo'], 'L3_xattn_Wq': _L3_xattn_in['Wq'], 'L3_xattn_Wkv': _L3_xattn_in['Wkv'], 'L3_xattn_Wout': _L3_xattn_in['Wout'], 'L3_xattn_bout': _L3_xattn_in['bout'], 'L3_ffn_w1': _L3_ffn_in['w1'], 'L3_ffn_conv_w': _L3_ffn_in['conv_w'], 'L3_ffn_conv_b': _L3_ffn_in['conv_b'], 'L3_ffn_w2': _L3_ffn_in['w2']}

def reference(x, ctx_1024, mask_BxS2_bk0, L0_attn_w_qkv, L0_attn_w_out, L0_xattn_Wk, L0_xattn_Wv, L0_xattn_bv, L0_xattn_Wq, L0_xattn_bq, L0_xattn_Wo, L0_xattn_bo, L0_ffn_router_kernel_DE, L0_ffn_kernel_gating_EDF, L0_ffn_kernel_up_EDF, L0_ffn_kernel_down_EFD, L1_attn_P_q, L1_attn_P_k, L1_attn_P_v, L1_attn_P_o, L1_xattn_Wq, L1_xattn_bq, L1_xattn_Wk, L1_xattn_bk, L1_xattn_Wv, L1_xattn_bv, L1_xattn_Wo, L1_xattn_bo, L1_ffn_gate_w, L1_ffn_w1, L1_ffn_b1, L1_ffn_w2, L1_ffn_b2, L1_ffn_gamma, L1_ffn_beta, L2_attn_ln_g, L2_attn_ln_b, L2_attn_in_proj_w, L2_attn_conv_w, L2_attn_conv_b, L2_attn_x_proj_w, L2_attn_dt_proj_w, L2_attn_dt_proj_b, L2_attn_A_log, L2_attn_D, L2_attn_out_proj_w, L2_attn_dim_reduce_w, L2_attn_dim_reduce_b, L2_attn_glu_w, L2_attn_glu_b, L2_xattn_wq, L2_xattn_bq, L2_xattn_wk, L2_xattn_bk, L2_xattn_wv, L2_xattn_bv, L2_xattn_wo, L2_xattn_bo, L2_ffn_gate_w, L2_ffn_w0, L2_ffn_b0, L2_ffn_w1, L2_ffn_b1, L3_attn_Wq, L3_attn_bq, L3_attn_Wk, L3_attn_bk, L3_attn_Wv, L3_attn_bv, L3_attn_Wo, L3_attn_bo, L3_xattn_Wq, L3_xattn_Wkv, L3_xattn_Wout, L3_xattn_bout, L3_ffn_w1, L3_ffn_conv_w, L3_ffn_conv_b, L3_ffn_w2):
    import jax
    import jax.numpy as jnp

    def _L0_attn_ref(x, w_qkv, w_out):
        import jax, jax.numpy as jnp
        import numpy as np
        D_MODEL = 128
        N_HEADS = 16
        D_HEAD = D_MODEL // N_HEADS
        EPS = 1e-06

        def _phi(x):
            return jax.nn.elu(x) + 1.0
        B, L, D = x.shape
        H, dh = (N_HEADS, D_HEAD)
        qkv = jnp.einsum('bld,ed->ble', x, w_qkv)
        qkv = qkv.reshape(B, L, 3, H, dh).transpose(2, 0, 3, 1, 4)
        q, k, v = (_phi(qkv[0]), _phi(qkv[1]), qkv[2])
        qT = q.transpose(2, 0, 1, 3)
        kT = k.transpose(2, 0, 1, 3)
        vT = v.transpose(2, 0, 1, 3)
        S0 = jnp.zeros((B, H, dh, dh), dtype=x.dtype)
        z0 = jnp.zeros((B, H, dh), dtype=x.dtype)

        def step(carry, inp):
            S, z = carry
            q_t, k_t, v_t = inp
            S = S + k_t[..., :, None] * v_t[..., None, :]
            z = z + k_t
            num = jnp.einsum('bhde,bhd->bhe', S, q_t)
            den = jnp.maximum(jnp.sum(z * q_t, axis=-1, keepdims=True), EPS)
            return ((S, z), num / den)
        _, out = jax.lax.scan(step, (S0, z0), (qT, kT, vT))
        out = out.transpose(1, 0, 2, 3).reshape(B, L, D)
        return jnp.einsum('bld,ed->ble', out, w_out)

    def _L0_xattn_ref(k, v, q, Wk, Wv, bv, Wq, bq, Wo, bo):
        import jax, jax.numpy as jnp
        import numpy as np
        D_MODEL = 128
        B, S = (4, 256)
        kp = jnp.einsum('bsd,ed->bse', k, Wk)
        vp = jnp.einsum('bsd,ed->bse', v, Wv) + bv
        qp = jnp.einsum('bsd,ed->bse', q, Wq) + bq
        scale = 1.0 / jnp.sqrt(jnp.float32(kp.shape[-1]))
        scores = jnp.einsum('bqd,bkd->bqk', qp, kp) * scale
        probs = jax.nn.softmax(scores, axis=-1)
        ctx = jnp.einsum('bqk,bkd->bqd', probs, vp)
        return jnp.einsum('bqd,ed->bqe', ctx, Wo) + bo

    def _L0_ffn_ref(x, router_kernel_DE, kernel_gating_EDF, kernel_up_EDF, kernel_down_EFD):
        import jax, jax.numpy as jnp
        import numpy as np
        TOP_K = 2
        E = router_kernel_DE.shape[-1]
        x = x.astype(jnp.float32)
        logits_BSE = jnp.einsum('BSD,DE->BSE', x, router_kernel_DE)
        probs_BSE = jax.nn.softmax(logits_BSE.astype(jnp.float32), axis=-1)
        weights_BSK, indices_BSK = jax.lax.top_k(probs_BSE, TOP_K)
        norm_weights_BSK = jax.nn.softmax(weights_BSK, axis=-1)
        one_hot_BSKE = jax.nn.one_hot(indices_BSK, num_classes=E, dtype=x.dtype)
        full_weights_BSE = jnp.sum(one_hot_BSKE * norm_weights_BSK[..., None], axis=2)
        gating_BSEF = jnp.einsum('BSD,EDF->BSEF', x, kernel_gating_EDF)
        act_BSEF = jax.nn.silu(gating_BSEF)
        up_BSEF = jnp.einsum('BSD,EDF->BSEF', x, kernel_up_EDF)
        fuse_BSEF = act_BSEF * up_BSEF
        down_BSED = jnp.einsum('BSEF,EFD->BSED', fuse_BSEF, kernel_down_EFD)
        out_BSD = jnp.einsum('BSED,BSE->BSD', down_BSED, full_weights_BSE)
        return out_BSD.astype(jnp.float32)

    def _L1_attn_ref(x, P_q, P_k, P_v, P_o):
        import jax, jax.numpy as jnp
        import numpy as np
        B, M, D, H, K, V = (4, 256, 128, 16, 64, 64)
        Q = jnp.einsum('bmd,hdk->bhmk', x, P_q)
        Kt = jnp.einsum('bmd,hdk->bhmk', x, P_k)
        Vt = jnp.einsum('bmd,hdv->bhmv', x, P_v)
        scale = 1.0 / jnp.sqrt(jnp.asarray(K, dtype=x.dtype))
        logits = jnp.einsum('bhmk,bhnk->bhmn', Q, Kt) * scale
        m = logits.shape[-1]
        causal = jnp.tril(jnp.ones((m, m), dtype=bool))
        logits = jnp.where(causal[None, None], logits, jnp.asarray(-jnp.inf, dtype=logits.dtype))
        weights = jax.nn.softmax(logits, axis=-1)
        o = jnp.einsum('bhmn,bhnv->bhmv', weights, Vt)
        y = jnp.einsum('bhmv,hdv->bmd', o, P_o)
        return y

    def _L1_xattn_ref(x_q, x_k, x_v, mask, Wq, bq, Wk, bk, Wv, bv, Wo, bo):
        import math
        import jax, jax.numpy as jnp
        import numpy as np
        B, S, D, H = (2, 256, 128, 16)
        DH = D // H
        Q = jnp.einsum('bsd,ed->bse', x_q, Wq) + bq
        K = jnp.einsum('bsd,ed->bse', x_k, Wk) + bk
        V = jnp.einsum('bsd,ed->bse', x_v, Wv) + bv
        b, sq, d = Q.shape
        Qh = Q.reshape(b, sq, H, DH)
        Kh = K.reshape(b, -1, H, DH)
        Vh = V.reshape(b, -1, H, DH)
        scores = jnp.einsum('bqhd,bkhd->bhqk', Qh, Kh) / math.sqrt(DH)
        scores = scores + jnp.where(mask[:, None, None, :], 0.0, -1000000000.0)
        A = jax.nn.softmax(scores, axis=-1)
        out = jnp.einsum('bhqk,bkhd->bqhd', A, Vh).reshape(b, sq, d)
        return jnp.einsum('bsd,ed->bse', out, Wo) + bo

    def _L1_ffn_ref(x, gate_w, w1, b1, w2, b2, gamma, beta):
        import jax, jax.numpy as jnp
        import numpy as np
        B, L, D, H, E, TOP_K = (4, 256, 128, 512, 8, 2)
        LN_EPS = 1e-05
        residual = x
        mu = jnp.mean(x, axis=-1, keepdims=True)
        var = jnp.mean(jnp.square(x - mu), axis=-1, keepdims=True)
        xn = (x - mu) * jax.lax.rsqrt(var + LN_EPS) * gamma + beta
        probs = jax.nn.softmax(jnp.einsum('bld,de->ble', xn, gate_w), axis=-1)
        w, idx = jax.lax.top_k(probs, TOP_K)
        w = w / jnp.sum(w, axis=-1, keepdims=True)
        cw = jnp.sum(w[..., None] * jax.nn.one_hot(idx, E, dtype=x.dtype), axis=2)
        h = jax.nn.gelu(jnp.einsum('bld,edh->eblh', xn, w1) + b1[:, None, None, :], approximate=False)
        out_e = jnp.einsum('eblh,ehd->ebld', h, w2) + b2[:, None, None, :]
        output = jnp.einsum('ble,ebld->bld', cw, out_e)
        return output + residual

    def _L2_attn_ref(x, ln_g, ln_b, in_proj_w, conv_w, conv_b, x_proj_w, dt_proj_w, dt_proj_b, A_log, D, out_proj_w, dim_reduce_w, dim_reduce_b, glu_w, glu_b):
        import jax, jax.numpy as jnp
        import numpy as np
        from jax import lax
        H = 128
        DI = 256
        N = 16
        DC = 4
        DTR = 64
        B, L = (2, 256)
        EPS = 1e-05

        def _selective_scan(u, delta, A, Bm, Cm, D):

            def step(h, inp):
                d, b, c, ut = inp
                dA = jnp.exp(d[:, :, None] * A)
                h = dA * h + (d * ut)[:, :, None] * b[:, None, :]
                y = jnp.einsum('bdn,bn->bd', h, c)
                return (h, y)
            h0 = jnp.zeros((u.shape[0], A.shape[0], A.shape[1]), u.dtype)
            xs = (delta.transpose(1, 0, 2), Bm.transpose(1, 0, 2), Cm.transpose(1, 0, 2), u.transpose(1, 0, 2))
            _, ys = lax.scan(step, h0, xs)
            return ys.transpose(1, 0, 2) + u * D

        def _mamba(x, in_proj_w, conv_w, conv_b, x_proj_w, dt_proj_w, dt_proj_b, A_log, D, out_proj_w):
            xz = x @ in_proj_w.T
            xi, z = (xz[..., :DI], xz[..., DI:])
            xc = lax.conv_general_dilated(xi.transpose(0, 2, 1), conv_w, window_strides=(1,), padding=[(DC - 1, 0)], feature_group_count=DI) + conv_b[None, :, None]
            xi = jax.nn.silu(xc.transpose(0, 2, 1))
            dbc = xi @ x_proj_w.T
            dt, Bm, Cm = (dbc[..., :DTR], dbc[..., DTR:DTR + N], dbc[..., DTR + N:])
            delta = jax.nn.softplus(dt @ dt_proj_w.T + dt_proj_b)
            A = -jnp.exp(A_log)
            y = _selective_scan(xi, delta, A, Bm, Cm, D)
            y = y * jax.nn.silu(z)
            return y @ out_proj_w.T
        skip = x
        mu = x.mean(-1, keepdims=True)
        var = ((x - mu) ** 2).mean(-1, keepdims=True)
        xn = (x - mu) * lax.rsqrt(var + EPS) * ln_g + ln_b
        margs = (in_proj_w, conv_w, conv_b, x_proj_w, dt_proj_w, dt_proj_b, A_log, D, out_proj_w)
        x_f = _mamba(xn, *margs)
        x_r = jnp.flip(_mamba(jnp.flip(xn, 1), *margs), 1)
        y = jnp.concatenate([x_f, x_r], axis=-1) @ dim_reduce_w.T + dim_reduce_b
        y = jax.nn.gelu(y, approximate=False)
        g = y @ glu_w.T + glu_b
        y = g[..., :H] * jax.nn.sigmoid(g[..., H:])
        return y + skip

    def _L2_xattn_ref(q, k, v, wq, bq, wk, bk, wv, bv, wo, bo):
        import jax, jax.numpy as jnp
        import numpy as np
        N_HEAD = 16
        D_MODEL = 128
        D_K = D_MODEL // N_HEAD
        B, S, _ = q.shape

        def proj(x, w, b):
            y = x @ w.T + b
            return y.reshape(B, -1, N_HEAD, D_K).transpose(0, 2, 1, 3)
        qh = proj(q, wq, bq)
        kh = proj(k, wk, bk)
        vh = proj(v, wv, bv)
        scale = jnp.sqrt(jnp.float32(D_K))
        scores = jnp.einsum('bhsd,bhtd->bhst', qh, kh) / scale
        attn = jax.nn.softmax(scores, axis=-1)
        out = jnp.einsum('bhst,bhtd->bhsd', attn, vh)
        out = out.transpose(0, 2, 1, 3).reshape(B, S, D_MODEL)
        return out @ wo.T + bo

    def _L2_ffn_ref(tokens, gate_w, w0, b0, w1, b1):
        import jax, jax.numpy as jnp
        import numpy as np
        B, S, D, E = (4, 512, 128, 8)
        b, s, d = tokens.shape
        logits = jnp.einsum('bsd,de->bse', tokens, gate_w)
        weights = jax.nn.softmax(logits, axis=-1)
        topk_w, topk_idx = jax.lax.top_k(weights, 2)
        x = tokens.reshape(b * s, d)
        fw = topk_w.reshape(b * s, 2)
        fidx = topk_idx.reshape(b * s, 2)
        e0 = jax.nn.silu(x @ w0.T + b0)
        e1 = jax.nn.silu(x @ w1.T + b1)
        m0 = (fidx[:, 0:1] == 0).astype(x.dtype)
        m1 = (fidx[:, 1:2] == 1).astype(x.dtype)
        out = e0 * fw[:, 0:1] * m0 + e1 * fw[:, 1:2] * m1
        return out.reshape(b, s, d)

    def _L3_attn_ref(x, Wq, bq, Wk, bk, Wv, bv, Wo, bo):
        import jax, jax.numpy as jnp
        import numpy as np
        EMBED_DIM = 128
        NUM_HEADS = 16
        HEAD_DIM = EMBED_DIM // NUM_HEADS

        def apply_rope(x):
            B, T, H, D = x.shape
            half = D // 2
            theta = 10000.0 ** (-jnp.arange(half, dtype=x.dtype) / half)
            freqs = jnp.arange(T, dtype=x.dtype)[:, None] * theta[None, :]
            cos = freqs.reshape(1, T, 1, half)
            sin = jnp.sin(freqs).reshape(1, T, 1, half)
            cos = jnp.cos(freqs).reshape(1, T, 1, half)
            x1, x2 = (x[..., :half], x[..., half:])
            return jnp.concatenate([x1 * cos - x2 * sin, x1 * sin + x2 * cos], axis=-1)
        B, T, C = x.shape
        H, D = (NUM_HEADS, HEAD_DIM)
        q = (x @ Wq.T + bq).reshape(B, T, H, D)
        k = (x @ Wk.T + bk).reshape(B, T, H, D)
        v = (x @ Wv.T + bv).reshape(B, T, H, D)
        q = apply_rope(q)
        k = apply_rope(k)
        scores = jnp.einsum('bthd,bshd->bhts', q, k) / np.sqrt(D).astype(x.dtype)
        attn = jax.nn.softmax(scores, axis=-1)
        out = jnp.einsum('bhts,bshd->bthd', attn, v).reshape(B, T, C)
        return out @ Wo.T + bo

    def _L3_xattn_ref(xq, xkv, Wq, Wkv, Wout, bout):
        import jax, jax.numpy as jnp
        import numpy as np
        HIDDEN = 128
        NUM_HEADS = 16
        HEAD_DIM = HIDDEN // NUM_HEADS
        B, SQ, H = xq.shape
        SKV = xkv.shape[1]
        scale = HEAD_DIM ** (-0.5)
        q = (xq @ Wq.T).reshape(B, SQ, NUM_HEADS, HEAD_DIM)
        kv = (xkv @ Wkv.T).reshape(B, SKV, 2, NUM_HEADS, HEAD_DIM)
        k, v = (kv[:, :, 0], kv[:, :, 1])
        att = jax.nn.softmax(jnp.einsum('bxhd,byhd->bhxy', q, k) * scale, axis=-1)
        x = jnp.einsum('bhxy,byhd->bxhd', att, v).reshape(B, SQ, H)
        return x @ Wout.T + bout

    def _L3_ffn_ref(x, w1, conv_w, conv_b, w2):
        import jax, jax.numpy as jnp
        import numpy as np
        B, S, D_MODEL, D_HIDDEN = (4, 256, 128, 512)

        def act_quant(x):
            scale = 127.0 / jnp.clip(jnp.max(jnp.abs(x), axis=-1, keepdims=True), 1e-05)
            return jnp.clip(jnp.round(x * scale), -128, 127) / scale

        def weight_quant(w):
            scale = 1.0 / jnp.clip(jnp.mean(jnp.abs(w)), 1e-05)
            return jnp.clip(jnp.round(w * scale), -1, 1) / scale

        def bit_linear(x, w):
            xq = x + jax.lax.stop_gradient(act_quant(x) - x)
            wq = w + jax.lax.stop_gradient(weight_quant(w) - w)
            return jnp.einsum('bsd,hd->bsh', xq, wq)

        def depthwise_conv1d(x_bcl, w, b):
            y = jax.lax.conv_general_dilated(x_bcl, w, window_strides=(1,), padding=[(1, 1)], dimension_numbers=('NCH', 'OIH', 'NCH'), feature_group_count=x_bcl.shape[1])
            return y + b[None, :, None]
        h = bit_linear(x, w1)
        h = depthwise_conv1d(h.transpose(0, 2, 1), conv_w, conv_b)
        h = h.transpose(0, 2, 1)
        h = jax.nn.silu(h)
        return bit_linear(h, w2)
    x = x + _L0_attn_ref(_layernorm(x, axis=-1), L0_attn_w_qkv, L0_attn_w_out)
    x = x + _L0_xattn_ref(ctx_1024, ctx_1024, _layernorm(x, axis=-1), L0_xattn_Wk, L0_xattn_Wv, L0_xattn_bv, L0_xattn_Wq, L0_xattn_bq, L0_xattn_Wo, L0_xattn_bo)
    x = x + _L0_ffn_ref(_layernorm(x, axis=-1), L0_ffn_router_kernel_DE, L0_ffn_kernel_gating_EDF, L0_ffn_kernel_up_EDF, L0_ffn_kernel_down_EFD)
    x = x + _L1_attn_ref(_layernorm(x, axis=-1), L1_attn_P_q, L1_attn_P_k, L1_attn_P_v, L1_attn_P_o)
    x = x + _L1_xattn_ref(_layernorm(x, axis=-1), ctx_1024, ctx_1024, mask_BxS2_bk0, L1_xattn_Wq, L1_xattn_bq, L1_xattn_Wk, L1_xattn_bk, L1_xattn_Wv, L1_xattn_bv, L1_xattn_Wo, L1_xattn_bo)
    x = x + _L1_ffn_ref(_layernorm(x, axis=-1), L1_ffn_gate_w, L1_ffn_w1, L1_ffn_b1, L1_ffn_w2, L1_ffn_b2, L1_ffn_gamma, L1_ffn_beta)
    x = x + _L2_attn_ref(_layernorm(x, axis=-1), L2_attn_ln_g, L2_attn_ln_b, L2_attn_in_proj_w, L2_attn_conv_w, L2_attn_conv_b, L2_attn_x_proj_w, L2_attn_dt_proj_w, L2_attn_dt_proj_b, L2_attn_A_log, L2_attn_D, L2_attn_out_proj_w, L2_attn_dim_reduce_w, L2_attn_dim_reduce_b, L2_attn_glu_w, L2_attn_glu_b)
    x = x + _L2_xattn_ref(_layernorm(x, axis=-1), ctx_1024, ctx_1024, L2_xattn_wq, L2_xattn_bq, L2_xattn_wk, L2_xattn_bk, L2_xattn_wv, L2_xattn_bv, L2_xattn_wo, L2_xattn_bo)
    x = x + _L2_ffn_ref(_layernorm(x, axis=-1), L2_ffn_gate_w, L2_ffn_w0, L2_ffn_b0, L2_ffn_w1, L2_ffn_b1)
    x = x + _L3_attn_ref(_layernorm(x, axis=-1), L3_attn_Wq, L3_attn_bq, L3_attn_Wk, L3_attn_bk, L3_attn_Wv, L3_attn_bv, L3_attn_Wo, L3_attn_bo)
    x = x + _L3_xattn_ref(_layernorm(x, axis=-1), ctx_1024, L3_xattn_Wq, L3_xattn_Wkv, L3_xattn_Wout, L3_xattn_bout)
    x = x + _L3_ffn_ref(_layernorm(x, axis=-1), L3_ffn_w1, L3_ffn_conv_w, L3_ffn_conv_b, L3_ffn_w2)
    return x

_drawn_inputs = setup_inputs


def setup_inputs(seed=0):
    import zlib

    import numpy as np

    out = dict(_drawn_inputs(seed))
    spreads = {'L0_xattn_bv': (0.0, 0.1),
     'L0_xattn_bq': (0.0, 0.1),
     'L0_xattn_bo': (0.0, 0.1),
     'L1_xattn_bq': (0.0, 0.1),
     'L1_xattn_bk': (0.0, 0.1),
     'L1_xattn_bv': (0.0, 0.1),
     'L1_xattn_bo': (0.0, 0.1),
     'L1_ffn_b1': (0.0, 0.1),
     'L1_ffn_b2': (0.0, 0.1),
     'L1_ffn_gamma': (1.0, 0.2),
     'L1_ffn_beta': (0.0, 0.1),
     'L2_attn_ln_g': (1.0, 0.2),
     'L2_attn_ln_b': (0.0, 0.1),
     'L2_attn_conv_b': (0.0, 0.1),
     'L2_attn_D': (1.0, 0.2),
     'L2_attn_dim_reduce_b': (0.0, 0.1),
     'L2_attn_glu_b': (0.0, 0.1),
     'L3_attn_bq': (0.0, 0.1),
     'L3_attn_bk': (0.0, 0.1),
     'L3_attn_bv': (0.0, 0.1),
     'L3_attn_bo': (0.0, 0.1)}
    factors = {}
    for name, (base, spread) in spreads.items():
        noise = np.random.default_rng([zlib.crc32(name.encode()), seed]).standard_normal(out[name].shape)
        drawn = base * np.exp(spread * noise) if base else spread * noise
        out[name] = jnp.asarray(drawn.astype(out[name].dtype))
    for name, factor in factors.items():
        out[name] = (out[name] * factor).astype(out[name].dtype)
    return out
```

```python
from contextlib import ExitStack

import numpy as np
import concourse.bass as bass
from concourse import mybir

ALU = mybir.AluOpType
ACT = mybir.ActivationFunctionType
AX = mybir.AxisListType
F32 = mybir.dt.float32
BF16 = mybir.dt.bfloat16
U32 = mybir.dt.uint32
U8 = mybir.dt.uint8

B, T, D, C = 32, 128, 128, 77
NB = 4
STREAMS = 2
PASSES = B // (NB * STREAMS)
N = NB * T
NC_ = NB * C
H, DH = 16, 8
H1, DH1 = 16, 64
E = 8
F0, F1 = 256, 512
DI, NS, DTR, DC = 256, 16, 64, 4
HID = 512
EPS = 1e-5
NEG = -1e9
ROUND = 12582912.0
FAR = 1e30
PRE_D = 13
NESTED = ("L1f", "L2a")
LAST = 12



def spread_heads(w):
    out = np.zeros((w.shape[0], 4, 4, 32), w.dtype)
    out[:, :, :, :DH] = w.reshape(w.shape[0], 4, 4, DH).transpose(0, 2, 1, 3)
    return out.reshape(w.shape[0], 512)


def spread_bias(b):
    return np.ascontiguousarray(spread_heads(b[None, :]).reshape(4, 128).T)


def swap_halves(w):
    return w.reshape(w.shape[0], H, 2, DH // 2)[:, :, ::-1, :].reshape(w.shape[0], H * DH)


def k_tiles(w):
    k = w.shape[0] // 128
    return w.reshape(k, 128, -1).transpose(1, 0, 2).reshape(128, -1)


def rows_below(w):
    out = np.zeros((128, w.shape[1]), w.dtype)
    out[:w.shape[0]] = w
    return out


def rotation_tables():
    half = DH // 2
    theta = np.float32(10000.0) ** (-np.arange(half, dtype=np.float32) / np.float32(half))
    angle = np.arange(T, dtype=np.float32)[None, :] * theta[:, None]
    cos = np.zeros((4, 32, T), np.float32)
    sin = np.zeros((4, 32, T), np.float32)
    cos[:, :half], cos[:, half:DH] = np.cos(angle), np.cos(angle)
    sin[:, :half], sin[:, half:DH] = -np.sin(angle), np.sin(angle)
    return cos.reshape(128, T), sin.reshape(128, T)


def layouts(w):
    cat = lambda *a: np.concatenate(a, axis=1)
    cos, sin = rotation_tables()
    qkv = w["L0_attn_w_qkv"]
    p = {}
    p["const"] = {
        "ident": np.eye(128, dtype=np.float32),
        "upper": np.triu(np.ones((128, 128), np.float32)),
        "causal": np.where(np.tril(np.ones((128, 128))), 0.0, -1e30).astype(np.float32),
        "ones": np.ones((128, 128), np.float32),
        "eight": np.tile(np.arange(8, dtype=np.float32), (128, 1)),
        "neghalf": np.full((128, 4), -0.5, np.float32),
    }
    p["L0a"] = {"q": spread_heads(qkv[0:128].T), "k": spread_heads(qkv[128:256].T), "v": qkv[256:384].T,
                "o": w["L0_attn_w_out"].T}
    p["L0x"] = {"q": w["L0_xattn_Wq"].T, "k": w["L0_xattn_Wk"].T, "v": w["L0_xattn_Wv"].T,
                "o": w["L0_xattn_Wo"].T, "qb": w["L0_xattn_bq"][:, None]}
    p["L0f"] = {"r": w["L0_ffn_router_kernel_DE"],
                "gate": w["L0_ffn_kernel_gating_EDF"].transpose(1, 0, 2).reshape(D, E * F0),
                "up": w["L0_ffn_kernel_up_EDF"].transpose(1, 0, 2).reshape(D, E * F0),
                "down": k_tiles(w["L0_ffn_kernel_down_EFD"].reshape(E * F0, D))}
    heads = lambda a: a.transpose(1, 0, 2).reshape(D, H1 * DH1)
    p["L1a"] = {"q": heads(w["L1_attn_P_q"]), "k": heads(w["L1_attn_P_k"]), "v": heads(w["L1_attn_P_v"]),
                "o": k_tiles(w["L1_attn_P_o"].transpose(0, 2, 1).reshape(H1 * DH1, D))}
    p["L1x"] = {"q": spread_heads(w["L1_xattn_Wq"].T), "k": spread_heads(w["L1_xattn_Wk"].T),
                "v": w["L1_xattn_Wv"].T, "o": w["L1_xattn_Wo"].T,
                "qb": spread_bias(w["L1_xattn_bq"]), "kb": spread_bias(w["L1_xattn_bk"])}
    p["L1f"] = {"r": w["L1_ffn_gate_w"], "g": w["L1_ffn_gamma"][:, None], "b": w["L1_ffn_beta"][:, None],
                "w1": w["L1_ffn_w1"].transpose(1, 0, 2).reshape(D, E * F1),
                "b1": w["L1_ffn_b1"].reshape(E * F1 // 128, 128).T,
                "w2": k_tiles(w["L1_ffn_w2"].reshape(E * F1, D)),
                "b2": rows_below(w["L1_ffn_b2"])}
    xp = w["L2_attn_x_proj_w"].T
    bc = xp[:, DTR:]
    p["L2a"] = {"g": w["L2_attn_ln_g"][:, None], "b": w["L2_attn_ln_b"][:, None],
                "in": w["L2_attn_in_proj_w"].T,
                "conv": k_tiles(w["L2_attn_conv_w"].reshape(DI, DC)), "convb": k_tiles(w["L2_attn_conv_b"][:, None]),
                "bc3": k_tiles(cat(bc, bc, bc)), "xdt": k_tiles(xp[:, :DTR]),
                "dt": rows_below(w["L2_attn_dt_proj_w"].T), "dtb": k_tiles(w["L2_attn_dt_proj_b"][:, None]),
                "alog": k_tiles(w["L2_attn_A_log"]), "dskip": k_tiles(w["L2_attn_D"][:, None]),
                "out": k_tiles(w["L2_attn_out_proj_w"].T),
                "dim": k_tiles(w["L2_attn_dim_reduce_w"].T), "dimb": w["L2_attn_dim_reduce_b"][:, None],
                "glu": w["L2_attn_glu_w"].T}
    p["L2x"] = {"q": spread_heads(w["L2_xattn_wq"].T), "k": spread_heads(w["L2_xattn_wk"].T),
                "v": w["L2_xattn_wv"].T, "o": w["L2_xattn_wo"].T,
                "qb": spread_bias(w["L2_xattn_bq"]), "kb": spread_bias(w["L2_xattn_bk"])}
    p["L2f"] = {"r": w["L2_ffn_gate_w"], "w0": w["L2_ffn_w0"].T, "w1": w["L2_ffn_w1"].T}
    q, k = w["L3_attn_Wq"].T, w["L3_attn_Wk"].T
    qb, kb = w["L3_attn_bq"], w["L3_attn_bk"]
    p["L3a"] = {"q": spread_heads(q), "k": spread_heads(k), "v": w["L3_attn_Wv"].T, "o": w["L3_attn_Wo"].T,
                "qs": spread_heads(swap_halves(q)), "ks": spread_heads(swap_halves(k)),
                "qb": spread_bias(qb), "kb": spread_bias(kb),
                "qsb": spread_bias(swap_halves(qb[None, :])[0]), "ksb": spread_bias(swap_halves(kb[None, :])[0]),
                "cos": cos, "sin": sin}
    kv = w["L3_xattn_Wkv"]
    p["L3x"] = {"q": spread_heads(w["L3_xattn_Wq"].T), "k": spread_heads(kv[:128].T), "v": kv[128:].T,
                "o": w["L3_xattn_Wout"].T}
    p["L3f"] = {"w1": w["L3_ffn_w1"].T, "conv": k_tiles(w["L3_ffn_conv_w"].reshape(HID, 3)),
                "convb": k_tiles(w["L3_ffn_conv_b"][:, None]), "w2": k_tiles(w["L3_ffn_w2"].T)}
    return p


def bias_rows(w):
    return {"L0xv": w["L0_xattn_bv"], "L0xo": w["L0_xattn_bo"], "L1xv": w["L1_xattn_bv"], "L1xo": w["L1_xattn_bo"],
            "glu": w["L2_attn_glu_b"], "L2xv": w["L2_xattn_bv"], "L2xo": w["L2_xattn_bo"],
            "L2f0": w["L2_ffn_b0"], "L2f1": w["L2_ffn_b1"], "L3av": w["L3_attn_bv"], "L3ao": w["L3_attn_bo"],
            "L3xo": w["L3_xattn_bout"]}



class Tally:

    def __init__(self, numbers):
        self.final = numbers is not None
        self.numbers = numbers if self.final else {}
        self.made = {}
        self.sems = {}

    def count(self, signal, name):
        self.made[signal] = self.made.get(signal, 0) + 1
        if self.final:
            assert self.numbers[signal][name] == self.made[signal], (signal, name)
        else:
            assert name not in self.numbers.setdefault(signal, {}), (signal, name)
            self.numbers[signal][name] = self.made[signal]

    def value(self, signal, name, i):
        if not self.final:
            return 1
        per_pass = self.numbers[signal]
        return i * len(per_pass) + per_pass[name]


SIGNALS = dict(
    mask="DVE: the additive mask of a stream",
    x_upd="DVE has updated the residual", ln_stat="DVE: statistics", ln_aggr="DVE: mean and variance",
    ln_var="DVE: variance + eps", ln_rstd="Pool: reciprocal deviation", ln_xn="DVE: normalised tile",
    ln_tr="PE: transposed normalised tile", ln_xT="ACT: it is in SBUF",
    proj="PE: a projection is in PSUM", proj_a="ACT has taken a projection", proj_d="DVE has taken a projection",
    proj_p="Pool has finished a projection",
    scores="PE: scores", shift="DVE: a step of the softmax's shift", prob="ACT: exponentials",
    prob_d="DVE: masked products of the linear attention",
    turn="PE: transposed probabilities", turned="ACT: they are in SBUF", pv="PE: probabilities times values",
    norm="DVE: a step of the normalisation", ctx_tr="PE: transposed heads", ctx_a="ACT: they are in SBUF",
    out="PE: output projection",
    rt_pe="PE: router", rt_d="DVE: router", rt_a="ACT: router",
    ff_pe="PE: hidden tile", ff_a="ACT: hidden tile", ff_d="DVE: hidden tile", dn_pe="PE: expert's output",
    dn_d="DVE: expert's output added",
    mb_pe="PE: Mamba", mb_a="ACT: Mamba", mb_d="DVE: Mamba", mb_p="Pool: Mamba",
    sc_bc="PE: a row of B or C on all partitions", sc_da="ACT: decay", sc_d="DVE: scan", sc_y="PE: state added to y",
    qf_pe="PE: quantised network", qf_a="ACT: quantised network", qf_d="DVE: quantised network",
    qf_p="Pool: quantised network",
)


class SharedNames:
    pass


def declare(nc, ins, out, cols, rows, nrows, ctx):
    m = SharedNames()
    m.ins, m.out, m.cols, m.rows = ins, out, cols, rows

    def sb(name, shape, dt=F32):
        return ctx.enter_context(nc.sbuf_tensor("sb_" + name, shape, dt))

    m.W = {st: sb("weights_" + st, [128, width]) for st, (width, _) in cols.items()}
    m.brow = sb("bias_rows", [nrows, 128])
    m.nrows = nrows
    m.mask = sb("mask", [128, STREAMS, NC_])
    m.mask8 = sb("mask8", [128, STREAMS, NC_], U8)
    m.sel3 = sb("sel3", [128, 32], BF16)
    m.Aneg = sb("Aneg", [128, 2 * NS])
    m.w2t = sb("w2t", [128, HID], BF16)
    m.identb = sb("identb", [128, 128], BF16)
    m.wsc = sb("wsc", [128, 8])
    m.carrier = sb("carrier", [128, 6])
    m.xin = [sb(f"xin{s}", [128, NB, D]) for s in range(STREAMS)]
    m.x = [sb(f"x{s}", [128, NB, D]) for s in range(STREAMS)]
    m.xn = [sb(f"xn{s}", [128, NB, D]) for s in range(STREAMS)]
    m.xT = [sb(f"xT{s}", [128, N]) for s in range(STREAMS)]
    m.ctxT = [sb(f"ctxT{s}", [128, NC_]) for s in range(STREAMS)]
    m.st = [sb(f"st{s}", [128, NB, 6]) for s in range(STREAMS)]
    m.mv = [sb(f"mv{s}", [128, NB, 2]) for s in range(STREAMS)]
    m.ve = [sb(f"ve{s}", [128, NB]) for s in range(STREAMS)]
    m.rs = [sb(f"rs{s}", [128, NB]) for s in range(STREAMS)]
    m.small = [sb(f"small{s}", [128, 256]) for s in range(STREAMS)]
    m.idx = [sb(f"idx{s}", [128, NB, 8], U32) for s in range(STREAMS)]
    m.big = [sb(f"big{s}", [128, SCRATCH]) for s in range(STREAMS)]
    m.bank = [[ctx.enter_context(nc.psum_tensor(f"bank{s}{k}", [128, 512], F32)) for k in range(4)]
              for s in range(STREAMS)]
    m.sem = {name: ctx.enter_context(nc.semaphore("s_" + name)) for name in SIGNALS}
    m.s_w = {st: ctx.enter_context(nc.semaphore("s_w_" + st)) for st in cols}
    m.s_rows = ctx.enter_context(nc.semaphore("s_rows"))
    m.s_xin = [ctx.enter_context(nc.semaphore(f"s_xin{s}")) for s in range(STREAMS)]
    m.s_ctx = [ctx.enter_context(nc.semaphore(f"s_ctx{s}")) for s in range(STREAMS)]
    m.s_mask = [ctx.enter_context(nc.semaphore(f"s_mask{s}")) for s in range(STREAMS)]
    m.s_out = [ctx.enter_context(nc.semaphore(f"s_out{s}")) for s in range(STREAMS)]
    m.s_pre_d = ctx.enter_context(nc.semaphore("s_pre_d"))
    m.s_pre_a = ctx.enter_context(nc.semaphore("s_pre_a"))
    m.s_pre_pe = ctx.enter_context(nc.semaphore("s_pre_pe"))
    m.s_pre_p = ctx.enter_context(nc.semaphore("s_pre_p"))
    return m


SCRATCH = 7808


def cut(t, at, *shape):
    n = int(np.prod(shape))
    v = t[:, at:at + n]
    if len(shape) == 2:
        return v.rearrange("p (a b) -> p a b", b=shape[1])
    if len(shape) == 3:
        return v.rearrange("p (a b c) -> p a b c", b=shape[1], c=shape[2])
    return v



class Attention:

    def __init__(self, m, key):
        self.key, self.m = key, m
        self.ctx = key.endswith("x")
        self.Tk = C if self.ctx else T
        self.wide = key == "L1a"
        self.single = key == "L0x"
        self.linear = key == "L0a"
        self.rotated = key == "L3a"
        self.masked = key in ("L1a", "L1x")
        self.blocks = 8 if self.wide else 1
        self.dh = DH1 if self.wide else D if self.single else DH
        self.nh = 2 if self.wide else 1 if self.single else H
        self.scale = float(self.dh) ** -0.5
        self.col = m.cols[key][1]
        self.units = 2 if self.wide else 2 if self.single else 16
        self.items = 2 if self.single else 4
        self.group = 1 if (self.wide or self.single) else 4

    def w(self, name, lo=0, hi=None):
        at, width = self.col[name]
        return self.m.W[self.key][:, at + lo:at + (width if hi is None else hi)]

    def q(self, s):
        return cut(self.m.big[s], 0, 4, N)

    def k(self, s):
        return cut(self.m.big[s], 2048, 4, NC_ if self.ctx else N)

    def v(self, s):
        return cut(self.m.big[s], 4096, NB, self.nh, self.dh + 1)[0:self.Tk]

    def p(self, s, u):
        return cut(self.m.big[s], 4736 + 512 * (u % 2), self.items, self.Tk)

    def pT(self, s, u):
        return cut(self.m.big[s], 5760 + 512 * (u % 2), self.items, T)[0:self.Tk]

    def on(self, s):
        return cut(self.m.big[s], 6784, NB, self.nh, self.dh)

    def cT(self, s):
        return cut(self.m.big[s], 7296, N)

    def turn_tmp(self, s, k):
        return cut(self.m.big[s], 4736 + 512 * k, NB, T)

    def tiles(self, block):
        out = []
        if self.wide:
            lo = 128 * block
            for n, dst in (("q", self.q), ("k", self.k)):
                out.append((n, "T", self.w(n, lo, lo + 128), None, (dst, block % 2)))
            out.append(("v", "V", self.w("v", lo, lo + 128), None, None))
            return out
        for n, dst in (("q", self.q), ("k", self.k)):
            for j in range(1 if self.single else 4):
                src = "C" if n == "k" and self.ctx else "T"
                bias = self.w(n + "b", j, j + 1) if n + "b" in self.col else None
                kind = "P" if self.linear else "T"
                if self.rotated:
                    out.append((n + str(j), "R0", self.w(n, 128 * j, 128 * j + 128), bias, (dst, j)))
                    out.append((n + "s" + str(j), "R1", self.w(n + "s", 128 * j, 128 * j + 128),
                                self.w(n + "sb", j, j + 1), (dst, j)))
                else:
                    out.append((n + str(j), src + kind if src == "C" else kind,
                                self.w(n, 128 * j, 128 * j + 128), bias, (dst, j)))
        out.append(("v", "V", self.w("v"), None, None))
        return out

    def taker(self, t, kind):
        if kind in ("P", "R0", "R1"):
            return "proj_d"
        return "proj_a" if t % 2 == 0 else "proj_d"

    def last_taken(self, block):
        last = {}
        for t, (name, kind, *_rest) in enumerate(self.tiles(block)):
            last[self.taker(t, kind)] = t
        return last

    def item(self, s, block, u, n):
        q, k = self.q(s), self.k(s)
        if self.wide:
            return (q[64 * u:64 * u + 64, block % 2, n * T:(n + 1) * T],
                    k[64 * u:64 * u + 64, block % 2, n * T:(n + 1) * T], n, u)
        if self.single:
            b = 2 * u + n
            return q[:, 0, b * T:(b + 1) * T], k[:, 0, b * C:(b + 1) * C], b, 0
        b, r = u // 4, u % 4
        return (q[32 * r:32 * r + DH, n, b * T:(b + 1) * T],
                k[32 * r:32 * r + DH, n, b * self.Tk:(b + 1) * self.Tk], b, 4 * r + n)

    def o(self, s, u):
        bank = self.m.bank[s][3]
        if self.wide or self.single:
            return bank[:, 0:self.items * (self.dh + 1)].rearrange("p (a c) -> p a c", c=self.dh + 1)
        at = 256 * (u // 4 % 2)
        return bank[:, at:at + H * (DH + 1)].rearrange("p (a c) -> p a c", c=DH + 1)

    def o_slot(self, u, n):
        return n if (self.wide or self.single) else 4 * (u % 4) + n

    def on_slice(self, s, u):
        on = self.on(s)
        if self.wide:
            return on[:, :, u, :]
        if self.single:
            return on[:, 2 * u:2 * u + 2, 0, :]
        return on[:, u // 4, :, :]


def bias_picker(m, row, n):
    return m.const["ident"][0:m.nrows, row:row + 1].to_broadcast([m.nrows, n])


def attention_pe(pe, g, m, A, free):
    ident = m.const["ident"]
    for block in range(A.blocks):
        tiles = A.tiles(block)
        for t, (name, kind, w, _bias, _dst) in enumerate(tiles):
            for s in range(STREAMS):
                pe.wait_ge(*g.at("ln_xT", (A.key, s)))
                if A.ctx and block == 0 and A.key == "L0x":
                    pe.wait_ge(m.s_ctx[s], g.i * 16 + 16)
                bank = m.bank[s][t % 3]
                g.wait_free(pe, free, s, t % 3)
                src = m.ctxT[s] if kind[0] == "C" or (kind == "V" and A.ctx) else m.xT[s]
                if kind == "V":
                    brow = m.rows.get(A.key + "v")
                    for b in range(NB):
                        if brow is not None:
                            pe.matmul(bank[0:A.Tk, 128 * b:128 * b + 128], bias_picker(m, brow, A.Tk), m.brow[:, :],
                                      start=True, stop=False)
                        last = pe.matmul(bank[0:A.Tk, 128 * b:128 * b + 128],
                                         src[:, b * A.Tk:(b + 1) * A.Tk], w, start=brow is None, stop=True)
                else:
                    n = NC_ if kind[0] == "C" else N
                    last = pe.matmul(bank[:, 0:n], w, src[:, 0:n], start=True, stop=True)
                last.then_inc(*g.one("proj", (A.key, block, t, s)))
                free[s, t % 3] = (A.taker(t, kind), (A.key, block, t, s))
        for k in range(A.units + 2):
            for s in range(STREAMS):
                if k >= A.units:
                    continue
                if k == 0:
                    for taker, t in A.last_taken(block).items():
                        pe.wait_ge(*g.at(taker, (A.key, block, t, s)))
                    if A.rotated:
                        pe.wait_ge(*g.at("proj_p", (A.key, "k", 3, s)))
                g.wait_free(pe, free, s, k % 2)
                for n in range(A.items):
                    q, kk, b, h = A.item(s, block, k, n)
                    if A.linear:
                        dst = m.bank[s][k % 2][0:A.Tk, n * T:(n + 1) * T]
                        last = pe.matmul(dst, kk, q, start=True, stop=True)
                    else:
                        dst = m.bank[s][k % 2][:, n * A.Tk:(n + 1) * A.Tk]
                        last = pe.matmul(dst, q, kk, start=True, stop=True)
                last.then_inc(*g.one("scores", (A.key, block, k, s)))
                free[s, k % 2] = (("prob_d", (A.key, block, k, s)) if A.linear else
                                  ("shift", (A.key, block, k, s, "z" if A.masked else "e")))
            for s in range(STREAMS):
                if A.linear or not 0 <= k - 1 < A.units:
                    continue
                u = k - 1
                pe.wait_ge(*g.at("prob", (A.key, block, u, s)))
                g.wait_free(pe, free, s, 2)
                for n in range(A.items):
                    last = pe.transpose(m.bank[s][2][0:A.Tk, n * T:(n + 1) * T], A.p(s, u)[:, n, :], ident)
                last.then_inc(*g.one("turn", (A.key, block, u, s)))
                free[s, 2] = ("turned", (A.key, block, u, s))
            for s in range(STREAMS):
                if not 0 <= k - 2 < A.units:
                    continue
                u = k - 2
                pe.wait_ge(*g.at("prob_d" if A.linear else "turned", (A.key, block, u, s)))
                if u == 0 and block == 0:
                    pe.wait_ge(*g.at("proj_p", (A.key, "ones", s)))
                if u % A.group == 0:
                    g.wait_free(pe, free, s, 3)
                for n in range(A.items):
                    _q, _k, b, h = A.item(s, block, u, n)
                    last = pe.matmul(A.o(s, u)[:, A.o_slot(u, n), :], A.pT(s, u)[:, n, :], A.v(s)[:, b, h, :],
                                     start=True, stop=True)
                last.then_inc(*g.one("pv", (A.key, block, u, s)))
                free[s, 3] = ("norm", (A.key, block, u // A.group, s, "n"))
        for s in range(STREAMS):
            pe.wait_ge(*g.at("norm", (A.key, block, A.units // A.group - 1, s, "n")))
            g.wait_free(pe, free, s, 2)
            on = A.on(s).rearrange("p b h d -> p b (h d)")
            for b in range(NB):
                last = pe.transpose(m.bank[s][2][:, b * T:(b + 1) * T], on[:, b, :], ident)
            last.then_inc(*g.one("ctx_tr", (A.key, block, s)))
            free[s, 2] = ("ctx_a", (A.key, block, s))
        for s in range(STREAMS):
            pe.wait_ge(*g.at("ctx_a", (A.key, block, s)))
            g.wait_free(pe, free, s, 0)
            w = A.w("o", 128 * block, 128 * block + 128)
            brow = m.rows.get(A.key + "o")
            for b in range(NB):
                dst = m.bank[s][0][:, b * D:(b + 1) * D]
                if brow is not None:
                    pe.matmul(dst, bias_picker(m, brow, T), m.brow[:, :], start=True, stop=False)
                last = pe.matmul(dst, A.cT(s)[:, b * T:(b + 1) * T], w, start=brow is None, stop=True)
            last.then_inc(*g.one("out", (A.key, block, s)))
            free[s, 0] = ("x_upd", (A.key, block, s))


def attention_act(act, g, m, A):
    for block in range(A.blocks):
        for t, (name, kind, _w, bias, dst) in enumerate(A.tiles(block)):
            for s in range(STREAMS):
                if kind == "P":
                    act.wait_ge(*g.at("proj", (A.key, block, t, s)))
                    act.activation(dst[0](s)[:, dst[1], :], m.bank[s][t % 3][:, 0:N], ACT.Exp)\
                       .then_inc(*g.one("proj_a", (A.key, block, t, s)))
                if A.taker(t, kind) != "proj_a":
                    continue
                act.wait_ge(*g.at("proj", (A.key, block, t, s)))
                if A.wide and block >= 1:
                    act.wait_ge(*g.at("pv", (A.key, block - 1, A.units - 1, s)))
                if kind == "V":
                    act.activation(A.v(s)[:, :, :, 0:A.dh].rearrange("p b h d -> p (b h) d"),
                                   m.bank[s][t % 3][0:A.Tk, :].rearrange("p (a d) -> p a d", d=A.dh), ACT.Copy)\
                       .then_inc(*g.one("proj_a", (A.key, block, t, s)))
                else:
                    n = NC_ if kind[0] == "C" else N
                    act.activation(dst[0](s)[:, dst[1], :], m.bank[s][t % 3][:, 0:n], ACT.Identity,
                                   bias=0.0 if bias is None else bias)\
                       .then_inc(*g.one("proj_a", (A.key, block, t, s)))
        for k in range(A.units + 1):
            for s in range(STREAMS):
                if A.linear or k >= A.units:
                    continue
                act.wait_ge(*g.at("shift", (A.key, block, k, s, "e")))
                act.activation(A.p(s, k), A.p(s, k), ACT.Exp, scale=1.0 if A.masked else A.scale)\
                   .then_inc(*g.one("prob", (A.key, block, k, s)))
            for s in range(STREAMS):
                if A.linear or k == 0:
                    continue
                u = k - 1
                act.wait_ge(*g.at("turn", (A.key, block, u, s)))
                if u >= 2:
                    act.wait_ge(*g.at("pv", (A.key, block, u - 2, s)))
                act.activation(A.pT(s, u).rearrange("p a b -> p (a b)"),
                               m.bank[s][2][0:A.Tk, 0:A.items * T], ACT.Copy)\
                   .then_inc(*g.one("turned", (A.key, block, u, s)))
        for s in range(STREAMS):
            act.wait_ge(*g.at("ctx_tr", (A.key, block, s)))
            act.activation(A.cT(s), m.bank[s][2][:, :], ACT.Copy).then_inc(*g.one("ctx_a", (A.key, block, s)))


def mask_dve(dve, g, m):
    for s in range(STREAMS):
        dve.wait_ge(m.s_mask[s], g.i * 16 + 16)
        dve.tensor_scalar(m.mask[:, s, :], m.mask8[:, s, :], -NEG, NEG, ALU.mult, ALU.add)\
           .then_inc(*g.one("mask", s))


def attention_dve(dve, g, m, A, base):
    for block in range(A.blocks):
        tiles = A.tiles(block)
        for t, (name, kind, _w, bias, dst) in enumerate(tiles):
            for s in range(STREAMS):
                if A.taker(t, kind) != "proj_d":
                    continue
                me = (A.key, block, t, s)
                if kind == "P":
                    dve.wait_ge(*g.at("proj_a", me))
                    o = dst[0](s)[:, dst[1], :]
                    dve.tensor_scalar(o, o, 1.0, None, ALU.min).then_inc(*g.one("shift", me + ("min",)))
                    dve.wait_ge(*g.at("shift", me + ("min",)))
                    dve.scalar_tensor_tensor(out=o, in0=m.bank[s][t % 3][:, 0:N], scalar=0.0, in1=o,
                                             op0=ALU.max, op1=ALU.add).then_inc(*g.one("proj_d", me))
                    continue
                dve.wait_ge(*g.at("proj", me))
                if A.wide and block >= 1:
                    dve.wait_ge(*g.at("pv", (A.key, block - 1, A.units - 1, s)))
                if kind in ("R0", "R1"):
                    table = m.W["L3a"][:, A.col["cos" if kind == "R0" else "sin"][0]:][:, 0:T]
                    if t >= 2:
                        dve.wait_ge(*g.at("proj_p", (A.key, name[0], int(name[-1]) - 1, s) if name[-1] != "0"
                                          else (A.key, "q", 3, s)))
                    dve.scalar_tensor_tensor(
                        out=A.turn_tmp(s, 0 if kind == "R0" else 1),
                        in0=m.bank[s][t % 3][:, :].rearrange("p (b t) -> p b t", t=T),
                        scalar=bias, in1=table[:, None, :].to_broadcast([128, NB, T]),
                        op0=ALU.add, op1=ALU.mult).then_inc(*g.one("proj_d", me))
                elif kind == "V":
                    dve.tensor_copy(A.v(s)[:, :, :, 0:A.dh].rearrange("p b h d -> p (b h) d"),
                                    m.bank[s][t % 3][0:A.Tk, :].rearrange("p (a d) -> p a d", d=A.dh))\
                       .then_inc(*g.one("proj_d", me))
                else:
                    n = NC_ if kind[0] == "C" else N
                    o = dst[0](s)[:, dst[1], :]
                    if bias is None:
                        dve.tensor_copy(o, m.bank[s][t % 3][:, 0:n]).then_inc(*g.one("proj_d", me))
                    else:
                        dve.tensor_scalar(o, m.bank[s][t % 3][:, 0:n], bias, None, ALU.add)\
                           .then_inc(*g.one("proj_d", me))

        def scores(s, k):
            return m.bank[s][k % 2][:, 0:A.items * A.Tk].rearrange("p (a c) -> p a c", c=A.Tk)

        def shift(k):
            me = lambda s, step: (A.key, block, k, s, step)
            top = lambda s: m.small[s][:, 4 * (k % 2):4 * (k % 2) + A.items]
            if A.masked:
                for s in range(STREAMS):
                    dve.wait_ge(*g.at("scores", (A.key, block, k, s)))
                    if k >= 2:
                        dve.wait_ge(*g.at("turn", (A.key, block, k - 2, s)))
                    if not A.wide:
                        dve.wait_ge(*g.at("mask", s))
                    if A.wide:
                        mask = m.const["causal"][:, None, :]
                    else:
                        b = k // 4
                        mask = m.mask[:, s, b * C:(b + 1) * C][:, None, :]
                    dve.scalar_tensor_tensor(out=A.p(s, k), in0=scores(s, k), scalar=A.scale,
                                             in1=mask.to_broadcast([128, A.items, A.Tk]),
                                             op0=ALU.mult, op1=ALU.add).then_inc(*g.one("shift", me(s, "z")))
            for s in range(STREAMS):
                if A.masked:
                    dve.wait_ge(*g.at("shift", me(s, "z")))
                else:
                    dve.wait_ge(*g.at("scores", (A.key, block, k, s)))
                dve.tensor_reduce(top(s), A.p(s, k) if A.masked else scores(s, k), AX.X, ALU.max)\
                   .then_inc(*g.one("shift", me(s, "m")))
            for s in range(STREAMS):
                dve.wait_ge(*g.at("shift", me(s, "m")))
                if k >= 2:
                    dve.wait_ge(*g.at("turn", (A.key, block, k - 2, s)))
                dve.tensor_tensor(A.p(s, k), A.p(s, k) if A.masked else scores(s, k),
                                  top(s)[:, :, None].to_broadcast([128, A.items, A.Tk]), ALU.subtract)\
                   .then_inc(*g.one("shift", me(s, "e")))

        def causal_products(k):
            for s in range(STREAMS):
                dve.wait_ge(*g.at("scores", (A.key, block, k, s)))
                if k >= 2:
                    dve.wait_ge(*g.at("pv", (A.key, block, k - 2, s)))
                dve.tensor_tensor(A.pT(s, k), m.bank[s][k % 2][:, :].rearrange("p (a c) -> p a c", c=T),
                                  m.const["upper"][:, None, :].to_broadcast([128, A.items, T]), ALU.mult)\
                   .then_inc(*g.one("prob_d", (A.key, block, k, s)))

        def norm(gr):
            u = gr * A.group
            me = lambda s, step: (A.key, block, gr, s, step)
            nt = A.items if (A.wide or A.single) else H
            rec = lambda s: m.small[s][:, 8 + 16 * (gr % 2):8 + 16 * (gr % 2) + nt]
            for s in range(STREAMS):
                dve.wait_ge(*g.at("pv", (A.key, block, u + A.group - 1, s)))
                if A.linear:
                    dve.tensor_scalar(rec(s), A.o(s, u)[:, :, A.dh], 1e-6, None, ALU.max)\
                       .then_inc(*g.one("norm", me(s, "c")))
                    dve.wait_ge(*g.at("norm", me(s, "c")))
                    dve.reciprocal(rec(s), rec(s)).then_inc(*g.one("norm", me(s, "r")))
                else:
                    dve.reciprocal(rec(s), A.o(s, u)[:, :, A.dh]).then_inc(*g.one("norm", me(s, "r")))
            for s in range(STREAMS):
                dve.wait_ge(*g.at("norm", me(s, "r")))
                if A.wide and block >= 1 and gr == 0:
                    dve.wait_ge(*g.at("ctx_tr", (A.key, block - 1, s)))
                dve.tensor_tensor(A.on_slice(s, u), A.o(s, u)[:, :, 0:A.dh],
                                  rec(s)[:, :, None].to_broadcast([128, nt, A.dh]), ALU.mult)\
                   .then_inc(*g.one("norm", me(s, "n")))

        for k in range(A.units + 2):
            if k < A.units:
                (causal_products if A.linear else shift)(k)
            u = k - 2
            if u >= 0 and u % A.group == A.group - 1:
                norm(u // A.group)
        for s in range(STREAMS):
            dve.wait_ge(*g.at("out", (A.key, block, s)))
            if g.last_upd[s] is not None:
                dve.wait_ge(*g.at(*g.last_upd[s]))
            else:
                dve.wait_ge(m.s_ctx[s], g.i * 16 + 16)
            dve.tensor_tensor(m.x[s].rearrange("p b d -> p (b d)"), m.bank[s][0][:, :],
                              base[s].rearrange("p b d -> p (b d)"), ALU.add)\
               .then_inc(*g.one("x_upd", (A.key, block, s)))
            g.last_upd[s] = ("x_upd", (A.key, block, s))
        base = m.x


def attention_pool(pool, g, m, A):
    for s in range(STREAMS):
        pool.memset(A.v(s)[:, :, :, A.dh:A.dh + 1].rearrange("p b h d -> p (b h) d"), 1.0)\
            .then_inc(*g.one("proj_p", (A.key, "ones", s)))
    if A.rotated:
        for n, dst in (("q", A.q), ("k", A.k)):
            for j in range(4):
                for s in range(STREAMS):
                    t = 2 * j + (8 if n == "k" else 0)
                    pool.wait_ge(*g.at("proj_d", (A.key, 0, t + 1, s)))
                    pool.tensor_tensor(dst(s)[:, j, :].rearrange("p (b t) -> p b t", t=T),
                                       A.turn_tmp(s, 0), A.turn_tmp(s, 1), ALU.add)\
                        .then_inc(*g.one("proj_p", (A.key, n, j, s)))



def norm_dve(dve, g, m, key, src, dst, made=None):
    for s in range(STREAMS):
        if made is not None:
            dve.wait_ge(*g.at("ln_xn", (made, s)))
        elif g.last_upd[s] is None:
            dve.wait_ge(m.s_xin[s], g.i * 16 + 16)
        else:
            dve.wait_ge(*g.at(*g.last_upd[s]))
        for b in range(NB):
            last = dve.bn_stats(m.st[s][:, b, :], src[s][:, b, :])
        last.then_inc(*g.one("ln_stat", (key, s)))
    for s in range(STREAMS):
        dve.wait_ge(*g.at("ln_stat", (key, s)))
        dve.memset(m.carrier[:, s:s + 1], 0.0)
        for b in range(NB):
            last = dve.bn_aggr(m.mv[s][:, b, :], m.st[s][:, b, :])
        last.then_inc(*g.one("ln_aggr", (key, s)))
    for s in range(STREAMS):
        dve.wait_ge(*g.at("ln_aggr", (key, s)))
        dve.tensor_scalar(m.ve[s][:, :], m.mv[s][:, :, 1], EPS, None, ALU.add)\
           .then_inc(*g.one("ln_var", (key, s)))
    for s in range(STREAMS):
        dve.wait_ge(*g.at("ln_rstd", (key, s)))
        for b in range(NB):
            last = dve.tensor_scalar(dst[s][:, b, :], src[s][:, b, :], m.mv[s][:, b, 0:1], m.rs[s][:, b:b + 1],
                                     ALU.subtract, ALU.mult)
        last.then_inc(*g.one("ln_xn", (key, s)))


def norm_pool(pool, g, m, key):
    for s in range(STREAMS):
        pool.wait_ge(*g.at("ln_var", (key, s)))
        pool.tensor_tensor(m.rs[s][:, :], m.ve[s][:, :], m.const["neghalf"], ALU.pow)\
            .then_inc(*g.one("ln_rstd", (key, s)))


def turn_pe(pe, g, m, key, src, free):
    for s in range(STREAMS):
        if key == "L3f":
            pe.wait_ge(*g.at("qf_d", ("r3", s)))
        else:
            pe.wait_ge(*g.at("ln_xn", (key + "i" if key in NESTED else key, s)))
        g.wait_free(pe, free, s, 2)
        for b in range(NB):
            last = pe.transpose(m.bank[s][2][:, b * T:(b + 1) * T], src[s][:, b, :], m.const["ident"])
        last.then_inc(*g.one("ln_tr", (key, s)))
        free[s, 2] = ("ln_xT", (key, s))


def turn_act(act, g, m, key, gain=None, shift=None):
    for s in range(STREAMS):
        act.wait_ge(*g.at("ln_tr", (key, s)))
        if gain is None:
            act.activation(m.xT[s][:, :], m.bank[s][2][:, :], ACT.Copy).then_inc(*g.one("ln_xT", (key, s)))
        else:
            act.activation(m.xT[s][:, :], m.bank[s][2][:, :], ACT.Identity, bias=shift, scale=gain)\
               .then_inc(*g.one("ln_xT", (key, s)))



class Router:
    def __init__(self, m, key):
        self.m, self.key = m, key
        at = m.cols[key][1]["r"][0]
        self.w = m.W[key][:, at:at + E]

    def part(self, s, at, *shape):
        return cut(self.m.small[s], at, *shape)

    def logits(self, s):
        return self.m.bank[s][3][:, 0:NB * E].rearrange("p (b e) -> p b e", e=E)


def router_pe(pe, g, m, R, free):
    for s in range(STREAMS):
        pe.wait_ge(*g.at("ln_xT", (R.key, s)))
        g.wait_free(pe, free, s, 3)
        for b in range(NB):
            last = pe.matmul(m.bank[s][3][:, E * b:E * b + E], m.xT[s][:, b * T:(b + 1) * T], R.w,
                             start=True, stop=True)
        last.then_inc(*g.one("rt_pe", (R.key, s)))
        free[s, 3] = ("rt_d", (R.key, s, "shift"))


def router_act(act, g, m, R):
    for s in range(STREAMS):
        act.wait_ge(*g.at("rt_d", (R.key, s, "shift")))
        act.activation(R.part(s, 80, NB, E), R.part(s, 80, NB, E), ACT.Exp).then_inc(*g.one("rt_a", (R.key, s, "e")))
    if R.key == "L0f":
        for s in range(STREAMS):
            act.wait_ge(*g.at("rt_d", (R.key, s, "gap")))
            act.activation(R.part(s, 224, NB), R.part(s, 224, NB), ACT.Exp).then_inc(*g.one("rt_a", (R.key, s, "x")))


def router_dve(dve, g, m, R):
    def step(s, name, last):
        last.then_inc(*g.one("rt_d", (R.key, s, name)))

    def after(s, name):
        dve.wait_ge(*g.at("rt_d", (R.key, s, name)))

    wide = lambda v: v[:, :, None].to_broadcast([128, NB, E])
    both = range(STREAMS)
    p = lambda s: R.part(s, 80, NB, E)
    top = lambda s: R.part(s, 112, NB, 8)
    idx = lambda s: R.part(s, 144, NB, 2)
    w = lambda s: R.part(s, 152, NB, 2)
    cw = lambda s: R.part(s, 160, NB, E)
    tmp = lambda s: R.part(s, 192, NB, E)
    a1 = lambda s: R.part(s, 224, NB)
    a2 = lambda s: R.part(s, 228, NB)
    for s in both:
        dve.wait_ge(*g.at("rt_pe", (R.key, s)))
        step(s, "max", dve.tensor_reduce(a1(s), R.logits(s), AX.X, ALU.max))
    for s in both:
        after(s, "max")
        step(s, "shift", dve.tensor_tensor(p(s), R.logits(s), wide(a1(s)), ALU.subtract))
    for s in both:
        dve.wait_ge(*g.at("rt_a", (R.key, s, "e")))
        step(s, "sum", dve.tensor_reduce(a1(s), p(s), AX.X, ALU.add))
    for s in both:
        after(s, "sum")
        step(s, "rec", dve.reciprocal(a2(s), a1(s)))
    for s in both:
        after(s, "rec")
        step(s, "p", dve.tensor_tensor(p(s), p(s), wide(a2(s)), ALU.mult))
    for s in both:
        after(s, "p")
        dve.memset(m.carrier[:, 2 + s:3 + s], 0.0)
        for b in range(NB):
            last = dve.max(top(s)[:, b, :], p(s)[:, b, :])
        step(s, "top", last)
    for s in both:
        after(s, "top")
        dve.memset(m.carrier[:, 4 + s:5 + s], 0.0)
        for b in range(NB):
            last = dve.max_index(m.idx[s][:, b, :], top(s)[:, b, :], p(s)[:, b, :])
        step(s, "idx", last)
    for s in both:
        after(s, "idx")
        step(s, "idxf", dve.tensor_copy(idx(s), m.idx[s][:, :, 0:2]))
    if R.key == "L0f":
        for s in both:
            step(s, "gap", dve.tensor_tensor(a1(s), top(s)[:, :, 1], top(s)[:, :, 0], ALU.subtract))
        for s in both:
            dve.wait_ge(*g.at("rt_a", (R.key, s, "x")))
            step(s, "one", dve.tensor_scalar(a2(s), a1(s), 1.0, None, ALU.add))
        for s in both:
            after(s, "one")
            step(s, "w1", dve.reciprocal(w(s)[:, :, 0], a2(s)))
        for s in both:
            after(s, "w1")
            step(s, "w", dve.tensor_tensor(w(s)[:, :, 1], w(s)[:, :, 0], a1(s), ALU.mult))
    elif R.key == "L1f":
        for s in both:
            step(s, "two", dve.tensor_tensor(a1(s), top(s)[:, :, 1], top(s)[:, :, 0], ALU.add))
        for s in both:
            after(s, "two")
            step(s, "one", dve.reciprocal(a2(s), a1(s)))
        for s in both:
            after(s, "one")
            step(s, "w", dve.tensor_tensor(w(s), top(s)[:, :, 0:2], a2(s)[:, :, None].to_broadcast([128, NB, 2]),
                                           ALU.mult))
    else:
        for s in both:
            after(s, "idxf")
            step(s, "m0", dve.tensor_scalar(w(s)[:, :, 0], idx(s)[:, :, 0], 0.0, None, ALU.is_equal))
            step(s, "m1", dve.tensor_scalar(w(s)[:, :, 1], idx(s)[:, :, 1], 1.0, None, ALU.is_equal))
        for s in both:
            after(s, "m1")
            step(s, "w", dve.tensor_tensor(w(s), w(s), top(s)[:, :, 0:2], ALU.mult))
        return
    eight = m.const["eight"][:, None, :].to_broadcast([128, NB, E])
    for s in both:
        after(s, "w")
        step(s, "e0", dve.tensor_tensor(cw(s), eight, wide(idx(s)[:, :, 0]), ALU.is_equal))
        step(s, "e1", dve.tensor_tensor(tmp(s), eight, wide(idx(s)[:, :, 1]), ALU.is_equal))
    for s in both:
        after(s, "e1")
        step(s, "f0", dve.tensor_tensor(cw(s), cw(s), wide(w(s)[:, :, 0]), ALU.mult))
        step(s, "f1", dve.tensor_tensor(tmp(s), tmp(s), wide(w(s)[:, :, 1]), ALU.mult))
    for s in both:
        after(s, "f1")
        step(s, "cw", dve.tensor_tensor(cw(s), cw(s), tmp(s), ALU.add))


class Experts:

    def __init__(self, m, key):
        self.m, self.key = m, key
        self.gated = key == "L0f"
        self.F = F0 if self.gated else F1
        self.ft = self.F // 128
        self.col = m.cols[key][1]

    def w(self, name, lo, hi):
        at = self.col[name][0]
        return self.m.W[self.key][:, at + lo:at + hi]

    def h(self, s, e, f):
        return cut(self.m.big[s], 2048 * (e % 2) + 512 * f, N)

    def gate(self, s, t):
        return cut(self.m.big[s], 4096 + 512 * (t % 2), N)

    def cwT(self, s):
        return cut(self.m.big[s], 5120, N)[0:E]

    def cw(self, s, b, e):
        return self.m.small[s][:, 160 + E * b + e:161 + E * b + e]


def experts_pe(pe, g, m, X, free):
    if not X.gated:
        for s in range(STREAMS):
            pe.wait_ge(*g.at("rt_d", (X.key, s, "cw")))
            g.wait_free(pe, free, s, 0)
            for b in range(NB):
                last = pe.transpose(m.bank[s][0][0:E, b * T:(b + 1) * T], cut(m.small[s], 160, NB, E)[:, b, :],
                                    m.const["ident"])
            last.then_inc(*g.one("ff_pe", (X.key, "cwT", s)))
            free[s, 0] = ("ff_a", (X.key, "cwT", s))
        for s in range(STREAMS):
            pe.wait_ge(*g.at("ff_a", (X.key, "cwT", s)))
            g.wait_free(pe, free, s, 3)
            for b in range(NB):
                last = pe.matmul(m.bank[s][3][:, b * D:(b + 1) * D], X.cwT(s)[:, b * T:(b + 1) * T],
                                 X.w("b2", 0, 128)[0:E], start=True, stop=True)
            last.then_inc(*g.one("dn_pe", (X.key, "b2", s)))
            free[s, 3] = ("dn_d", (X.key, "b2", s))
    turn = 0
    for e in range(E + 1):
        for f in range(X.ft):
            if e == E:
                break
            lo = e * X.F + 128 * f
            for name in (("gate", "up") if X.gated else ("w1",)):
                for s in range(STREAMS):
                    k = turn % 3
                    g.wait_free(pe, free, s, k)
                    pe.matmul(m.bank[s][k][:, :], X.w(name, lo, lo + 128), m.xT[s][:, :], start=True, stop=True)\
                      .then_inc(*g.one("ff_pe", (X.key, name, e, f, s)))
                    free[s, k] = ("ff_d" if name == "up" else "ff_a", (X.key, e, f, s))
                turn += 1
        if e >= 1:
            for s in range(STREAMS):
                pe.wait_ge(*g.at("ff_d" if X.gated else "ff_a", (X.key, e - 1, X.ft - 1, s)))
                g.wait_free(pe, free, s, 3)
                for b in range(NB):
                    for f in range(X.ft):
                        k = (e - 1) * X.ft + f
                        last = pe.matmul(m.bank[s][3][:, b * D:(b + 1) * D], X.h(s, e - 1, f)[:, b * T:(b + 1) * T],
                                         X.w("down" if X.gated else "w2", 128 * k, 128 * k + 128),
                                         start=(f == 0), stop=(f == X.ft - 1))
                last.then_inc(*g.one("dn_pe", (X.key, e - 1, s)))
                free[s, 3] = ("dn_d", (X.key, e - 1, s))


def experts_act(act, g, m, X):
    if not X.gated:
        for s in range(STREAMS):
            act.wait_ge(*g.at("ff_pe", (X.key, "cwT", s)))
            act.activation(X.cwT(s), m.bank[s][0][0:E, :], ACT.Copy).then_inc(*g.one("ff_a", (X.key, "cwT", s)))
    turn = 0
    for e in range(E):
        for f in range(X.ft):
            for s in range(STREAMS):
                t = e * X.ft + f
                if X.gated:
                    act.wait_ge(*g.at("ff_pe", (X.key, "gate", e, f, s)))
                    if t >= 2:
                        act.wait_ge(*g.at("ff_d", (X.key, (t - 2) // X.ft, (t - 2) % X.ft, s)))
                    act.activation(X.gate(s, t), m.bank[s][turn % 3][:, :], ACT.Silu)\
                       .then_inc(*g.one("ff_a", (X.key, e, f, s)))
                else:
                    act.wait_ge(*g.at("ff_pe", (X.key, "w1", e, f, s)))
                    if e >= 2:
                        act.wait_ge(*g.at("dn_pe", (X.key, e - 2, s)))
                    act.activation(X.h(s, e, f), m.bank[s][turn % 3][:, :], ACT.Gelu, bias=X.w("b1", t, t + 1))\
                       .then_inc(*g.one("ff_a", (X.key, e, f, s)))
            turn += 2 if X.gated else 1


def experts_dve(dve, g, m, X):
    for s in range(STREAMS):
        dve.wait_ge(*g.at("rt_d", (X.key, s, "cw")))
    if not X.gated:
        for s in range(STREAMS):
            dve.tensor_tensor(m.x[s][:, :, :], m.x[s][:, :, :], m.xn[s][:, :, :], ALU.add)\
               .then_inc(*g.one("x_upd", (X.key, "res", s)))
        for s in range(STREAMS):
            dve.wait_ge(*g.at("dn_pe", (X.key, "b2", s)))
            dve.wait_ge(*g.at("x_upd", (X.key, "res", s)))
            dve.tensor_tensor(m.x[s].rearrange("p b d -> p (b d)"), m.bank[s][3][:, :],
                              m.x[s].rearrange("p b d -> p (b d)"), ALU.add)\
               .then_inc(*g.one("dn_d", (X.key, "b2", s)))
    turn = 1
    for e in range(E + 1):
        for f in range(X.ft):
            if e == E or not X.gated:
                break
            for s in range(STREAMS):
                t = e * X.ft + f
                dve.wait_ge(*g.at("ff_a", (X.key, e, f, s)))
                dve.wait_ge(*g.at("ff_pe", (X.key, "up", e, f, s)))
                if e >= 2:
                    dve.wait_ge(*g.at("dn_pe", (X.key, e - 2, s)))
                dve.tensor_tensor(X.h(s, e, f), m.bank[s][turn % 3][:, :], X.gate(s, t), ALU.mult)\
                   .then_inc(*g.one("ff_d", (X.key, e, f, s)))
            turn += 2
        if e >= 1:
            for s in range(STREAMS):
                dve.wait_ge(*g.at("dn_pe", (X.key, e - 1, s)))
                if e >= 2:
                    dve.wait_ge(*g.at("dn_d", (X.key, e - 2, s)))
                elif not X.gated:
                    dve.wait_ge(*g.at("dn_d", (X.key, "b2", s)))
                for b in range(NB):
                    last = dve.scalar_tensor_tensor(out=m.x[s][:, b, :], in0=m.bank[s][3][:, b * D:(b + 1) * D],
                                                    scalar=X.cw(s, b, e - 1), in1=m.x[s][:, b, :],
                                                    op0=ALU.mult, op1=ALU.add)
                last.then_inc(*g.one("dn_d", (X.key, e - 1, s)))
    for s in range(STREAMS):
        g.last_upd[s] = ("dn_d", (X.key, E - 1, s))



class Mamba:

    def __init__(self, m):
        self.m, self.key = m, "L2a"
        self.col = m.cols["L2a"][1]

    def w(self, name, lo=0, hi=None):
        at, width = self.col[name]
        return self.m.W["L2a"][:, at + lo:at + (width if hi is None else hi)]

    def xi(self, s, half):
        return cut(self.m.big[s], 536 * half, NB, T + 6)

    def sz(self, s, half):
        return cut(self.m.big[s], 1072 + 512 * half, N)

    def u(self, s, half):
        return cut(self.m.big[s], 2096 + 512 * half, N)

    def dl(self, s, half):
        return cut(self.m.big[s], 3120 + 512 * half, N)

    def du(self, s, half):
        return cut(self.m.big[s], 4144 + 512 * half, N)

    def parts(self, s):
        return cut(self.m.big[s], 5168, 256).bitcast(BF16)[0:96]

    def dA(self, s, half):
        return cut(self.m.big[s], 5424 + 512 * half, N)

    def h(self, s, half):
        return cut(self.m.big[s], 6448 + 512 * half, N)

    def rest(self, s):
        return self.dA(s, 0)[0:96]

    def mid(self, s):
        return cut(self.m.big[s], 5936, 256).bitcast(BF16)[0:96]

    def dtT(self, s):
        return self.h(s, 1)[0:DTR]

    def mo(self, s, way):
        return self.m.xT[s][:, :] if way == 0 else self.dl(s, 0)

    def timed(self, v, way):
        v = v.rearrange("p (b t) -> p b t", t=T)
        return v if way == 0 else v[:, :, ::-1]


def mamba_pe(pe, g, m, M, free):
    both = range(STREAMS)
    for k in range(4):
        for s in both:
            pe.wait_ge(*g.at("ln_xT", ("L2a", s)))
            g.wait_free(pe, free, s, k)
            pe.matmul(m.bank[s][k][:, :], M.w("in", 128 * k, 128 * k + 128), m.xT[s][:, :], start=True, stop=True)\
              .then_inc(*g.one("mb_pe", ("in", k, s)))
            free[s, k] = ("mb_d", ("xi", k, s)) if k < 2 else ("mb_a", ("sz", k - 2, s))
    for way in range(2):
        for s in both:
            pe.wait_ge(*g.at("mb_a", ("u", way, 1, s)))
            if way == 0:
                g.wait_free(pe, free, s, 0)
            for half in range(2):
                last = pe.matmul(m.bank[s][0][0:96, :], M.w("bc3", 96 * half, 96 * half + 96), M.u(s, half),
                                 start=half == 0, stop=half == 1)
            last.then_inc(*g.one("mb_pe", ("bc", way, s)))
            free[s, 0] = ("mb_d", ("rest", way, s))
            g.wait_free(pe, free, s, 1)
            for half in range(2):
                last = pe.matmul(m.bank[s][1][0:DTR, :], M.w("xdt", DTR * half, DTR * half + DTR), M.u(s, half),
                                 start=half == 0, stop=half == 1)
            last.then_inc(*g.one("mb_pe", ("xdt", way, s)))
            free[s, 1] = ("mb_a", ("dtT", way, s))
        for s in both:
            pe.wait_ge(*g.at("mb_a", ("dtT", way, s)))
            for half in range(2):
                if way == 1:
                    g.wait_free(pe, free, s, 2 + half)
                pe.matmul(m.bank[s][2 + half][:, :], M.w("dt", 128 * half, 128 * half + 128)[0:DTR], M.dtT(s),
                          start=True, stop=True).then_inc(*g.one("mb_pe", ("dt", way, half, s)))
                free[s, 2 + half] = ("mb_d", ("abs", way, half, s))

        def spread(n):
            for k, row in ((0, n), (1, NS + n)):
                for s in both:
                    if n == 0:
                        pe.wait_ge(*g.at("mb_d", ("parts", way, s)))
                    g.wait_free(pe, free, s, k)
                    pe.matmul(m.bank[s][k][:, :], m.sel3[0:96, row:row + 1].to_broadcast([96, 128]), M.parts(s),
                              start=True, stop=True).then_inc(*g.one("sc_bc", (way, n, k, s)))
                    free[s, k] = ("sc_d", (way, n, ("in", "out")[k], 1, s))

        spread(0)
        for n in range(NS):
            if n + 1 < NS:
                spread(n + 1)
            for half in range(2):
                for s in both:
                    pe.wait_ge(*g.at("sc_d", (way, n, "out", half, s)))
                    if n == 0:
                        g.wait_free(pe, free, s, 2 + half)
                    last = pe.matmul(m.bank[s][2 + half][:, :], m.const["ident"], M.h(s, half),
                                     start=n == 0, stop=n == NS - 1)
                    last.then_inc(*g.one("sc_y", (way, n, half, s)))
                    free[s, 2 + half] = ("mb_d", ("yd", way, half, s))
        for s in both:
            g.wait_free(pe, free, s, 0)
            for half in range(2):
                pe.wait_ge(*g.at("mb_d", ("gated", way, half, s)))
                last = pe.matmul(m.bank[s][0][:, :], M.w("out", 128 * half, 128 * half + 128), M.du(s, half),
                                 start=half == 0, stop=half == 1)
            last.then_inc(*g.one("mb_pe", ("out", way, s)))
            free[s, 0] = ("mb_a", ("mo", way, s))
    for s in both:
        pe.wait_ge(*g.at("mb_a", ("mo", 1, s)))
        g.wait_free(pe, free, s, 1)
        for way in range(2):
            last = pe.matmul(m.bank[s][1][:, :], M.w("dim", 128 * way, 128 * way + 128), M.mo(s, way),
                             start=way == 0, stop=way == 1)
        last.then_inc(*g.one("mb_pe", ("dim", s)))
        free[s, 1] = ("mb_a", ("gelu", s))
    for s in both:
        pe.wait_ge(*g.at("mb_a", ("gelu", s)))
        row = m.rows["glu"]
        for pair in range(2):
            bank = m.bank[s][2 + pair]
            g.wait_free(pe, free, s, 2 + pair)
            for b in range(2):
                for part in range(2):
                    dst = bank[:, 256 * b + 128 * part:256 * b + 128 * part + 128]
                    pe.matmul(dst, bias_picker(m, row + part, T), m.brow[:, :], start=True, stop=False)
                    at = (2 * pair + b) * T
                    last = pe.matmul(dst, M.u(s, 0)[:, at:at + T], M.w("glu", 128 * part, 128 * part + 128),
                                     start=False, stop=True)
            last.then_inc(*g.one("mb_pe", ("glu", pair, s)))
            free[s, 2 + pair] = ("mb_d", ("prod", pair, s))


def mamba_act(act, g, m, M):
    both = range(STREAMS)
    for half in range(2):
        for s in both:
            act.wait_ge(*g.at("mb_pe", ("in", 2 + half, s)))
            act.activation(M.sz(s, half), m.bank[s][2 + half][:, :], ACT.Silu)\
               .then_inc(*g.one("mb_a", ("sz", half, s)))
    for way in range(2):
        for half in range(2):
            for s in both:
                act.wait_ge(*g.at("mb_d", ("conv", way, half, DC - 1, s)))
                act.activation(M.u(s, half), M.u(s, half), ACT.Silu, bias=M.w("convb", half, half + 1))\
                   .then_inc(*g.one("mb_a", ("u", way, half, s)))
        for s in both:
            act.wait_ge(*g.at("mb_pe", ("xdt", way, s)))
            act.activation(M.dtT(s), m.bank[s][1][0:DTR, :], ACT.Copy).then_inc(*g.one("mb_a", ("dtT", way, s)))
        for half in range(2):
            for s in both:
                act.wait_ge(*g.at("mb_d", ("abs", way, half, s)))
                act.activation(M.dl(s, half), M.dl(s, half), ACT.Exp, bias=M.w("dtb", half, half + 1))\
                   .then_inc(*g.one("mb_a", ("exp", way, half, s)))
        for half in range(2):
            for s in both:
                act.wait_ge(*g.at("mb_a", ("exp", way, half, s)))
                act.activation(M.dl(s, half), M.dl(s, half), ACT.Ln, bias=1.0)\
                   .then_inc(*g.one("mb_a", ("ln", way, half, s)))
        for n in range(NS):
            for half in range(2):
                for s in both:
                    if n == 0:
                        act.wait_ge(*g.at("mb_d", ("far", way, half, s)))
                        act.wait_ge(*g.at("mb_d", ("parts", way, s)))
                    else:
                        act.wait_ge(*g.at("sc_d", (way, n - 1, "scan", half, s)))
                    act.activation(M.dA(s, half), M.dl(s, half), ACT.Exp,
                                   scale=m.Aneg[:, NS * half + n:NS * half + n + 1])\
                       .then_inc(*g.one("sc_da", (way, n, half, s)))
        for s in both:
            act.wait_ge(*g.at("mb_pe", ("out", way, s)))
            act.activation(M.mo(s, way), m.bank[s][0][:, :], ACT.Copy).then_inc(*g.one("mb_a", ("mo", way, s)))
    for s in both:
        act.wait_ge(*g.at("mb_pe", ("dim", s)))
        act.activation(M.u(s, 0), m.bank[s][1][:, :], ACT.Gelu, bias=M.w("dimb"))\
           .then_inc(*g.one("mb_a", ("gelu", s)))
    for pair in range(2):
        for s in both:
            act.wait_ge(*g.at("mb_pe", ("glu", pair, s)))
            act.activation(cut(m.big[s], 2608 + 256 * pair, 2, T),
                           m.bank[s][2 + pair][:, :].rearrange("p (b c t) -> p b c t", b=2, c=2)[:, :, 1, :],
                           ACT.Sigmoid).then_inc(*g.one("mb_a", ("sig", pair, s)))


def mamba_pool(pool, g, m, M):
    for s in range(STREAMS):
        for half in range(2):
            for at in (0, T + 3):
                last = pool.memset(M.xi(s, half)[:, :, at:at + 3], 0.0)
        last.then_inc(*g.one("mb_p", ("pad", s)))


def mamba_dve(dve, g, m, M):
    both = range(STREAMS)
    for half in range(2):
        for s in both:
            dve.wait_ge(*g.at("mb_pe", ("in", half, s)))
            dve.tensor_copy(M.xi(s, half)[:, :, 3:3 + T],
                            m.bank[s][half][:, :].rearrange("p (b t) -> p b t", t=T))\
               .then_inc(*g.one("mb_d", ("xi", half, s)))
    for s in both:
        dve.wait_ge(*g.at("mb_p", ("pad", s)))
        dve.tensor_tensor(m.x[s][:, :, :], m.x[s][:, :, :], m.xn[s][:, :, :], ALU.add)\
           .then_inc(*g.one("x_upd", ("L2a", "res", s)))
    for way in range(2):
        for j in range(DC):
            for half in range(2):
                for s in both:
                    at = j if way == 0 else 6 - j
                    src = M.xi(s, half)[:, :, at:at + T]
                    dst = M.timed(M.u(s, half), way)
                    tap = M.w("conv", DC * half + j, DC * half + j + 1)
                    if j == 0:
                        dve.wait_ge(*g.at("mb_d", ("xi", half, s)))
                        ins = dve.tensor_scalar(dst, src, tap, None, ALU.mult)
                    else:
                        dve.wait_ge(*g.at("mb_d", ("conv", way, half, j - 1, s)))
                        ins = dve.scalar_tensor_tensor(out=dst, in0=src, scalar=tap, in1=dst,
                                                       op0=ALU.mult, op1=ALU.add)
                    ins.then_inc(*g.one("mb_d", ("conv", way, half, j, s)))
        for s in both:
            dve.wait_ge(*g.at("mb_pe", ("bc", way, s)))
            dve.tensor_copy(M.parts(s), m.bank[s][0][0:96, :]).then_inc(*g.one("mb_d", ("hi", way, s)))
        for s in both:
            dve.wait_ge(*g.at("mb_d", ("hi", way, s)))
            dve.tensor_tensor(M.rest(s), m.bank[s][0][0:96, :], M.parts(s), ALU.subtract)\
               .then_inc(*g.one("mb_d", ("rest", way, s)))
        for s in both:
            dve.wait_ge(*g.at("mb_d", ("rest", way, s)))
            dve.tensor_copy(M.mid(s), M.rest(s)).then_inc(*g.one("mb_d", ("mid", way, s)))
        for s in both:
            dve.wait_ge(*g.at("mb_d", ("mid", way, s)))
            dve.tensor_copy(M.parts(s)[32:64], M.mid(s)[32:64])
            dve.tensor_tensor(M.parts(s)[64:96], M.rest(s)[64:96], M.mid(s)[64:96], ALU.subtract)\
               .then_inc(*g.one("mb_d", ("parts", way, s)))
        for half in range(2):
            for s in both:
                b = M.w("dtb", half, half + 1)
                dve.wait_ge(*g.at("mb_pe", ("dt", way, half, s)))
                dve.tensor_scalar(M.h(s, half), m.bank[s][2 + half][:, :], b, 0.0, ALU.add, ALU.max)\
                   .then_inc(*g.one("mb_d", ("pos", way, half, s)))
        for half in range(2):
            for s in both:
                dve.wait_ge(*g.at("mb_d", ("pos", way, half, s)))
                dve.scalar_tensor_tensor(out=M.dl(s, half), in0=M.h(s, half), scalar=-2.0,
                                         in1=m.bank[s][2 + half][:, :], op0=ALU.mult, op1=ALU.add)\
                   .then_inc(*g.one("mb_d", ("abs", way, half, s)))
        for half in range(2):
            for s in both:
                dve.wait_ge(*g.at("mb_a", ("ln", way, half, s)))
                dve.wait_ge(*g.at("mb_d", ("pos", way, half, s)))
                dve.tensor_tensor(M.dl(s, half), M.dl(s, half), M.h(s, half), ALU.add)\
                   .then_inc(*g.one("mb_d", ("delta", way, half, s)))
        for half in range(2):
            for s in both:
                dve.wait_ge(*g.at("mb_d", ("delta", way, half, s)))
                dve.tensor_tensor(M.du(s, half), M.dl(s, half), M.u(s, half), ALU.mult)\
                   .then_inc(*g.one("mb_d", ("du", way, half, s)))
        for half in range(2):
            for s in both:
                dve.wait_ge(*g.at("mb_d", ("du", way, half, s)))
                dve.memset(M.dl(s, half).rearrange("p (b t) -> p b t", t=T)[:, :, 0:1], FAR)\
                   .then_inc(*g.one("mb_d", ("far", way, half, s)))
        for n in range(NS):
            for half in range(2):
                for s in both:
                    dve.wait_ge(*g.at("sc_bc", (way, n, 0, s)))
                    if n >= 1:
                        dve.wait_ge(*g.at("sc_y", (way, n - 1, half, s)))
                    dve.tensor_tensor(M.h(s, half), m.bank[s][0][:, :], M.du(s, half), ALU.mult)\
                       .then_inc(*g.one("sc_d", (way, n, "in", half, s)))
            for half in range(2):
                for s in both:
                    dve.wait_ge(*g.at("sc_da", (way, n, half, s)))
                    dve.wait_ge(*g.at("sc_d", (way, n, "in", half, s)))
                    dve.tensor_tensor_scan(M.h(s, half), M.dA(s, half), M.h(s, half), 0.0, ALU.mult, ALU.add)\
                       .then_inc(*g.one("sc_d", (way, n, "scan", half, s)))
            for half in range(2):
                for s in both:
                    dve.wait_ge(*g.at("sc_bc", (way, n, 1, s)))
                    dve.wait_ge(*g.at("sc_d", (way, n, "scan", half, s)))
                    dve.tensor_tensor(M.h(s, half), m.bank[s][1][:, :], M.h(s, half), ALU.mult)\
                       .then_inc(*g.one("sc_d", (way, n, "out", half, s)))
        for half in range(2):
            for s in both:
                dve.wait_ge(*g.at("sc_y", (way, NS - 1, half, s)))
                dve.wait_ge(*g.at("sc_d", (way, NS - 1, "in", half, s)))
                dve.scalar_tensor_tensor(out=M.timed(M.du(s, half), way),
                                         in0=M.u(s, half).rearrange("p (b t) -> p b t", t=T),
                                         scalar=M.w("dskip", half, half + 1),
                                         in1=m.bank[s][2 + half][:, :].rearrange("p (b t) -> p b t", t=T),
                                         op0=ALU.mult, op1=ALU.add).then_inc(*g.one("mb_d", ("yd", way, half, s)))
        for half in range(2):
            for s in both:
                dve.wait_ge(*g.at("mb_d", ("yd", way, half, s)))
                dve.tensor_tensor(M.du(s, half), M.du(s, half), M.sz(s, half), ALU.mult)\
                   .then_inc(*g.one("mb_d", ("gated", way, half, s)))
    for pair in range(2):
        for s in both:
            dve.wait_ge(*g.at("mb_a", ("sig", pair, s)))
            dve.tensor_tensor(cut(m.big[s], 4144 + 256 * pair, 2, T),
                              m.bank[s][2 + pair][:, :].rearrange("p (b c t) -> p b c t", b=2, c=2)[:, :, 0, :],
                              cut(m.big[s], 2608 + 256 * pair, 2, T), ALU.mult)\
               .then_inc(*g.one("mb_d", ("prod", pair, s)))
    for s in both:
        dve.wait_ge(*g.at("mb_d", ("prod", 1, s)))
        dve.tensor_tensor(m.x[s][:, :, :], m.x[s][:, :, :], cut(m.big[s], 4144, NB, T), ALU.add)\
           .then_inc(*g.one("x_upd", ("L2a", s)))
        g.last_upd[s] = ("x_upd", ("L2a", s))



def maps_pe(pe, g, m, free):
    col = m.cols["L2f"][1]
    for k in range(2):
        for s in range(STREAMS):
            pe.wait_ge(*g.at("ln_xT", ("L2f", s)))
            g.wait_free(pe, free, s, k)
            for b in range(NB):
                dst = m.bank[s][k][:, b * D:(b + 1) * D]
                pe.matmul(dst, bias_picker(m, m.rows[f"L2f{k}"], T), m.brow[:, :], start=True, stop=False)
                last = pe.matmul(dst, m.xT[s][:, b * T:(b + 1) * T],
                                 m.W["L2f"][:, col[f"w{k}"][0]:][:, 0:D], start=False, stop=True)
            last.then_inc(*g.one("ff_pe", ("L2f", k, s)))
            free[s, k] = ("ff_a", ("L2f", k, s))


def maps_act(act, g, m):
    for k in range(2):
        for s in range(STREAMS):
            act.wait_ge(*g.at("ff_pe", ("L2f", k, s)))
            act.activation(cut(m.big[s], 512 * k, N), m.bank[s][k][:, :], ACT.Silu)\
               .then_inc(*g.one("ff_a", ("L2f", k, s)))


def maps_dve(dve, g, m):
    for k in range(2):
        for s in range(STREAMS):
            dve.wait_ge(*g.at("rt_d", ("L2f", s, "w")))
            dve.wait_ge(*g.at("ff_a", ("L2f", k, s)))
            if k == 1:
                dve.wait_ge(*g.at("dn_d", ("L2f", 0, s)))
            for b in range(NB):
                at = 152 + 2 * b + k
                last = dve.scalar_tensor_tensor(out=m.x[s][:, b, :], in0=cut(m.big[s], 512 * k, NB, D)[:, b, :],
                                                scalar=m.small[s][:, at:at + 1], in1=m.x[s][:, b, :],
                                                op0=ALU.mult, op1=ALU.add)
            last.then_inc(*g.one("dn_d", ("L2f", k, s)))
            g.last_upd[s] = ("dn_d", ("L2f", 1, s))



class Quantised:

    def __init__(self, m):
        self.m = m
        self.col = m.cols["L3f"][1]

    def w(self, name, lo=0, hi=None):
        at, width = self.col[name]
        return self.m.W["L3f"][:, at + lo:at + (width if hi is None else hi)]

    def xq(self, s):
        return cut(self.m.big[s], 0, NB, D)

    def hp(self, s, j):
        return cut(self.m.big[s], 512 + 520 * j, NB, T + 2)

    def hs(self, s, j):
        return cut(self.m.big[s], 2592 + 512 * j, NB, T)

    def qT(self, s):
        return cut(self.m.big[s], 4640, 1024).bitcast(BF16).rearrange("p (j n) -> p j n", n=N)

    def qa(self, s, b):
        return cut(self.m.big[s], 5664 + 512 * (b % 2), HID)

    def qb(self, s, b):
        return cut(self.m.big[s], 6688 + 256 * (b % 2), 256).bitcast(BF16)

    def sm(self, s, k, b=None):
        v = self.m.small[s]
        return v[:, 4 * k:4 * k + 4] if b is None else v[:, 4 * k + b:4 * k + b + 1]


def quantised_pe(pe, g, m, Q, free):
    both = range(STREAMS)
    for j in range(4):
        for s in both:
            k = j % 2
            pe.wait_ge(*g.at("ln_xT", ("L3f", s)))
            g.wait_free(pe, free, s, k)
            pe.matmul(m.bank[s][k][:, :], Q.w("w1", 128 * j, 128 * j + 128), m.xT[s][:, :], start=True, stop=True)\
              .then_inc(*g.one("qf_pe", ("h", j, s)))
            free[s, k] = ("qf_a", ("h", j, s))
    for b in range(NB + 1):
        for s in both:
            if b < NB:
                if b == 0:
                    pe.wait_ge(*g.at("qf_a", ("hs", 3, s)))
                if b >= 2:
                    g.wait_free(pe, free, s, b % 2)
                for j in range(4):
                    last = pe.transpose(m.bank[s][b % 2][:, 128 * j:128 * j + 128], Q.hs(s, j)[:, b, :],
                                        m.const["ident"])
                last.then_inc(*g.one("qf_pe", ("tok", b, s)))
                free[s, b % 2] = ("qf_d", ("q1", b, s))
        for s in both:
            if b >= 1:
                pe.wait_ge(*g.at("qf_d", ("q3", b - 1, s)))
                g.wait_free(pe, free, s, 2)
                for j in range(4):
                    last = pe.transpose(m.bank[s][2][:, :].bitcast(BF16)[:, 128 * j:128 * j + 128],
                                        Q.qb(s, b - 1)[:, 128 * j:128 * j + 128], m.identb[:, :])
                last.then_inc(*g.one("qf_pe", ("back", b - 1, s)))
                free[s, 2] = ("qf_a", ("qT", b - 1, s))
    for s in both:
        g.wait_free(pe, free, s, 3)
        pe.wait_ge(*g.at("qf_a", ("qT", NB - 1, s)))
        for b in range(NB):
            for j in range(4):
                last = pe.matmul(m.bank[s][3][:, b * D:(b + 1) * D], Q.qT(s)[:, j, b * T:(b + 1) * T],
                                 m.w2t[:, 128 * j:128 * j + 128], start=j == 0, stop=j == 3)
        last.then_inc(*g.one("qf_pe", ("out", s)))
        free[s, 3] = ("x_upd", ("L3f", s))


def quantised_act(act, g, m, Q):
    both = range(STREAMS)
    for j in range(4):
        for s in both:
            act.wait_ge(*g.at("qf_pe", ("h", j, s)))
            act.activation(Q.hp(s, j)[:, :, 1:T + 1], m.bank[s][j % 2][:, :].rearrange("p (b t) -> p b t", t=T),
                           ACT.Copy).then_inc(*g.one("qf_a", ("h", j, s)))
    for j in range(4):
        for s in both:
            act.wait_ge(*g.at("qf_d", ("conv", j, 2, s)))
            act.activation(Q.hs(s, j), Q.hs(s, j), ACT.Silu, bias=Q.w("convb", j, j + 1))\
               .then_inc(*g.one("qf_a", ("hs", j, s)))
    for b in range(NB):
        for s in both:
            act.wait_ge(*g.at("qf_pe", ("back", b, s)))
            act.activation(Q.qT(s)[:, :, b * T:(b + 1) * T],
                           m.bank[s][2][:, :].bitcast(BF16)[:, 0:512].rearrange("p (j t) -> p j t", t=T),
                           ACT.Copy).then_inc(*g.one("qf_a", ("qT", b, s)))


def quantised_pool(pool, g, m, Q):
    for s in range(STREAMS):
        for j in range(4):
            for at in (0, T + 1):
                last = pool.memset(Q.hp(s, j)[:, :, at:at + 1], 0.0)
        last.then_inc(*g.one("qf_p", ("pad", s)))


def quantise_tokens_dve(dve, g, m, Q):
    both = range(STREAMS)

    def step(s, name, last):
        last.then_inc(*g.one("qf_d", (name, s)))

    def after(s, name):
        dve.wait_ge(*g.at("qf_d", (name, s)))

    for s in both:
        dve.wait_ge(*g.at("ln_xn", ("L3f", s)))
        step(s, "abs", dve.scalar_tensor_tensor(out=Q.xq(s), in0=m.xn[s][:, :, :], scalar=-1.0, in1=m.xn[s][:, :, :],
                                                op0=ALU.mult, op1=ALU.max))
    for s in both:
        after(s, "abs")
        step(s, "am", dve.tensor_reduce(Q.sm(s, 0), Q.xq(s), AX.X, ALU.max))
    for s in both:
        after(s, "am")
        step(s, "clip", dve.tensor_scalar(Q.sm(s, 0), Q.sm(s, 0), 1e-5, None, ALU.max))
    for s in both:
        after(s, "clip")
        step(s, "rec", dve.reciprocal(Q.sm(s, 1), Q.sm(s, 0)))
    for s in both:
        after(s, "rec")
        step(s, "sc", dve.tensor_scalar(Q.sm(s, 1), Q.sm(s, 1), 127.0, None, ALU.mult))
    for s in both:
        after(s, "sc")
        step(s, "inv", dve.reciprocal(Q.sm(s, 2), Q.sm(s, 1)))
    for s in both:
        for b in range(NB):
            last = dve.tensor_scalar(Q.xq(s)[:, b, :], m.xn[s][:, b, :], Q.sm(s, 1, b), 127.0, ALU.mult, ALU.min)
        step(s, "r1", last)
    for s in both:
        after(s, "r1")
        step(s, "r2", dve.tensor_scalar(Q.xq(s), Q.xq(s), -128.0, ROUND, ALU.max, ALU.add))
    for s in both:
        after(s, "r2")
        after(s, "inv")
        for b in range(NB):
            last = dve.tensor_scalar(Q.xq(s)[:, b, :], Q.xq(s)[:, b, :], ROUND, Q.sm(s, 2, b),
                                     ALU.subtract, ALU.mult)
        step(s, "r3", last)


def quantised_dve(dve, g, m, Q):
    both = range(STREAMS)
    for j in range(4):
        for tap in range(3):
            for s in both:
                src, w = Q.hp(s, j)[:, :, tap:tap + T], Q.w("conv", 3 * j + tap, 3 * j + tap + 1)
                if tap == 0:
                    dve.wait_ge(*g.at("qf_a", ("h", j, s)))
                    dve.wait_ge(*g.at("qf_p", ("pad", s)))
                    ins = dve.tensor_scalar(Q.hs(s, j), src, w, None, ALU.mult)
                else:
                    dve.wait_ge(*g.at("qf_d", ("conv", j, tap - 1, s)))
                    ins = dve.scalar_tensor_tensor(out=Q.hs(s, j), in0=src, scalar=w, in1=Q.hs(s, j),
                                                   op0=ALU.mult, op1=ALU.add)
                ins.then_inc(*g.one("qf_d", ("conv", j, tap, s)))
    for b in range(NB):
        def step(s, name, last):
            last.then_inc(*g.one("qf_d", (name, b, s)))

        def after(s, name):
            dve.wait_ge(*g.at("qf_d", (name, b, s)))

        for s in both:
            dve.wait_ge(*g.at("qf_pe", ("tok", b, s)))
            step(s, "mx", dve.tensor_reduce(Q.sm(s, 4, b), m.bank[s][b % 2][:, :], AX.X, ALU.max))
            step(s, "mn", dve.tensor_reduce(Q.sm(s, 5, b), m.bank[s][b % 2][:, :], AX.X, ALU.min))
        for s in both:
            after(s, "mn")
            step(s, "m", dve.scalar_tensor_tensor(out=Q.sm(s, 6, b), in0=Q.sm(s, 5, b), scalar=-1.0,
                                                  in1=Q.sm(s, 4, b), op0=ALU.mult, op1=ALU.max))
        for s in both:
            after(s, "m")
            step(s, "mc", dve.tensor_scalar(Q.sm(s, 6, b), Q.sm(s, 6, b), 1e-5, None, ALU.max))
        for s in both:
            after(s, "mc")
            step(s, "mr", dve.reciprocal(Q.sm(s, 7, b), Q.sm(s, 6, b)))
        for s in both:
            after(s, "mr")
            step(s, "ms", dve.tensor_scalar(Q.sm(s, 7, b), Q.sm(s, 7, b), 127.0, None, ALU.mult))
        for s in both:
            after(s, "ms")
            step(s, "q1", dve.tensor_scalar(Q.qa(s, b), m.bank[s][b % 2][:, :], Q.sm(s, 7, b), 127.0,
                                            ALU.mult, ALU.min))
        for s in both:
            after(s, "q1")
            step(s, "q2", dve.tensor_scalar(Q.qa(s, b), Q.qa(s, b), -128.0, ROUND, ALU.max, ALU.add))
        for s in both:
            after(s, "q2")
            if b >= 2:
                dve.wait_ge(*g.at("qf_pe", ("back", b - 2, s)))
            step(s, "q3", dve.tensor_scalar(Q.qb(s, b), Q.qa(s, b), ROUND, None, ALU.subtract))
    for s in both:
        dve.reciprocal(Q.sm(s, 8), Q.sm(s, 7)).then_inc(*g.one("qf_d", ("inv2", s)))
    for s in both:
        dve.wait_ge(*g.at("qf_d", ("inv2", s)))
        dve.tensor_scalar(Q.sm(s, 8), Q.sm(s, 8), m.wsc[:, 3:4], None, ALU.mult).then_inc(*g.one("qf_d", ("f", s)))
    for s in both:
        dve.wait_ge(*g.at("qf_d", ("f", s)))
        dve.wait_ge(*g.at("qf_pe", ("out", s)))
        for b in range(NB):
            last = dve.scalar_tensor_tensor(out=m.x[s][:, b, :], in0=m.bank[s][3][:, b * D:(b + 1) * D],
                                            scalar=Q.sm(s, 8, b), in1=m.x[s][:, b, :], op0=ALU.mult, op1=ALU.add)
        last.then_inc(*g.one("x_upd", ("L3f", s)))
        g.last_upd[s] = ("x_upd", ("L3f", s))



class Gauge:

    def __init__(self, m, tally, i):
        self.m, self.tally, self.i = m, tally, i
        self.last_upd = [None] * STREAMS

    def at(self, signal, name):
        return self.m.sem[signal], self.tally.value(signal, name, self.i)

    def one(self, signal, name):
        self.tally.count(signal, name)
        return self.m.sem[signal], 1

    def wait_free(self, pe, free, s, k):
        if (s, k) in free:
            pe.wait_ge(*self.at(*free[s, k]))


def write_program(nc, m, tally, last):
    A = {key: Attention(m, key) for key in ("L0a", "L0x", "L1a", "L1x", "L2x", "L3a", "L3x")}
    R = {key: Router(m, key) for key in ("L0f", "L1f", "L2f")}
    X = {key: Experts(m, key) for key in ("L0f", "L1f")}
    M = Mamba(m)
    Q = Quantised(m)
    order = ["L0a", "L0x", "L0f", "L1a", "L1x", "L1f", "L2a", "L2x", "L2f", "L3a", "L3x", "L3f"][:last]
    at = m.cols["const"][1]
    m.const = {n: m.W["const"][:, a:a + width] for n, (a, width) in at.items()}
    done = {}
    inner = [t[:, :].rearrange("p (b d) -> p b d", d=D) for t in m.xT]

    quantised = [Q.xq(s) for s in range(STREAMS)]

    with nc.Block() as block:

        @block.tensor
        def _(pe):
            setup_pe(pe, m)
            with pe.Fori(0, PASSES) as i:
                g, free = Gauge(m, tally, i), {}
                for key in order:
                    pe.wait_ge(m.s_w[key], 16)
                    turn_pe(pe, g, m, key, inner if key in NESTED else quantised if key == "L3f" else m.xn, free)
                    if key in A:
                        attention_pe(pe, g, m, A[key], free)
                    if key in R:
                        router_pe(pe, g, m, R[key], free)
                    if key in X:
                        experts_pe(pe, g, m, X[key], free)
                    if key == "L2a":
                        mamba_pe(pe, g, m, M, free)
                    if key == "L2f":
                        maps_pe(pe, g, m, free)
                    if key == "L3f":
                        quantised_pe(pe, g, m, Q, free)

        @block.scalar
        def _(act):
            setup_act(act, m)
            with act.Fori(0, PASSES) as i:
                g = Gauge(m, tally, i)
                for key in order:
                    act.wait_ge(m.s_w[key], 16)
                    if key in NESTED:
                        gain, shift = (m.W[key][:, a:a + 1] for a, _ in (m.cols[key][1]["g"], m.cols[key][1]["b"]))
                        turn_act(act, g, m, key, gain, shift)
                    else:
                        turn_act(act, g, m, key)
                    if key in A:
                        attention_act(act, g, m, A[key])
                    if key in R:
                        router_act(act, g, m, R[key])
                    if key in X:
                        experts_act(act, g, m, X[key])
                    if key == "L2a":
                        mamba_act(act, g, m, M)
                    if key == "L2f":
                        maps_act(act, g, m)
                    if key == "L3f":
                        quantised_act(act, g, m, Q)

        @block.vector
        def _(dve):
            setup_dve(dve, m)
            with dve.Fori(0, PASSES) as i:
                g = Gauge(m, tally, i)
                for key in order:
                    dve.wait_ge(m.s_w[key], 16)
                    base = m.xin if key == "L0a" else m.x
                    norm_dve(dve, g, m, key, base, m.xn)
                    if key in NESTED:
                        norm_dve(dve, g, m, key + "i", m.xn, inner, made=key)
                    if key == "L3f":
                        quantise_tokens_dve(dve, g, m, Q)
                    if key == "L1x":
                        mask_dve(dve, g, m)
                    if key in A:
                        attention_dve(dve, g, m, A[key], base)
                    if key in R:
                        router_dve(dve, g, m, R[key])
                    if key in X:
                        experts_dve(dve, g, m, X[key])
                    if key == "L2a":
                        mamba_dve(dve, g, m, M)
                    if key == "L2f":
                        maps_dve(dve, g, m)
                    if key == "L3f":
                        quantised_dve(dve, g, m, Q)
                done.update(enumerate(g.last_upd))

        @block.gpsimd
        def _(pool):
            setup_pool(pool, m)
            with pool.Fori(0, PASSES) as i:
                g = Gauge(m, tally, i)
                for key in order:
                    norm_pool(pool, g, m, key)
                    if key in NESTED:
                        norm_pool(pool, g, m, key + "i")
                    if key in A:
                        attention_pool(pool, g, m, A[key])
                    if key == "L2a":
                        mamba_pool(pool, g, m, M)
                    if key == "L3f":
                        quantised_pool(pool, g, m, Q)

        @block.sync
        def _(sp):
            def load_x(i, s):
                lo = (i * STREAMS + s) * NB
                sp.dma_start(m.xin[s][:, :, :], m.ins["x"][lo:lo + NB].rearrange("b t d -> t b d"))\
                  .then_inc(m.s_xin[s], 16)

            def load_context(i, s):
                lo = (i * STREAMS + s) * NB
                sp.dma_start(m.ctxT[s][:, :], m.ins["ctxT"][:, lo * C:(lo + NB) * C]).then_inc(m.s_ctx[s], 16)
                sp.dma_start(m.mask8[:, s, :], m.ins["mask"][:, lo * C:(lo + NB) * C]).then_inc(m.s_mask[s], 16)

            sp.dma_start(m.W["const"][:, :], m.ins["w_const"]).then_inc(m.s_w["const"], 16)
            sp.dma_start(m.brow[:, :], m.ins["rows"]).then_inc(m.s_rows, 16)
            for s in range(STREAMS):
                load_x(0, s)
                load_context(0, s)
            for key in list(m.W)[1:]:
                sp.dma_start(m.W[key][:, :], m.ins["w_" + key]).then_inc(m.s_w[key], 16)
            for i in range(PASSES):
                g = Gauge(m, tally, i)
                for s in range(STREAMS):
                    if i + 1 < PASSES:
                        sp.wait_ge(*g.at("x_upd", ("L0a", 0, s)))
                        load_x(i + 1, s)
                for s in range(STREAMS):
                    lo = (i * STREAMS + s) * NB
                    sp.wait_ge(*g.at(*done[s]))
                    sp.dma_start(m.out[lo:lo + NB].rearrange("b t d -> t b d"), m.x[s][:, :, :])\
                      .then_inc(m.s_out[s], 16)
                for s in range(STREAMS):
                    sp.wait_ge(m.s_out[s], 16 * (i + 1))
                    if i + 1 < PASSES:
                        load_context(i + 1, s)


def build(nc, ins, out, cols, rows, nrows, numbers, last):
    with ExitStack() as ctx:
        m = declare(nc, ins, out, cols, rows, nrows, ctx)
        tally = Tally(numbers)
        write_program(nc, m, tally, last)
    return tally.numbers


def setup_pe(pe, m):
    pe.wait_ge(m.s_w["const"], 16)
    pe.wait_ge(m.s_rows, 16)
    pe.wait_ge(m.s_pre_d, 5)
    pe.matmul(m.bank[0][0][:, 0:2], m.const["ones"], m.wsc[:, 0:2], start=True, stop=True).then_inc(m.s_pre_pe, 1)
    pe.wait_ge(m.s_pre_d, PRE_D)


def setup_act(act, m):
    act.wait_ge(m.s_w["const"], 16)
    act.wait_ge(m.s_w["L2a"], 16)
    at = m.cols["L2a"][1]["alog"][0]
    act.activation(m.Aneg[:, :], m.W["L2a"][:, at:at + 2 * NS], ACT.Exp).then_inc(m.s_pre_a, 1)
    act.wait_ge(m.s_pre_a, 1)
    act.activation(m.Aneg[:, :], m.Aneg[:, :], ACT.Copy, scale=-1.0).then_inc(m.s_pre_a, 1)
    act.wait_ge(m.s_pre_a, 2)


def setup_dve(dve, m):
    dve.wait_ge(m.s_w["const"], 16)
    ident = m.const["ident"]
    dve.tensor_tensor(m.sel3[0:32, :], ident[0:32, 0:32], ident[0:32, 32:64], ALU.add)
    dve.tensor_tensor(m.sel3[32:64, :], ident[32:64, 32:64], ident[32:64, 0:32], ALU.add)
    dve.tensor_tensor(m.sel3[64:96, :], ident[64:96, 64:96], ident[64:96, 0:32], ALU.add)
    dve.tensor_copy(m.identb[:, :], ident).then_inc(m.s_pre_d, 1)

    dve.wait_ge(m.s_w["L3f"], 16)
    col = m.cols["L3f"][1]
    w = [m.W["L3f"][:, col[n][0]:col[n][0] + HID] for n in ("w1", "w2")]
    made = 1
    for k in range(2):
        t = cut(m.big[0], 512 * k, HID)
        dve.scalar_tensor_tensor(out=t, in0=w[k], scalar=-1.0, in1=w[k], op0=ALU.mult, op1=ALU.max)\
           .then_inc(m.s_pre_d, 1)
        dve.wait_ge(m.s_pre_d, made + 1)
        dve.tensor_reduce(m.wsc[:, k:k + 1], t, AX.X, ALU.add).then_inc(m.s_pre_d, 1)
        made += 2
    dve.wait_ge(m.s_pre_pe, 1)
    dve.tensor_scalar(m.wsc[:, 2:4], m.bank[0][0][:, 0:2], 1.0 / (D * HID), 1e-5, ALU.mult, ALU.max)\
       .then_inc(m.s_pre_d, 1)
    dve.wait_ge(m.s_pre_d, made + 1)
    dve.reciprocal(m.wsc[:, 4:6], m.wsc[:, 2:4]).then_inc(m.s_pre_d, 1)
    dve.wait_ge(m.s_pre_d, made + 2)
    made += 2
    for k in range(2):
        dve.tensor_scalar(w[k], w[k], m.wsc[:, 4 + k:5 + k], ROUND, ALU.mult, ALU.add).then_inc(m.s_pre_d, 1)
        dve.wait_ge(m.s_pre_d, made + 1)
        dve.tensor_scalar(w[k], w[k], ROUND, 1.0, ALU.subtract, ALU.min).then_inc(m.s_pre_d, 1)
        dve.wait_ge(m.s_pre_d, made + 2)
        if k == 0:
            dve.tensor_scalar(w[0], w[0], -1.0, m.wsc[:, 2:3], ALU.max, ALU.mult).then_inc(m.s_pre_d, 1)
        else:
            dve.tensor_scalar(m.w2t[:, :], w[1], -1.0, None, ALU.max).then_inc(m.s_pre_d, 1)
        made += 3
    assert made == PRE_D


def setup_pool(pool, m):
    pool.wait_ge(m.s_w["const"], 16)



def kernel(**inputs):
    import concourse.bacc as bacc
    from concourse.bass_utils import run_bass_kernel_spmd

    w = {k: np.asarray(v) for k, v in inputs.items()}
    blocks = layouts(w)
    arrays, cols = {}, {}
    for st, parts in blocks.items():
        at, where = 0, {}
        for name, a in parts.items():
            assert a.shape[0] == 128, (st, name, a.shape)
            where[name] = (at, a.shape[1])
            at += a.shape[1]
        cols[st] = (at, where)
        arrays["w_" + st] = np.ascontiguousarray(np.concatenate(list(parts.values()), axis=1))
    rows, stack = {}, []
    for name, a in bias_rows(w).items():
        rows[name] = len(stack)
        stack += list(a.reshape(-1, 128))
    arrays["rows"] = np.stack(stack)
    arrays["x"] = np.ascontiguousarray(w["x"])
    arrays["ctxT"] = np.ascontiguousarray(w["ctx_1024"].transpose(2, 0, 1).reshape(D, B * C))
    arrays["mask"] = np.ascontiguousarray(
        np.broadcast_to(w["mask_BxS2_bk0"].reshape(1, B * C), (128, B * C)))

    numbers = None
    for _ in range(2):
        nc = bacc.Bacc("TRN2", target_bir_lowering=False, num_devices=1)
        ins = {n: nc.dram_tensor(n, a.shape, U8 if n == "mask" else F32, kind="ExternalInput").ap()
               for n, a in arrays.items()}
        out = nc.dram_tensor("out", (B, T, D), F32, kind="ExternalOutput").ap()
        numbers = build(nc, ins, out, cols, rows, len(stack), numbers, LAST)
    r = run_bass_kernel_spmd(nc, [arrays], core_ids=[0])
    return r.results[0]["out"]
```

```python
from contextlib import ExitStack

import numpy as np
import concourse.bass as bass
from concourse import mybir

ALU = mybir.AluOpType
ACT = mybir.ActivationFunctionType
AX = mybir.AxisListType
F32 = mybir.dt.float32
BF16 = mybir.dt.bfloat16
U32 = mybir.dt.uint32
U8 = mybir.dt.uint8

B, T, D, C = 32, 128, 128, 77
NB = 4
STREAMS = 2
PASSES = B // (NB * STREAMS)
N = NB * T
NC_ = NB * C
H, DH = 16, 8
H1, DH1 = 16, 64
E = 8
F0, F1 = 256, 512
DI, NS, DTR, DC = 256, 16, 64, 4
HID = 512
EPS = 1e-5
NEG = -1e9
ROUND = 12582912.0
FAR = 1e30
PRE_D = 17
NESTED = ("L1f", "L2a")
LAST = 12
SCRATCH = 7984



def spread_heads(w):
    out = np.zeros((w.shape[0], 4, 4, 32), w.dtype)
    out[:, :, :, :DH] = w.reshape(w.shape[0], 4, 4, DH).transpose(0, 2, 1, 3)
    return out.reshape(w.shape[0], 512)


def spread_bias(b):
    return np.ascontiguousarray(spread_heads(b[None, :]).reshape(4, 128).T)


def swap_halves(w):
    return w.reshape(w.shape[0], H, 2, DH // 2)[:, :, ::-1, :].reshape(w.shape[0], H * DH)


def k_tiles(w):
    k = w.shape[0] // 128
    return w.reshape(k, 128, -1).transpose(1, 0, 2).reshape(128, -1)


def rows_below(w):
    out = np.zeros((128, w.shape[1]), w.dtype)
    out[:w.shape[0]] = w
    return out


def rotation_tables():
    half = DH // 2
    theta = np.float32(10000.0) ** (-np.arange(half, dtype=np.float32) / np.float32(half))
    angle = np.arange(T, dtype=np.float32)[None, :] * theta[:, None]
    cos = np.zeros((4, 32, T), np.float32)
    sin = np.zeros((4, 32, T), np.float32)
    cos[:, :half], cos[:, half:DH] = np.cos(angle), np.cos(angle)
    sin[:, :half], sin[:, half:DH] = -np.sin(angle), np.sin(angle)
    return cos.reshape(128, T), sin.reshape(128, T)


def layouts(w):
    cat = lambda *a: np.concatenate(a, axis=1)
    cos, sin = rotation_tables()
    qkv = w["L0_attn_w_qkv"]
    p = {}
    p["const"] = {
        "ident": np.eye(128, dtype=np.float32),
        "upper": np.triu(np.ones((128, 128), np.float32)),
        "causal": np.where(np.tril(np.ones((128, 128))), 0.0, -1e30).astype(np.float32),
        "ones": np.ones((128, 128), np.float32),
        "eight": np.tile(np.arange(8, dtype=np.float32), (128, 1)),
        "neghalf": np.full((128, 4), -0.5, np.float32),
    }
    p["L0a"] = {"q": spread_heads(qkv[0:128].T), "k": spread_heads(qkv[128:256].T), "v": qkv[256:384].T,
                "o": w["L0_attn_w_out"].T}
    p["L0x"] = {"q": w["L0_xattn_Wq"].T, "k": w["L0_xattn_Wk"].T, "v": w["L0_xattn_Wv"].T,
                "o": w["L0_xattn_Wo"].T, "qb": w["L0_xattn_bq"][:, None]}
    p["L0f"] = {"r": w["L0_ffn_router_kernel_DE"],
                "gate": w["L0_ffn_kernel_gating_EDF"].transpose(1, 0, 2).reshape(D, E * F0),
                "up": w["L0_ffn_kernel_up_EDF"].transpose(1, 0, 2).reshape(D, E * F0),
                "down": k_tiles(w["L0_ffn_kernel_down_EFD"].reshape(E * F0, D))}
    heads = lambda a: a.transpose(1, 0, 2).reshape(D, H1 * DH1)
    p["L1a"] = {"q": heads(w["L1_attn_P_q"]), "k": heads(w["L1_attn_P_k"]), "v": heads(w["L1_attn_P_v"]),
                "o": k_tiles(w["L1_attn_P_o"].transpose(0, 2, 1).reshape(H1 * DH1, D))}
    p["L1x"] = {"q": spread_heads(w["L1_xattn_Wq"].T), "k": spread_heads(w["L1_xattn_Wk"].T),
                "v": w["L1_xattn_Wv"].T, "o": w["L1_xattn_Wo"].T,
                "qb": spread_bias(w["L1_xattn_bq"]), "kb": spread_bias(w["L1_xattn_bk"])}
    p["L1f"] = {"r": w["L1_ffn_gate_w"], "g": w["L1_ffn_gamma"][:, None], "b": w["L1_ffn_beta"][:, None],
                "w1": w["L1_ffn_w1"].transpose(1, 0, 2).reshape(D, E * F1),
                "b1": w["L1_ffn_b1"].reshape(E * F1 // 128, 128).T,
                "w2": k_tiles(w["L1_ffn_w2"].reshape(E * F1, D)),
                "b2": rows_below(w["L1_ffn_b2"])}
    xp = w["L2_attn_x_proj_w"].T
    bc = xp[:, DTR:]
    p["L2a"] = {"g": w["L2_attn_ln_g"][:, None], "b": w["L2_attn_ln_b"][:, None],
                "in": w["L2_attn_in_proj_w"].T,
                "conv": k_tiles(w["L2_attn_conv_w"].reshape(DI, DC)), "convb": k_tiles(w["L2_attn_conv_b"][:, None]),
                "bc3": k_tiles(cat(bc, bc, bc)), "xdt": k_tiles(xp[:, :DTR]),
                "dt": rows_below(w["L2_attn_dt_proj_w"].T), "dtb": k_tiles(w["L2_attn_dt_proj_b"][:, None]),
                "alog": k_tiles(w["L2_attn_A_log"]), "dskip": k_tiles(w["L2_attn_D"][:, None]),
                "out": k_tiles(w["L2_attn_out_proj_w"].T),
                "dim": k_tiles(w["L2_attn_dim_reduce_w"].T), "dimb": w["L2_attn_dim_reduce_b"][:, None],
                "glu": w["L2_attn_glu_w"].T}
    p["L2x"] = {"q": spread_heads(w["L2_xattn_wq"].T), "k": spread_heads(w["L2_xattn_wk"].T),
                "v": w["L2_xattn_wv"].T, "o": w["L2_xattn_wo"].T,
                "qb": spread_bias(w["L2_xattn_bq"]), "kb": spread_bias(w["L2_xattn_bk"])}
    p["L2f"] = {"r": w["L2_ffn_gate_w"], "w0": w["L2_ffn_w0"].T, "w1": w["L2_ffn_w1"].T}
    q, k = w["L3_attn_Wq"].T, w["L3_attn_Wk"].T
    qb, kb = w["L3_attn_bq"], w["L3_attn_bk"]
    p["L3a"] = {"q": spread_heads(q), "k": spread_heads(k), "v": w["L3_attn_Wv"].T, "o": w["L3_attn_Wo"].T,
                "qs": spread_heads(swap_halves(q)), "ks": spread_heads(swap_halves(k)),
                "qb": spread_bias(qb), "kb": spread_bias(kb),
                "qsb": spread_bias(swap_halves(qb[None, :])[0]), "ksb": spread_bias(swap_halves(kb[None, :])[0]),
                "cos": cos, "sin": sin}
    kv = w["L3_xattn_Wkv"]
    p["L3x"] = {"q": spread_heads(w["L3_xattn_Wq"].T), "k": spread_heads(kv[:128].T), "v": kv[128:].T,
                "o": w["L3_xattn_Wout"].T}
    p["L3f"] = {"w1": w["L3_ffn_w1"].T, "conv": k_tiles(w["L3_ffn_conv_w"].reshape(HID, 3)),
                "convb": k_tiles(w["L3_ffn_conv_b"][:, None]), "w2": k_tiles(w["L3_ffn_w2"].T)}
    return p


def bias_rows(w):
    return {"L0xv": w["L0_xattn_bv"], "L0xo": w["L0_xattn_bo"], "L1xv": w["L1_xattn_bv"], "L1xo": w["L1_xattn_bo"],
            "glu": w["L2_attn_glu_b"], "L2xv": w["L2_xattn_bv"], "L2xo": w["L2_xattn_bo"],
            "L2f0": w["L2_ffn_b0"], "L2f1": w["L2_ffn_b1"], "L3av": w["L3_attn_bv"], "L3ao": w["L3_attn_bo"],
            "L3xo": w["L3_xattn_bout"]}



class Numbers:

    def __init__(self, known):
        self.final = known is not None
        self.known = known if self.final else {}

    def count(self, signal, name, number):
        names = self.known.setdefault(signal, {})
        assert names.setdefault(name, number) == number, (signal, name)

    def value(self, signal, name, i, ahead=0):
        if not self.final:
            return 1
        per_pass = self.known[signal]
        return i * len(per_pass) + (ahead * len(per_pass) + per_pass[name])


SIGNALS = dict(
    mask="DVE: the additive mask of a stream",
    x_upd="DVE has updated the residual", ln_stat="DVE: statistics", ln_aggr="DVE: mean and variance",
    ln_var="DVE: variance + eps", ln_rstd="Pool: reciprocal deviation", ln_xn="DVE: normalised tile",
    ln_tr="PE: transposed normalised tile", ln_xT="ACT: it is in SBUF",
    proj="PE: a projection is in PSUM", proj_a="ACT has taken a projection", proj_d="DVE has taken a projection",
    proj_p="Pool has finished a projection",
    scores="PE: scores", shift="DVE: a step of the softmax's shift", prob="ACT: exponentials",
    prob_d="DVE: masked products of the linear attention",
    turn="PE: transposed probabilities", turned="ACT: they are in SBUF", pv="PE: probabilities times values",
    norm="DVE: a step of the normalisation", ctx_tr="PE: transposed heads", ctx_a="ACT: they are in SBUF",
    out="PE: output projection",
    rt_pe="PE: router", rt_d="DVE: router", rt_a="ACT: router",
    ff_pe="PE: hidden tile", ff_a="ACT: hidden tile", ff_d="DVE: hidden tile", dn_pe="PE: expert's output",
    dn_d="DVE: expert's output added",
    mb_pe="PE: Mamba", mb_a="ACT: Mamba", mb_d="DVE: Mamba", mb_p="Pool: Mamba",
    sc_bc="PE: a row of B or C on all partitions", sc_da="ACT: decay", sc_d="DVE: scan", sc_y="PE: state added to y",
    qf_pe="PE: quantised network", qf_a="ACT: quantised network", qf_d="DVE: quantised network",
    qf_p="Pool: quantised network",
)


class SharedNames:
    pass


def declare(nc, ins, out, cols, rows, ctx):
    m = SharedNames()
    m.ins, m.out, m.cols, m.rows = ins, out, cols, rows

    def sb(name, shape, dt=F32):
        return ctx.enter_context(nc.sbuf_tensor("sb_" + name, shape, dt))

    m.W = {st: sb("weights_" + st, [128, width]) for st, (width, _) in cols.items()}
    m.brow3 = sb("bias_rows", [128, 128], BF16)
    m.mask8 = sb("mask8", [128, STREAMS, NC_], U8)
    m.sel3 = sb("sel3", [128, 32], BF16)
    m.Aneg = sb("Aneg", [128, 2 * NS])
    m.w2t = sb("w2t", [128, HID], BF16)
    m.identb = sb("identb", [128, 128], BF16)
    m.causalb = sb("causalb", [128, 128], BF16)
    m.wsc = sb("wsc", [128, 8])
    m.carrier = sb("carrier", [128, 6])
    m.xin = [sb(f"xin{s}", [128, NB, D]) for s in range(STREAMS)]
    m.x = [sb(f"x{s}", [128, NB, D]) for s in range(STREAMS)]
    m.xn = [sb(f"xn{s}", [128, NB, D]) for s in range(STREAMS)]
    m.xT = [sb(f"xT{s}", [128, N]) for s in range(STREAMS)]
    m.ctxT = [sb(f"ctxT{s}", [128, NC_]) for s in range(STREAMS)]
    m.st = [sb(f"st{s}", [128, NB, 6]) for s in range(STREAMS)]
    m.mv = [sb(f"mv{s}", [128, NB, 2]) for s in range(STREAMS)]
    m.ve = [sb(f"ve{s}", [128, NB]) for s in range(STREAMS)]
    m.rs = [sb(f"rs{s}", [128, NB]) for s in range(STREAMS)]
    m.small = [sb(f"small{s}", [128, 256]) for s in range(STREAMS)]
    m.idx = [sb(f"idx{s}", [128, NB, 8], U32) for s in range(STREAMS)]
    m.big = [sb(f"big{s}", [128, SCRATCH]) for s in range(STREAMS)]
    m.bank = [[ctx.enter_context(nc.psum_tensor(f"bank{s}{k}", [128, 512], F32)) for k in range(4)]
              for s in range(STREAMS)]
    m.sem = [{name: ctx.enter_context(nc.semaphore(f"s_{name}{s}")) for name in SIGNALS} for s in range(STREAMS)]
    m.s_w = {st: ctx.enter_context(nc.semaphore("s_w_" + st)) for st in cols}
    m.s_rows = ctx.enter_context(nc.semaphore("s_rows"))
    m.s_xin = [ctx.enter_context(nc.semaphore(f"s_xin{s}")) for s in range(STREAMS)]
    m.s_ctx = [ctx.enter_context(nc.semaphore(f"s_ctx{s}")) for s in range(STREAMS)]
    m.s_mask = [ctx.enter_context(nc.semaphore(f"s_mask_in{s}")) for s in range(STREAMS)]
    m.s_out = [ctx.enter_context(nc.semaphore(f"s_stored{s}")) for s in range(STREAMS)]
    m.s_pre_d = ctx.enter_context(nc.semaphore("s_pre_d"))
    m.s_pre_a = ctx.enter_context(nc.semaphore("s_pre_a"))
    m.s_pre_pe = ctx.enter_context(nc.semaphore("s_pre_pe"))
    m.s_pre_p = ctx.enter_context(nc.semaphore("s_pre_p"))
    return m




def cut(t, at, *shape):
    n = int(np.prod(shape))
    v = t[:, at:at + n]
    if len(shape) == 2:
        return v.rearrange("p (a b) -> p a b", b=shape[1])
    if len(shape) == 3:
        return v.rearrange("p (a b c) -> p a b c", b=shape[1], c=shape[2])
    return v



class Attention:

    def __init__(self, m, key):
        self.key, self.m = key, m
        self.ctx = key.endswith("x")
        self.Tk = C if self.ctx else T
        self.wide = key == "L1a"
        self.single = key == "L0x"
        self.linear = key == "L0a"
        self.rotated = key == "L3a"
        self.masked = key == "L1x"
        self.blocks = 4 if self.wide else 1
        self.pairs = 2 if self.wide else 1
        self.dh = DH1 if self.wide else D if self.single else DH
        self.nh = 4 if self.wide else 1 if self.single else H
        self.scale = float(self.dh) ** -0.5
        self.col = m.cols[key][1]
        self.units = 4 if self.wide else 2 if self.single else 16
        self.items = 2 if self.single else 4
        self.group = 1 if (self.wide or self.single) else 4
        self.period = self.units + 4
        self.lag = 1 if self.linear else 3
        self.early = [t for t, x in enumerate(self.tiles(0)) if self.ctx and x[0][0] in "kv"]

        tiles = self.tiles(0)
        self.main = [t for t in range(len(tiles)) if t not in self.early]
        self.before = 0.5 * len(self.main) + 1.2


    def time(self, tick):
        whole = self.before + self.period * self.blocks + 1
        return 0.05 + 0.945 * (tick + self.before) / whole

    def first_tick(self, t):
        return -self.before + 0.5 * self.main.index(t)

    def unit(self, tick, delay):
        block, k = divmod(tick - delay, self.period)
        return (block, k) if 0 <= block < self.blocks and k < self.units else None

    def next_tiles(self, tick):
        block, j = divmod(tick + 4, self.period)
        return (block, range(2 * j, 2 * j + 2)) if 1 <= block < self.blocks and j < 3 else (block, ())

    def finished(self, tick, delay=0):
        block, k = divmod(tick - delay + 1, self.period)
        return block - 1 if k == 0 and 1 <= block <= self.blocks else None

    def bank(self, t):
        if t in self.early:
            return (0, 1, 3)[self.early.index(t) % 3]
        return t % 2 if self.wide else (0, 1, 3, 2)[t % 4]

    def w(self, name, lo=0, hi=None):
        at, width = self.col[name]
        return self.m.W[self.key][:, at + lo:at + (width if hi is None else hi)]

    def q(self, s):
        return cut(self.m.big[s], 0, 4, N)

    def k(self, s):
        return cut(self.m.big[s], 2048, 4, NC_ if self.ctx else N)

    def v(self, s):
        at = 3584 if self.wide else 4096
        return cut(self.m.big[s], at, NB, self.nh, self.dh + 1)[0:self.Tk]

    def v_part(self, s, kind):
        v = self.v(s)[:, :, :, 0:self.dh]
        return v[:, :, 2 * int(kind[1]):2 * int(kind[1]) + 2, :] if self.wide else v

    def p(self, s, u):
        return cut(self.m.big[s], 4736 + 512 * (u % 3), self.items, self.Tk)

    def pT(self, s, u):
        return cut(self.m.big[s], 6272 + 512 * (u % 2), self.items, T)[0:self.Tk]

    def on(self, s):
        return cut(self.m.big[s], 1024 if self.wide else 7296, NB, self.nh, self.dh)

    def on_pair(self, s, pair):
        on = self.on(s)
        if self.wide:
            on = on[:, :, 2 * pair:2 * pair + 2, :]
        return on

    def cT(self, s, pair):
        return cut(self.m.big[s], 6272 + 512 * pair, N)

    def turn_tmp(self, s, k):
        return cut(self.m.big[s], 4736 + 512 * k, NB, T)

    def tiles(self, block):
        out = []
        if self.wide:
            for name, dst in (("q", self.q), ("k", self.k), ("v", None)):
                for pair in range(2):
                    lo = 128 * (2 * block + pair)
                    kind = "T" if dst else f"V{pair}"
                    out.append((name, kind, self.w(name, lo, lo + 128), None, (dst, pair)))
            return out
        for n, dst in (("q", self.q), ("k", self.k)):
            for j in range(1 if self.single else 4):
                src = "C" if n == "k" and self.ctx else "T"
                bias = self.w(n + "b", j, j + 1) if n + "b" in self.col else None
                kind = "P" if self.linear else src
                if self.rotated:
                    out.append((n + str(j), "R0", self.w(n, 128 * j, 128 * j + 128), bias, (dst, j)))
                    out.append((n + "s" + str(j), "R1", self.w(n + "s", 128 * j, 128 * j + 128),
                                self.w(n + "sb", j, j + 1), (dst, j)))
                else:
                    out.append((n + str(j), kind, self.w(n, 128 * j, 128 * j + 128), bias, (dst, j)))
        out.append(("v", "V", self.w("v"), None, None))
        return out

    def taker(self, t, kind):
        if kind in ("P", "R0", "R1"):
            return "proj_d"
        if t in self.early:
            return "proj_a"
        return "proj_a" if t % 2 == 0 else "proj_d"

    def last_taken(self, block):
        last = {}
        tiles = self.tiles(block)
        for t in self.early + [t for t in range(len(tiles)) if t not in self.early]:
            last[self.taker(t, tiles[t][1])] = t
        return last

    def item(self, s, block, u, n):
        q, k = self.q(s), self.k(s)
        if self.wide:
            half = 64 * (u % 2)
            return (q[half:half + 64, u // 2, n * T:(n + 1) * T],
                    k[half:half + 64, u // 2, n * T:(n + 1) * T], n, u)
        if self.single:
            b = 2 * u + n
            return q[:, 0, b * T:(b + 1) * T], k[:, 0, b * C:(b + 1) * C], b, 0
        b, r = u // 4, u % 4
        rows = DH if self.linear else 32
        return (q[32 * r:32 * r + rows, n, b * T:(b + 1) * T],
                k[32 * r:32 * r + rows, n, b * self.Tk:(b + 1) * self.Tk], b, 4 * r + n)

    def o(self, s, u):
        bank = self.m.bank[s][3]
        if self.wide or self.single:
            return bank[:, 0:self.items * (self.dh + 1)].rearrange("p (a c) -> p a c", c=self.dh + 1)
        at = 256 * (u // 4 % 2)
        return bank[:, at:at + H * (DH + 1)].rearrange("p (a c) -> p a c", c=DH + 1)

    def o_slot(self, u, n):
        return n if (self.wide or self.single) else 4 * (u % 4) + n

    def on_slice(self, s, u):
        on = self.on(s)
        if self.wide:
            return on[:, :, u, :]
        if self.single:
            return on[:, 2 * u:2 * u + 2, 0, :]
        return on[:, u // 4, :, :]


def bias_picker(m, row, n):
    return m.sel3[0:96, row:row + 1].to_broadcast([96, n])


def attention_project_pe(pe, g, m, A, free, block, t):
    s = g.s
    name, kind, w, _bias, _dst = A.tiles(block)[t]
    k = A.bank(t)
    bank = m.bank[s][k]
    g.wait_free(pe, free, s, k)
    src = m.ctxT[s] if kind[0] == "C" or (kind[0] == "V" and A.ctx) else m.xT[s]
    if kind[0] == "V":
        brow = m.rows.get(A.key + "v")
        for b in range(NB):
            if brow is not None:
                pe.matmul(bank[0:A.Tk, 128 * b:128 * b + 128], bias_picker(m, brow, A.Tk), m.brow3[0:96, :],
                          start=True, stop=False)
            last = pe.matmul(bank[0:A.Tk, 128 * b:128 * b + 128],
                             src[:, b * A.Tk:(b + 1) * A.Tk], w, start=brow is None, stop=True)
    else:
        n = NC_ if kind[0] == "C" else N
        last = pe.matmul(bank[:, 0:n], w, src[:, 0:n], start=True, stop=True)
    last.then_inc(*g.one("proj", (A.key, block, t)))
    free[s, k] = (A.taker(t, kind), (A.key, block, t))


def attention_early_pe(pe, g, m, A, free):
    yield 0.0
    if A.early:
        pe.wait_ge(*g.context_at())
    for t in A.early:
        attention_project_pe(pe, g, m, A, free, 0, t)


def attention_pe(pe, g, m, A, free):
    s, ident = g.s, m.const["ident"]

    def turn_results(block):
        for pair in range(A.pairs):
            pe.wait_ge(*g.at("norm", (A.key, block, A.units // A.group - 1, "n")))
            g.wait_free(pe, free, s, 2 + pair)
            for b in range(NB):
                last = pe.transpose(m.bank[s][2 + pair][:, b * T:(b + 1) * T], A.on_pair(s, pair)[:, b, :], ident)
            last.then_inc(*g.one("ctx_tr", (A.key, block, pair)))
            free[s, 2 + pair] = ("ctx_a", (A.key, block, pair))

    def output(block):
        pe.wait_ge(*g.at("ctx_a", (A.key, block, A.pairs - 1)))
        if A.pairs == 1:
            g.wait_free(pe, free, s, 3)
        brow = m.rows.get(A.key + "o")
        for b in range(NB):
            dst = m.bank[s][3][:, b * D:(b + 1) * D]
            if brow is not None:
                pe.matmul(dst, bias_picker(m, brow, T), m.brow3[0:96, :], start=True, stop=False)
            for pair in range(A.pairs):
                at = 128 * (A.pairs * block + pair)
                last = pe.matmul(dst, A.cT(s, pair)[:, b * T:(b + 1) * T], A.w("o", at, at + 128),
                                 start=brow is None and pair == 0, stop=pair == A.pairs - 1)
        last.then_inc(*g.one("out", (A.key, block)))
        free[s, 3] = ("x_upd", (A.key, block))

    def scores(block, k):
        if k == 0:
            for taker, t in A.last_taken(block).items():
                pe.wait_ge(*g.at(taker, (A.key, block, t)))
            if A.rotated:
                pe.wait_ge(*g.at("proj_p", (A.key, 7)))
        if free[s, k % 2][0] not in ("proj_a", "proj_d"):
            g.wait_free(pe, free, s, k % 2)
        for n in range(A.items):
            q, kk, b, h = A.item(s, block, k, n)
            if A.linear:
                last = pe.matmul(m.bank[s][k % 2][0:A.Tk, n * T:(n + 1) * T], kk, q, start=True, stop=True)
            else:
                dst = m.bank[s][k % 2][:, n * A.Tk:(n + 1) * A.Tk]
                if A.wide:
                    pe.matmul(dst, m.identb[:, :], m.causalb[:, :], start=True, stop=False)
                last = pe.matmul(dst, q, kk, start=not A.wide, stop=True)
        last.then_inc(*g.one("scores", (A.key, block, k)))
        free[s, k % 2] = (("prob_d", (A.key, block, k)) if A.linear else
                          ("shift", (A.key, block, k, "z" if A.masked else "e")))

    def turn(block, u):
        pe.wait_ge(*g.at("prob", (A.key, block, u)))
        g.wait_free(pe, free, s, 2)
        for n in range(A.items):
            last = pe.transpose(m.bank[s][2][0:A.Tk, n * T:(n + 1) * T], A.p(s, u)[:, n, :], ident)
        last.then_inc(*g.one("turn", (A.key, block, u)))
        free[s, 2] = ("turned", (A.key, block, u))

    def values(block, u):
        pe.wait_ge(*g.at("prob_d" if A.linear else "turned", (A.key, block, u)))
        if u == 0 and block == 0:
            pe.wait_ge(*g.at("proj_p", (A.key, "ones")))
        if u % A.group == 0:
            g.wait_free(pe, free, s, 3)
        for n in range(A.items):
            _q, _k, b, h = A.item(s, block, u, n)
            last = pe.matmul(A.o(s, u)[:, A.o_slot(u, n), :], A.pT(s, u)[:, n, :], A.v(s)[:, b, h, :],
                             start=True, stop=True)
        last.then_inc(*g.one("pv", (A.key, block, u)))
        free[s, 3] = ("norm", (A.key, block, u // A.group, "n"))

    for t in A.main:
        yield A.time(A.first_tick(t))
        pe.wait_ge(*g.at("ln_xT", A.key))
        attention_project_pe(pe, g, m, A, free, 0, t)
    for tick in range(-1, A.period * A.blocks + 1):
        block, tiles = A.next_tiles(tick)
        for t in tiles:
            yield A.time(tick + 0.5 * (t % 2))
            attention_project_pe(pe, g, m, A, free, block, t)
        if A.finished(tick) is not None:
            yield A.time(tick)
            turn_results(A.finished(tick))
        if A.finished(tick, 1) is not None:
            yield A.time(tick)
            output(A.finished(tick, 1))
        if A.unit(tick, 1) and not A.linear:
            yield A.time(tick + 0.4)
            turn(*A.unit(tick, 1))
        if A.unit(tick, -1):
            yield A.time(tick + 0.4)
            scores(*A.unit(tick, -1))
        if A.unit(tick, A.lag - 1):
            yield A.time(tick + 0.8)
            values(*A.unit(tick, A.lag - 1))


def attention_project_act(act, g, m, A, block, t):
    s = g.s
    _name, kind, _w, bias, dst = A.tiles(block)[t]
    act.wait_ge(*g.at("proj", (A.key, block, t)))
    if block >= 1:
        act.wait_ge(*g.at("pv" if kind[0] == "V" else "scores", (A.key, block - 1, A.units - 1)))
    bank = m.bank[s][A.bank(t)]
    if kind[0] == "V":
        act.activation(A.v_part(s, kind), bank[0:A.Tk, :].rearrange("p (b h d) -> p b h d", b=NB, d=A.dh), ACT.Copy)\
           .then_inc(*g.one("proj_a", (A.key, block, t)))
    elif bias is None:
        n = NC_ if kind[0] == "C" else N
        act.activation(dst[0](s)[:, dst[1], :], bank[:, 0:n], ACT.Copy)\
           .then_inc(*g.one("proj_a", (A.key, block, t)))
    else:
        n = NC_ if kind[0] == "C" else N
        act.activation(dst[0](s)[:, dst[1], :], bank[:, 0:n], ACT.Identity, bias=bias)\
           .then_inc(*g.one("proj_a", (A.key, block, t)))


def attention_early_act(act, g, m, A):
    yield 0.0
    if A.early:
        act.wait_ge(*g.at(*g.before))
    for t in A.early:
        attention_project_act(act, g, m, A, 0, t)


def attention_act(act, g, m, A):
    s = g.s

    def project(block, t):
        _name, kind, _w, _bias, dst = A.tiles(block)[t]
        if kind == "P":
            act.wait_ge(*g.at("proj", (A.key, block, t)))
            act.activation(dst[0](s)[:, dst[1], :], m.bank[s][A.bank(t)][:, 0:N], ACT.Exp)\
               .then_inc(*g.one("proj_a", (A.key, block, t)))
        elif A.taker(t, kind) == "proj_a":
            attention_project_act(act, g, m, A, block, t)

    def exponentials(block, k):
        act.wait_ge(*g.at("shift", (A.key, block, k, "e")))
        act.activation(A.p(s, k), A.p(s, k), ACT.Exp, scale=1.0 if A.masked else A.scale)\
           .then_inc(*g.one("prob", (A.key, block, k)))

    def take_turned(block, u):
        act.wait_ge(*g.at("turn", (A.key, block, u)))
        if u >= 2:
            act.wait_ge(*g.at("pv", (A.key, block, u - 2)))
        elif block >= 1:
            act.wait_ge(*g.at("out", (A.key, block - 1)))
        act.activation(A.pT(s, u).rearrange("p a b -> p (a b)"), m.bank[s][2][0:A.Tk, 0:A.items * T], ACT.Copy)\
           .then_inc(*g.one("turned", (A.key, block, u)))

    def take_results(block):
        for pair in range(A.pairs):
            act.wait_ge(*g.at("ctx_tr", (A.key, block, pair)))
            act.activation(A.cT(s, pair), m.bank[s][2 + pair][:, :], ACT.Copy)\
               .then_inc(*g.one("ctx_a", (A.key, block, pair)))

    for t in A.main:
        yield A.time(A.first_tick(t) + 0.5)
        project(0, t)
    for tick in range(-2, A.period * A.blocks + 1):
        if A.finished(tick) is not None:
            yield A.time(tick + 0.5)
            take_results(A.finished(tick))
        block, tiles = A.next_tiles(tick)
        for t in tiles:
            yield A.time(tick + 0.5 + 0.5 * (t % 2))
            project(block, t)
        if A.unit(tick, 0) and not A.linear:
            yield A.time(tick + 0.6)
            exponentials(*A.unit(tick, 0))
        if A.unit(tick, 1) and not A.linear:
            yield A.time(tick + 0.9)
            take_turned(*A.unit(tick, 1))


def additive_mask(m, s):
    return cut(m.big[s], 2048 + 4 * NC_, NC_)


def mask_dve(dve, g, m):
    s = g.s
    dve.wait_ge(*g.mask_at())
    dve.tensor_scalar(additive_mask(m, s), m.mask8[:, s, :], -NEG, NEG, ALU.mult, ALU.add)\
       .then_inc(*g.one("mask", "made"))


def attention_dve(dve, g, m, A, base):
    s = g.s

    def project(block, t):
        name, kind, _w, bias, dst = A.tiles(block)[t]
        me = (A.key, block, t)
        bank = m.bank[s][A.bank(t)]
        if kind == "P":
            dve.wait_ge(*g.at("proj_a", me))
            o = dst[0](s)[:, dst[1], :]
            dve.tensor_scalar(o, o, 1.0, None, ALU.min).then_inc(*g.one("shift", me + ("min",)))
            dve.wait_ge(*g.at("shift", me + ("min",)))
            dve.scalar_tensor_tensor(out=o, in0=bank[:, 0:N], scalar=0.0, in1=o,
                                     op0=ALU.max, op1=ALU.add).then_inc(*g.one("proj_d", me))
            return
        dve.wait_ge(*g.at("proj", me))
        if block >= 1:
            dve.wait_ge(*g.at("pv" if kind[0] == "V" else "scores", (A.key, block - 1, A.units - 1)))
        if kind in ("R0", "R1"):
            table = m.W["L3a"][:, A.col["cos" if kind == "R0" else "sin"][0]:][:, 0:T]
            if t >= 4:
                dve.wait_ge(*g.at("proj_p", (A.key, t // 2 - 2)))
            dve.scalar_tensor_tensor(
                out=A.turn_tmp(s, t % 4), in0=bank[:, :].rearrange("p (b t) -> p b t", t=T),
                scalar=bias, in1=table[:, None, :].to_broadcast([128, NB, T]),
                op0=ALU.add, op1=ALU.mult).then_inc(*g.one("proj_d", me))
        elif kind[0] == "V":
            dve.tensor_copy(A.v_part(s, kind), bank[0:A.Tk, :].rearrange("p (b h d) -> p b h d", b=NB, d=A.dh))\
               .then_inc(*g.one("proj_d", me))
        else:
            n = NC_ if kind[0] == "C" else N
            o = dst[0](s)[:, dst[1], :]
            if bias is None:
                dve.tensor_copy(o, bank[:, 0:n]).then_inc(*g.one("proj_d", me))
            else:
                dve.tensor_scalar(o, bank[:, 0:n], bias, None, ALU.add).then_inc(*g.one("proj_d", me))

    def scores(k):
        return m.bank[s][k % 2][:, 0:A.items * A.Tk].rearrange("p (a c) -> p a c", c=A.Tk)

    def shift(block, k):
        me = (A.key, block, k)
        top = m.small[s][:, 4 * (k % 3):4 * (k % 3) + A.items]
        p, wide = A.p(s, k), [128, A.items, A.Tk]
        dve.wait_ge(*g.at("scores", me))
        if k >= 3:
            dve.wait_ge(*g.at("turn", (A.key, block, k - 3)))
        if A.masked:
            mask = additive_mask(m, s)[:, (k // 4) * C:(k // 4 + 1) * C]
            dve.scalar_tensor_tensor(out=p, in0=scores(k), scalar=A.scale, in1=mask[:, None, :].to_broadcast(wide),
                                     op0=ALU.mult, op1=ALU.add).then_inc(*g.one("shift", me + ("z",)))
            yield A.time(A.period * block + k + 0.2)
            dve.wait_ge(*g.at("shift", me + ("z",)))
        src = p if A.masked else scores(k)
        dve.tensor_reduce(top, src, AX.X, ALU.max).then_inc(*g.one("shift", me + ("m",)))
        yield A.time(A.period * block + k + 0.4)
        dve.wait_ge(*g.at("shift", me + ("m",)))
        dve.tensor_tensor(p, src, top[:, :, None].to_broadcast(wide), ALU.subtract)\
           .then_inc(*g.one("shift", me + ("e",)))

    def causal_products(block, k):
        dve.wait_ge(*g.at("scores", (A.key, block, k)))
        if k >= 2:
            dve.wait_ge(*g.at("pv", (A.key, block, k - 2)))
        dve.tensor_tensor(A.pT(s, k), m.bank[s][k % 2][:, :].rearrange("p (a c) -> p a c", c=T),
                          m.const["upper"][:, None, :].to_broadcast([128, A.items, T]), ALU.mult)\
           .then_inc(*g.one("prob_d", (A.key, block, k)))

    def norm(block, gr):
        u = gr * A.group
        me = (A.key, block, gr)
        nt = A.items if (A.wide or A.single) else H
        rec = m.small[s][:, 16 + 16 * (gr % 2):16 + 16 * (gr % 2) + nt]
        dve.wait_ge(*g.at("pv", (A.key, block, u + A.group - 1)))
        if A.linear:
            dve.tensor_scalar(rec, A.o(s, u)[:, :, A.dh], 1e-6, None, ALU.max)\
               .then_inc(*g.one("norm", me + ("c",)))
            dve.wait_ge(*g.at("norm", me + ("c",)))
            dve.reciprocal(rec, rec).then_inc(*g.one("norm", me + ("r",)))
        else:
            dve.reciprocal(rec, A.o(s, u)[:, :, A.dh]).then_inc(*g.one("norm", me + ("r",)))
        dve.wait_ge(*g.at("norm", me + ("r",)))
        if A.wide and block >= 1 and gr == 0:
            dve.wait_ge(*g.at("ctx_tr", (A.key, block - 1, A.pairs - 1)))
        dve.tensor_tensor(A.on_slice(s, u), A.o(s, u)[:, :, 0:A.dh],
                          rec[:, :, None].to_broadcast([128, nt, A.dh]), ALU.mult)\
           .then_inc(*g.one("norm", me + ("n",)))

    def add(block):
        dve.wait_ge(*g.at("out", (A.key, block)))
        src = m.x
        if block >= 1:
            dve.wait_ge(*g.at("x_upd", (A.key, block - 1)))
        elif base is m.xin:
            dve.wait_ge(*g.context_at())
            src = base
        dve.tensor_tensor(m.x[s].rearrange("p b d -> p (b d)"), m.bank[s][3][:, :],
                          src[s].rearrange("p b d -> p (b d)"), ALU.add)\
           .then_inc(*g.one("x_upd", (A.key, block)))

    for t in A.main:
        if A.taker(t, A.tiles(0)[t][1]) == "proj_d":
            yield A.time(A.first_tick(t) + (0.9 if A.linear else 0.5))
            project(0, t)
    for tick in range(-2, A.period * A.blocks + 1):
        if A.unit(tick, 0):
            yield A.time(tick)
            if A.linear:
                causal_products(*A.unit(tick, 0))
            else:
                yield from shift(*A.unit(tick, 0))
        if A.unit(tick, A.lag):
            block, u = A.unit(tick, A.lag)
            if u % A.group == A.group - 1:
                yield A.time(tick + 0.2)
                norm(block, u // A.group)
        if A.finished(tick, 1) is not None:
            yield A.time(tick + 0.5)
            add(A.finished(tick, 1))
        block, tiles = A.next_tiles(tick)
        for t in tiles:
            if A.taker(t, A.tiles(block)[t][1]) == "proj_d":
                yield A.time(tick + 0.5 + 0.5 * (t % 2))
                project(block, t)


def attention_pool(pool, g, m, A):
    s = g.s
    yield 0.04
    pool.memset(A.v(s)[:, :, :, A.dh:A.dh + 1].rearrange("p b h d -> p (b h) d"), 1.0)\
        .then_inc(*g.one("proj_p", (A.key, "ones")))
    if A.rotated:
        for n, dst in (("q", A.q), ("k", A.k)):
            for j in range(4):
                t = 2 * j + (8 if n == "k" else 0)
                yield A.time(A.first_tick(t + 1) + 0.6)
                pool.wait_ge(*g.at("proj_d", (A.key, 0, t + 1)))
                pool.tensor_tensor(dst(s)[:, j, :].rearrange("p (b t) -> p b t", t=T),
                                   A.turn_tmp(s, t % 4), A.turn_tmp(s, t % 4 + 1), ALU.add)\
                    .then_inc(*g.one("proj_p", (A.key, t // 2)))



def norm_dve(dve, g, m, key, src, dst, made=None):
    s = g.s
    yield 0.0 if made is None else 0.02
    if made is not None:
        dve.wait_ge(*g.at("ln_xn", made))
    elif g.before is None:
        dve.wait_ge(m.s_xin[s], g.loads())
    else:
        dve.wait_ge(*g.at(*g.before))
    for b in range(NB):
        last = dve.bn_stats(m.st[s][:, b, :], src[s][:, b, :])
    last.then_inc(*g.one("ln_stat", key))
    yield 0.002 if made is None else 0.022
    dve.wait_ge(*g.at("ln_stat", key))
    dve.memset(m.carrier[:, s:s + 1], 0.0)
    for b in range(NB):
        last = dve.bn_aggr(m.mv[s][:, b, :], m.st[s][:, b, :])
    last.then_inc(*g.one("ln_aggr", key))
    yield 0.004 if made is None else 0.024
    dve.wait_ge(*g.at("ln_aggr", key))
    dve.tensor_scalar(m.ve[s][:, :], m.mv[s][:, :, 1], EPS, None, ALU.add)\
       .then_inc(*g.one("ln_var", key))
    yield 0.01 if made is None else 0.03
    dve.wait_ge(*g.at("ln_rstd", key))
    for b in range(NB):
        last = dve.tensor_scalar(dst[s][:, b, :], src[s][:, b, :], m.mv[s][:, b, 0:1], m.rs[s][:, b:b + 1],
                                 ALU.subtract, ALU.mult)
    last.then_inc(*g.one("ln_xn", key))


def norm_pool(pool, g, m, key):
    s = g.s
    yield 0.03 if key in (k + "i" for k in NESTED) else 0.01
    pool.wait_ge(*g.at("ln_var", key))
    pool.tensor_tensor(m.rs[s][:, :], m.ve[s][:, :], m.const["neghalf"], ALU.pow)\
        .then_inc(*g.one("ln_rstd", key))


def turn_pe(pe, g, m, key, src, free):
    s = g.s
    yield 0.04
    if key == "L3f":
        pe.wait_ge(*g.at("qf_d", "r3"))
    else:
        pe.wait_ge(*g.at("ln_xn", (key + "i" if key in NESTED else key)))
    g.wait_free(pe, free, s, 2)
    for b in range(NB):
        last = pe.transpose(m.bank[s][2][:, b * T:(b + 1) * T], src[s][:, b, :], m.const["ident"])
    last.then_inc(*g.one("ln_tr", key))
    free[s, 2] = ("ln_xT", key)


def turn_act(act, g, m, key, gain=None, shift=None):
    s = g.s
    yield 0.042
    act.wait_ge(*g.at("ln_tr", key))
    if gain is None:
        act.activation(m.xT[s][:, :], m.bank[s][2][:, :], ACT.Copy).then_inc(*g.one("ln_xT", key))
    else:
        act.activation(m.xT[s][:, :], m.bank[s][2][:, :], ACT.Identity, bias=shift, scale=gain)\
           .then_inc(*g.one("ln_xT", key))



class Router:
    def __init__(self, m, key):
        self.m, self.key = m, key
        at = m.cols[key][1]["r"][0]
        self.w = m.W[key][:, at:at + E]

    def part(self, s, at, *shape):
        return cut(self.m.small[s], at, *shape)

    def logits(self, s):
        return self.m.bank[s][3][:, 0:NB * E].rearrange("p (b e) -> p b e", e=E)


def router_pe(pe, g, m, R, free):
    s = g.s
    yield 0.05
    pe.wait_ge(*g.at("ln_xT", R.key))
    g.wait_free(pe, free, s, 3)
    for b in range(NB):
        last = pe.matmul(m.bank[s][3][:, E * b:E * b + E], m.xT[s][:, b * T:(b + 1) * T], R.w,
                         start=True, stop=True)
    last.then_inc(*g.one("rt_pe", R.key))
    free[s, 3] = ("rt_d", (R.key, "shift"))


def router_act(act, g, m, R):
    s = g.s
    yield router_time(R.key, 1)
    act.wait_ge(*g.at("rt_d", (R.key, "shift")))
    act.activation(R.part(s, 80, NB, E), R.part(s, 80, NB, E), ACT.Exp).then_inc(*g.one("rt_a", (R.key, "e")))
    if R.key == "L0f":
        yield router_time(R.key, 8)
        act.wait_ge(*g.at("rt_d", (R.key, "gap")))
        act.activation(R.part(s, 224, NB), R.part(s, 224, NB), ACT.Exp).then_inc(*g.one("rt_a", (R.key, "x")))


def router_time(key, step):
    return 0.05 + (0.06 if key == "L2f" else 0.008) * step


def router_dve(dve, g, m, R):
    s = g.s
    def step(name, last):
        last.then_inc(*g.one("rt_d", (R.key, name)))

    def after(name):
        dve.wait_ge(*g.at("rt_d", (R.key, name)))

    wide = lambda v: v[:, :, None].to_broadcast([128, NB, E])
    p = lambda s: R.part(s, 80, NB, E)
    top = lambda s: R.part(s, 112, NB, 8)
    idx = lambda s: R.part(s, 144, NB, 2)
    w = lambda s: R.part(s, 152, NB, 2)
    cw = lambda s: R.part(s, 160, NB, E)
    tmp = lambda s: R.part(s, 192, NB, E)
    a1 = lambda s: R.part(s, 224, NB)
    a2 = lambda s: R.part(s, 228, NB)
    yield router_time(R.key, 0)
    dve.wait_ge(*g.at("rt_pe", R.key))
    step("max", dve.tensor_reduce(a1(s), R.logits(s), AX.X, ALU.max))
    yield router_time(R.key, 1)
    after("max")
    step("shift", dve.tensor_tensor(p(s), R.logits(s), wide(a1(s)), ALU.subtract))
    yield router_time(R.key, 2)
    dve.wait_ge(*g.at("rt_a", (R.key, "e")))
    step("sum", dve.tensor_reduce(a1(s), p(s), AX.X, ALU.add))
    yield router_time(R.key, 3)
    after("sum")
    step("rec", dve.reciprocal(a2(s), a1(s)))
    yield router_time(R.key, 4)
    after("rec")
    step("p", dve.tensor_tensor(p(s), p(s), wide(a2(s)), ALU.mult))
    yield router_time(R.key, 5)
    after("p")
    dve.memset(m.carrier[:, 2 + s:3 + s], 0.0)
    for b in range(NB):
        last = dve.max(top(s)[:, b, :], p(s)[:, b, :])
    step("top", last)
    yield router_time(R.key, 6)
    after("top")
    dve.memset(m.carrier[:, 4 + s:5 + s], 0.0)
    for b in range(NB):
        last = dve.max_index(m.idx[s][:, b, :], top(s)[:, b, :], p(s)[:, b, :])
    step("idx", last)
    yield router_time(R.key, 7)
    after("idx")
    step("idxf", dve.tensor_copy(idx(s), m.idx[s][:, :, 0:2]))
    if R.key == "L0f":
        yield router_time(R.key, 8)
        step("gap", dve.tensor_tensor(a1(s), top(s)[:, :, 1], top(s)[:, :, 0], ALU.subtract))
        yield router_time(R.key, 9)
        dve.wait_ge(*g.at("rt_a", (R.key, "x")))
        step("one", dve.tensor_scalar(a2(s), a1(s), 1.0, None, ALU.add))
        yield router_time(R.key, 10)
        after("one")
        step("w1", dve.reciprocal(w(s)[:, :, 0], a2(s)))
        yield router_time(R.key, 11)
        after("w1")
        step("w", dve.tensor_tensor(w(s)[:, :, 1], w(s)[:, :, 0], a1(s), ALU.mult))
    elif R.key == "L1f":
        yield router_time(R.key, 8)
        step("two", dve.tensor_tensor(a1(s), top(s)[:, :, 1], top(s)[:, :, 0], ALU.add))
        yield router_time(R.key, 9)
        after("two")
        step("one", dve.reciprocal(a2(s), a1(s)))
        yield router_time(R.key, 11)
        after("one")
        step("w", dve.tensor_tensor(w(s), top(s)[:, :, 0:2], a2(s)[:, :, None].to_broadcast([128, NB, 2]),
                                       ALU.mult))
    else:
        yield router_time(R.key, 8)
        after("idxf")
        step("m0", dve.tensor_scalar(w(s)[:, :, 0], idx(s)[:, :, 0], 0.0, None, ALU.is_equal))
        yield router_time(R.key, 8)
        step("m1", dve.tensor_scalar(w(s)[:, :, 1], idx(s)[:, :, 1], 1.0, None, ALU.is_equal))
        yield router_time(R.key, 11)
        after("m1")
        step("w", dve.tensor_tensor(w(s), w(s), top(s)[:, :, 0:2], ALU.mult))
        return
    eight = m.const["eight"][:, None, :].to_broadcast([128, NB, E])
    yield router_time(R.key, 12)
    after("w")
    step("e0", dve.tensor_tensor(cw(s), eight, wide(idx(s)[:, :, 0]), ALU.is_equal))
    yield router_time(R.key, 12)
    step("e1", dve.tensor_tensor(tmp(s), eight, wide(idx(s)[:, :, 1]), ALU.is_equal))
    yield router_time(R.key, 13)
    after("e1")
    step("f0", dve.tensor_tensor(cw(s), cw(s), wide(w(s)[:, :, 0]), ALU.mult))
    yield router_time(R.key, 13)
    step("f1", dve.tensor_tensor(tmp(s), tmp(s), wide(w(s)[:, :, 1]), ALU.mult))
    yield router_time(R.key, 14)
    after("f1")
    step("cw", dve.tensor_tensor(cw(s), cw(s), tmp(s), ALU.add))


class Experts:

    def __init__(self, m, key):
        self.m, self.key = m, key
        self.gated = key == "L0f"
        self.F = F0 if self.gated else F1
        self.ft = self.F // 128
        self.col = m.cols[key][1]

    def w(self, name, lo, hi):
        at = self.col[name][0]
        return self.m.W[self.key][:, at + lo:at + hi]

    def h(self, s, e, f):
        return cut(self.m.big[s], 2048 * (e % 2) + 512 * f, N)

    def gate(self, s, t):
        return cut(self.m.big[s], 4096 + 512 * (t % 2), N)

    def cwT(self, s):
        return cut(self.m.big[s], 5120, N)[0:E]

    def time(self, e, f):
        return 0.2 + 0.8 * (e * self.ft + f) / ((E + 1) * self.ft)

    def cw(self, s, b, e):
        return self.m.small[s][:, 160 + E * b + e:161 + E * b + e]


def experts_pe(pe, g, m, X, free):
    s = g.s
    if not X.gated:
        yield 0.18
        pe.wait_ge(*g.at("rt_d", (X.key, "cw")))
        g.wait_free(pe, free, s, 0)
        for b in range(NB):
            last = pe.transpose(m.bank[s][0][0:E, b * T:(b + 1) * T], cut(m.small[s], 160, NB, E)[:, b, :],
                                m.const["ident"])
        last.then_inc(*g.one("ff_pe", (X.key, "cwT")))
        free[s, 0] = ("ff_a", (X.key, "cwT"))
        yield 0.19
        pe.wait_ge(*g.at("ff_a", (X.key, "cwT")))
        g.wait_free(pe, free, s, 3)
        for b in range(NB):
            last = pe.matmul(m.bank[s][3][:, b * D:(b + 1) * D], X.cwT(s)[:, b * T:(b + 1) * T],
                             X.w("b2", 0, 128)[0:E], start=True, stop=True)
        last.then_inc(*g.one("dn_pe", (X.key, "b2")))
        free[s, 3] = ("dn_d", (X.key, "b2"))
    turn = 0
    for e in range(E + 1):
        for b in range(NB):
            f, rest = divmod(b * X.ft, NB)
            if e < E and rest == 0:
                yield X.time(e, f)
                lo = e * X.F + 128 * f
                for name in (("gate", "up") if X.gated else ("w1",)):
                    k = turn % 3
                    g.wait_free(pe, free, s, k)
                    pe.matmul(m.bank[s][k][:, :], X.w(name, lo, lo + 128), m.xT[s][:, :], start=True, stop=True)\
                      .then_inc(*g.one("ff_pe", (X.key, name, e, f)))
                    free[s, k] = ("ff_d" if name == "up" else "ff_a", (X.key, e, f))
                    turn += 1
            if e >= 1:
                yield X.time(e, X.ft * (b + 0.5) / NB)
                if b == 0:
                    pe.wait_ge(*g.at("ff_d" if X.gated else "ff_a", (X.key, e - 1, X.ft - 1)))
                    g.wait_free(pe, free, s, 3)
                for f in range(X.ft):
                    k = (e - 1) * X.ft + f
                    last = pe.matmul(m.bank[s][3][:, b * D:(b + 1) * D], X.h(s, e - 1, f)[:, b * T:(b + 1) * T],
                                     X.w("down" if X.gated else "w2", 128 * k, 128 * k + 128),
                                     start=(f == 0), stop=(f == X.ft - 1))
        if e >= 1:
            last.then_inc(*g.one("dn_pe", (X.key, e - 1)))
            free[s, 3] = ("dn_d", (X.key, e - 1))


def experts_act(act, g, m, X):
    s = g.s
    if not X.gated:
        yield 0.18
        act.wait_ge(*g.at("ff_pe", (X.key, "cwT")))
        act.activation(X.cwT(s), m.bank[s][0][0:E, :], ACT.Copy).then_inc(*g.one("ff_a", (X.key, "cwT")))
    turn = 0
    for e in range(E):
        for f in range(X.ft):
            t = e * X.ft + f
            yield X.time(e, f if X.gated else f | 1)
            if X.gated:
                act.wait_ge(*g.at("ff_pe", (X.key, "gate", e, f)))
                if t >= 2:
                    act.wait_ge(*g.at("ff_d", (X.key, (t - 2) // X.ft, (t - 2) % X.ft)))
                act.activation(X.gate(s, t), m.bank[s][turn % 3][:, :], ACT.Silu)\
                   .then_inc(*g.one("ff_a", (X.key, e, f)))
            else:
                act.wait_ge(*g.at("ff_pe", (X.key, "w1", e, f)))
                if e >= 2:
                    act.wait_ge(*g.at("dn_pe", (X.key, e - 2)))
                act.activation(X.h(s, e, f), m.bank[s][turn % 3][:, :], ACT.Gelu, bias=X.w("b1", t, t + 1))\
                   .then_inc(*g.one("ff_a", (X.key, e, f)))
            turn += 2 if X.gated else 1


def experts_dve(dve, g, m, X):
    s = g.s
    yield 0.19
    dve.wait_ge(*g.at("rt_d", (X.key, "cw")))
    if not X.gated:
        dve.tensor_tensor(m.x[s][:, :, :], m.x[s][:, :, :], m.xn[s][:, :, :], ALU.add)\
           .then_inc(*g.one("x_upd", (X.key, "res")))
        dve.wait_ge(*g.at("dn_pe", (X.key, "b2")))
        dve.wait_ge(*g.at("x_upd", (X.key, "res")))
        dve.tensor_tensor(m.x[s].rearrange("p b d -> p (b d)"), m.bank[s][3][:, :],
                          m.x[s].rearrange("p b d -> p (b d)"), ALU.add)\
           .then_inc(*g.one("dn_d", (X.key, "b2")))
    turn = 1
    for e in range(E + 1):
        for f in range(X.ft):
            if e == E or not X.gated:
                break
            t = e * X.ft + f
            yield X.time(e, f)
            dve.wait_ge(*g.at("ff_a", (X.key, e, f)))
            dve.wait_ge(*g.at("ff_pe", (X.key, "up", e, f)))
            if e >= 2:
                dve.wait_ge(*g.at("dn_pe", (X.key, e - 2)))
            dve.tensor_tensor(X.h(s, e, f), m.bank[s][turn % 3][:, :], X.gate(s, t), ALU.mult)\
               .then_inc(*g.one("ff_d", (X.key, e, f)))
            turn += 2
        if e >= 1:
            yield X.time(e, X.ft - 0.1)
            dve.wait_ge(*g.at("dn_pe", (X.key, e - 1)))
            if e >= 2:
                dve.wait_ge(*g.at("dn_d", (X.key, e - 2)))
            elif not X.gated:
                dve.wait_ge(*g.at("dn_d", (X.key, "b2")))
            for b in range(NB):
                last = dve.scalar_tensor_tensor(out=m.x[s][:, b, :], in0=m.bank[s][3][:, b * D:(b + 1) * D],
                                                scalar=X.cw(s, b, e - 1), in1=m.x[s][:, b, :],
                                                op0=ALU.mult, op1=ALU.add)
            last.then_inc(*g.one("dn_d", (X.key, e - 1)))



class Mamba:

    def __init__(self, m):
        self.m, self.key = m, "L2a"
        self.col = m.cols["L2a"][1]

    def w(self, name, lo=0, hi=None):
        at, width = self.col[name]
        return self.m.W["L2a"][:, at + lo:at + (width if hi is None else hi)]

    def xi(self, s, half):
        return cut(self.m.big[s], 536 * half, NB, T + 6)

    def sz(self, s, half):
        return cut(self.m.big[s], 1072 + 512 * half, N)

    def u(self, s, half):
        return cut(self.m.big[s], 2096 + 512 * half, N)

    def dl(self, s, half):
        return cut(self.m.big[s], 3120 + 512 * half, N)

    def du(self, s, half):
        return cut(self.m.big[s], 4144 + 512 * half, N)

    def parts(self, s):
        return cut(self.m.big[s], 5168, 256).bitcast(BF16)[0:96]

    def dA(self, s, half):
        return cut(self.m.big[s], 5424 + 512 * half, N)

    def h(self, s, k):
        return self.m.xn[s].rearrange("p b d -> p (b d)") if k == 3 else cut(self.m.big[s], 6448 + 512 * k, N)

    def rest(self, s):
        return self.dA(s, 0)[0:96]

    def mid(self, s):
        return cut(self.m.big[s], 5936, 256).bitcast(BF16)[0:96]

    def dtT(self, s):
        return self.h(s, 1)[0:DTR]

    def mo(self, s, way):
        return self.m.xT[s][:, :] if way == 0 else self.dl(s, 0)

    def at(self, way, part):
        return 0.06 + 0.45 * (way + part)

    def scan_at(self, way, n, part=0.0):
        return self.at(way, 0.15 + 0.8 * (n + part) / NS)

    def timed(self, v, way):
        v = v.rearrange("p (b t) -> p b t", t=T)
        return v if way == 0 else v[:, :, ::-1]


def mamba_pe(pe, g, m, M, free):
    s = g.s
    for k in range(4):
        yield 0.05 + 0.001 * k
        pe.wait_ge(*g.at("ln_xT", "L2a"))
        g.wait_free(pe, free, s, k)
        pe.matmul(m.bank[s][k][:, :], M.w("in", 128 * k, 128 * k + 128), m.xT[s][:, :], start=True, stop=True)\
          .then_inc(*g.one("mb_pe", ("in", k)))
        free[s, k] = ("mb_d", ("xi", k)) if k < 2 else ("mb_a", ("sz", k - 2))
    for way in range(2):
        yield M.at(way, 0.04)
        pe.wait_ge(*g.at("mb_a", ("u", way, 1)))
        if way == 0:
            g.wait_free(pe, free, s, 0)
        for half in range(2):
            last = pe.matmul(m.bank[s][0][0:96, :], M.w("bc3", 96 * half, 96 * half + 96), M.u(s, half),
                             start=half == 0, stop=half == 1)
        last.then_inc(*g.one("mb_pe", ("bc", way)))
        free[s, 0] = ("mb_d", ("rest", way))
        g.wait_free(pe, free, s, 1)
        for half in range(2):
            last = pe.matmul(m.bank[s][1][0:DTR, :], M.w("xdt", DTR * half, DTR * half + DTR), M.u(s, half),
                             start=half == 0, stop=half == 1)
        last.then_inc(*g.one("mb_pe", ("xdt", way)))
        free[s, 1] = ("mb_a", ("dtT", way))
        yield M.at(way, 0.05)
        pe.wait_ge(*g.at("mb_a", ("dtT", way)))
        for half in range(2):
            if way == 1:
                g.wait_free(pe, free, s, 2 + half)
            pe.matmul(m.bank[s][2 + half][:, :], M.w("dt", 128 * half, 128 * half + 128)[0:DTR], M.dtT(s),
                      start=True, stop=True).then_inc(*g.one("mb_pe", ("dt", way, half)))
            free[s, 2 + half] = ("mb_d", ("abs", way, half))

        def spread(n, k):
            row = n + NS * k
            if n == 0:
                pe.wait_ge(*g.at("mb_d", ("parts", way)))
            g.wait_free(pe, free, s, k)
            pe.matmul(m.bank[s][k][:, :], m.sel3[0:96, row:row + 1].to_broadcast([96, 128]), M.parts(s),
                      start=True, stop=True).then_inc(*g.one("sc_bc", (way, n, k)))
            free[s, k] = ("sc_d", (way, n, ("in", "out")[k], 1))

        yield M.at(way, 0.13)
        spread(0, 0)
        spread(0, 1)
        for n in range(NS):
            if n + 1 < NS:
                yield M.scan_at(way, n, 0.5)
                spread(n + 1, 0)
                yield M.scan_at(way, n, 1.1)
                spread(n + 1, 1)
            for half in range(2):
                yield M.scan_at(way, n, 1.1 + 0.2 * half)
                pe.wait_ge(*g.at("sc_d", (way, n, "out", half)))
                if n == 0:
                    g.wait_free(pe, free, s, 2 + half)
                last = pe.matmul(m.bank[s][2 + half][:, :], m.const["ident"], M.h(s, 2 * (n % 2) + half),
                                 start=n == 0, stop=n == NS - 1)
                last.then_inc(*g.one("sc_y", (way, n, half)))
                free[s, 2 + half] = ("mb_d", ("yd", way, half))
        yield M.at(way, 0.98)
        g.wait_free(pe, free, s, 0)
        for half in range(2):
            pe.wait_ge(*g.at("mb_d", ("gated", way, half)))
            last = pe.matmul(m.bank[s][0][:, :], M.w("out", 128 * half, 128 * half + 128), M.du(s, half),
                             start=half == 0, stop=half == 1)
        last.then_inc(*g.one("mb_pe", ("out", way)))
        free[s, 0] = ("mb_a", ("mo", way))
    yield 0.965
    pe.wait_ge(*g.at("mb_a", ("mo", 1)))
    g.wait_free(pe, free, s, 1)
    for way in range(2):
        last = pe.matmul(m.bank[s][1][:, :], M.w("dim", 128 * way, 128 * way + 128), M.mo(s, way),
                         start=way == 0, stop=way == 1)
    last.then_inc(*g.one("mb_pe", "dim"))
    free[s, 1] = ("mb_a", "gelu")
    yield 0.975
    pe.wait_ge(*g.at("mb_a", "gelu"))
    row = m.rows["glu"]
    for pair in range(2):
        bank = m.bank[s][2 + pair]
        g.wait_free(pe, free, s, 2 + pair)
        for b in range(2):
            for part in range(2):
                dst = bank[:, 256 * b + 128 * part:256 * b + 128 * part + 128]
                pe.matmul(dst, bias_picker(m, row + part, T), m.brow3[0:96, :], start=True, stop=False)
                at = (2 * pair + b) * T
                last = pe.matmul(dst, M.u(s, 0)[:, at:at + T], M.w("glu", 128 * part, 128 * part + 128),
                                 start=False, stop=True)
        last.then_inc(*g.one("mb_pe", ("glu", pair)))
        free[s, 2 + pair] = ("mb_d", ("prod", pair))


def mamba_act(act, g, m, M):
    s = g.s
    for half in range(2):
        yield 0.052 + 0.001 * half
        act.wait_ge(*g.at("mb_pe", ("in", 2 + half)))
        act.activation(M.sz(s, half), m.bank[s][2 + half][:, :], ACT.Silu)\
           .then_inc(*g.one("mb_a", ("sz", half)))
    for way in range(2):
        for half in range(2):
            yield M.at(way, 0.04)
            act.wait_ge(*g.at("mb_d", ("conv", way, half, DC - 1)))
            act.activation(M.u(s, half), M.u(s, half), ACT.Silu, bias=M.w("convb", half, half + 1))\
               .then_inc(*g.one("mb_a", ("u", way, half)))
        act.wait_ge(*g.at("mb_pe", ("xdt", way)))
        act.activation(M.dtT(s), m.bank[s][1][0:DTR, :], ACT.Copy).then_inc(*g.one("mb_a", ("dtT", way)))
        for half in range(2):
            yield M.at(way, 0.065 + 0.005 * half)
            act.wait_ge(*g.at("mb_d", ("abs", way, half)))
            act.activation(M.dl(s, half), M.dl(s, half), ACT.Exp, bias=M.w("dtb", half, half + 1))\
               .then_inc(*g.one("mb_a", ("exp", way, half)))
        for half in range(2):
            yield M.at(way, 0.08)
            act.wait_ge(*g.at("mb_a", ("exp", way, half)))
            act.activation(M.dl(s, half), M.dl(s, half), ACT.Ln, bias=1.0)\
               .then_inc(*g.one("mb_a", ("ln", way, half)))
        for n in range(NS):
            for half in range(2):
                yield M.at(way, 0.13) if n == 0 else M.scan_at(way, n - 1, 0.7 + 0.2 * half)
                if n == 0:
                    act.wait_ge(*g.at("mb_d", ("far", way, half)))
                    act.wait_ge(*g.at("mb_d", ("parts", way)))
                else:
                    act.wait_ge(*g.at("sc_d", (way, n - 1, "scan", half)))
                act.activation(M.dA(s, half), M.dl(s, half), ACT.Exp,
                               scale=m.Aneg[:, NS * half + n:NS * half + n + 1])\
                   .then_inc(*g.one("sc_da", (way, n, half)))
        yield M.at(way, 0.99)
        act.wait_ge(*g.at("mb_pe", ("out", way)))
        act.activation(M.mo(s, way), m.bank[s][0][:, :], ACT.Copy).then_inc(*g.one("mb_a", ("mo", way)))
    yield 0.967
    act.wait_ge(*g.at("mb_pe", "dim"))
    act.activation(M.u(s, 0), m.bank[s][1][:, :], ACT.Gelu, bias=M.w("dimb"))\
       .then_inc(*g.one("mb_a", "gelu"))
    for pair in range(2):
        yield 0.98
        act.wait_ge(*g.at("mb_pe", ("glu", pair)))
        act.activation(cut(m.big[s], 2608 + 256 * pair, 2, T),
                       m.bank[s][2 + pair][:, :].rearrange("p (b c t) -> p b c t", b=2, c=2)[:, :, 1, :],
                       ACT.Sigmoid).then_inc(*g.one("mb_a", ("sig", pair)))


def mamba_pool(pool, g, m, M):
    s = g.s
    yield 0.04
    for half in range(2):
        for at in (0, T + 3):
            last = pool.memset(M.xi(s, half)[:, :, at:at + 3], 0.0)
    last.then_inc(*g.one("mb_p", "pad"))


def mamba_dve(dve, g, m, M):
    s = g.s
    for half in range(2):
        yield 0.05 + 0.001 * half
        dve.wait_ge(*g.at("mb_pe", ("in", half)))
        dve.tensor_copy(M.xi(s, half)[:, :, 3:3 + T],
                        m.bank[s][half][:, :].rearrange("p (b t) -> p b t", t=T))\
           .then_inc(*g.one("mb_d", ("xi", half)))
    dve.wait_ge(*g.at("mb_p", "pad"))
    dve.tensor_tensor(m.x[s][:, :, :], m.x[s][:, :, :], m.xn[s][:, :, :], ALU.add)\
       .then_inc(*g.one("x_upd", ("L2a", "res")))
    for way in range(2):
        for j in range(DC):
            for half in range(2):
                yield M.at(way, 0.005 * j)
                at = j if way == 0 else 6 - j
                src = M.xi(s, half)[:, :, at:at + T]
                dst = M.timed(M.u(s, half), way)
                tap = M.w("conv", DC * half + j, DC * half + j + 1)
                if j == 0:
                    dve.wait_ge(*g.at("mb_d", ("xi", half)))
                    ins = dve.tensor_scalar(dst, src, tap, None, ALU.mult)
                else:
                    dve.wait_ge(*g.at("mb_d", ("conv", way, half, j - 1)))
                    ins = dve.scalar_tensor_tensor(out=dst, in0=src, scalar=tap, in1=dst,
                                                   op0=ALU.mult, op1=ALU.add)
                ins.then_inc(*g.one("mb_d", ("conv", way, half, j)))
        yield M.at(way, 0.04)
        dve.wait_ge(*g.at("mb_pe", ("bc", way)))
        dve.tensor_copy(M.parts(s), m.bank[s][0][0:96, :]).then_inc(*g.one("mb_d", ("hi", way)))
        yield M.at(way, 0.043)
        dve.wait_ge(*g.at("mb_d", ("hi", way)))
        dve.tensor_tensor(M.rest(s), m.bank[s][0][0:96, :], M.parts(s), ALU.subtract)\
           .then_inc(*g.one("mb_d", ("rest", way)))
        yield M.at(way, 0.046)
        dve.wait_ge(*g.at("mb_d", ("rest", way)))
        dve.tensor_copy(M.mid(s), M.rest(s)).then_inc(*g.one("mb_d", ("mid", way)))
        yield M.at(way, 0.049)
        dve.wait_ge(*g.at("mb_d", ("mid", way)))
        dve.tensor_copy(M.parts(s)[32:64], M.mid(s)[32:64])
        dve.tensor_tensor(M.parts(s)[64:96], M.rest(s)[64:96], M.mid(s)[64:96], ALU.subtract)\
           .then_inc(*g.one("mb_d", ("parts", way)))
        for half in range(2):
            b = M.w("dtb", half, half + 1)
            yield M.at(way, 0.055)
            dve.wait_ge(*g.at("mb_pe", ("dt", way, half)))
            dve.tensor_scalar(M.h(s, half), m.bank[s][2 + half][:, :], b, 0.0, ALU.add, ALU.max)\
               .then_inc(*g.one("mb_d", ("pos", way, half)))
        for half in range(2):
            yield M.at(way, 0.06 + 0.005 * half)
            dve.wait_ge(*g.at("mb_d", ("pos", way, half)))
            dve.scalar_tensor_tensor(out=M.dl(s, half), in0=M.h(s, half), scalar=-2.0,
                                     in1=m.bank[s][2 + half][:, :], op0=ALU.mult, op1=ALU.add)\
               .then_inc(*g.one("mb_d", ("abs", way, half)))
        for half in range(2):
            yield M.at(way, 0.1)
            dve.wait_ge(*g.at("mb_a", ("ln", way, half)))
            dve.wait_ge(*g.at("mb_d", ("pos", way, half)))
            dve.tensor_tensor(M.dl(s, half), M.dl(s, half), M.h(s, half), ALU.add)\
               .then_inc(*g.one("mb_d", ("delta", way, half)))
        for half in range(2):
            yield M.at(way, 0.105)
            dve.wait_ge(*g.at("mb_d", ("delta", way, half)))
            dve.tensor_tensor(M.du(s, half), M.dl(s, half), M.u(s, half), ALU.mult)\
               .then_inc(*g.one("mb_d", ("du", way, half)))
        for half in range(2):
            yield M.at(way, 0.11)
            dve.wait_ge(*g.at("mb_d", ("du", way, half)))
            dve.memset(M.dl(s, half).rearrange("p (b t) -> p b t", t=T)[:, :, 0:1], FAR)\
               .then_inc(*g.one("mb_d", ("far", way, half)))
        for n in range(NS):
            for half in range(2):
                yield M.scan_at(way, n, 0.15 * half)
                dve.wait_ge(*g.at("sc_bc", (way, n, 0)))
                if n >= 2:
                    dve.wait_ge(*g.at("sc_y", (way, n - 2, half)))
                h = M.h(s, 2 * (n % 2) + half)
                dve.tensor_tensor(h, m.bank[s][0][:, :], M.du(s, half), ALU.mult)\
                   .then_inc(*g.one("sc_d", (way, n, "in", half)))
            for half in range(2):
                yield M.scan_at(way, n, 0.33 + 0.17 * half)
                dve.wait_ge(*g.at("sc_da", (way, n, half)))
                dve.wait_ge(*g.at("sc_d", (way, n, "in", half)))
                h = M.h(s, 2 * (n % 2) + half)
                dve.tensor_tensor_scan(h, M.dA(s, half), h, 0.0, ALU.mult, ALU.add)\
                   .then_inc(*g.one("sc_d", (way, n, "scan", half)))
            for half in range(2):
                yield M.scan_at(way, n, 0.67 + 0.16 * half)
                dve.wait_ge(*g.at("sc_bc", (way, n, 1)))
                dve.wait_ge(*g.at("sc_d", (way, n, "scan", half)))
                h = M.h(s, 2 * (n % 2) + half)
                dve.tensor_tensor(h, m.bank[s][1][:, :], h, ALU.mult)\
                   .then_inc(*g.one("sc_d", (way, n, "out", half)))
        for half in range(2):
            yield M.at(way, 0.96)
            dve.wait_ge(*g.at("sc_y", (way, NS - 1, half)))
            dve.wait_ge(*g.at("sc_d", (way, NS - 1, "in", half)))
            dve.scalar_tensor_tensor(out=M.timed(M.du(s, half), way),
                                     in0=M.u(s, half).rearrange("p (b t) -> p b t", t=T),
                                     scalar=M.w("dskip", half, half + 1),
                                     in1=m.bank[s][2 + half][:, :].rearrange("p (b t) -> p b t", t=T),
                                     op0=ALU.mult, op1=ALU.add).then_inc(*g.one("mb_d", ("yd", way, half)))
        for half in range(2):
            yield M.at(way, 0.97)
            dve.wait_ge(*g.at("mb_d", ("yd", way, half)))
            dve.tensor_tensor(M.du(s, half), M.du(s, half), M.sz(s, half), ALU.mult)\
               .then_inc(*g.one("mb_d", ("gated", way, half)))
    for pair in range(2):
        yield 0.99
        dve.wait_ge(*g.at("mb_a", ("sig", pair)))
        dve.tensor_tensor(cut(m.big[s], 4144 + 256 * pair, 2, T),
                          m.bank[s][2 + pair][:, :].rearrange("p (b c t) -> p b c t", b=2, c=2)[:, :, 0, :],
                          cut(m.big[s], 2608 + 256 * pair, 2, T), ALU.mult)\
           .then_inc(*g.one("mb_d", ("prod", pair)))
    dve.wait_ge(*g.at("mb_d", ("prod", 1)))
    dve.tensor_tensor(m.x[s][:, :, :], m.x[s][:, :, :], cut(m.big[s], 4144, NB, T), ALU.add)\
       .then_inc(*g.one("x_upd", "L2a"))



def maps_pe(pe, g, m, free):
    s = g.s
    col = m.cols["L2f"][1]
    for k in range(2):
        yield 0.06
        pe.wait_ge(*g.at("ln_xT", "L2f"))
        g.wait_free(pe, free, s, k)
        for b in range(NB):
            dst = m.bank[s][k][:, b * D:(b + 1) * D]
            pe.matmul(dst, bias_picker(m, m.rows[f"L2f{k}"], T), m.brow3[0:96, :], start=True, stop=False)
            last = pe.matmul(dst, m.xT[s][:, b * T:(b + 1) * T],
                             m.W["L2f"][:, col[f"w{k}"][0]:][:, 0:D], start=False, stop=True)
        last.then_inc(*g.one("ff_pe", ("L2f", k)))
        free[s, k] = ("ff_a", ("L2f", k))


def maps_act(act, g, m):
    s = g.s
    for k in range(2):
        yield router_time("L2f", 3)
        act.wait_ge(*g.at("ff_pe", ("L2f", k)))
        act.activation(cut(m.big[s], 512 * k, N), m.bank[s][k][:, :], ACT.Silu)\
           .then_inc(*g.one("ff_a", ("L2f", k)))


def maps_dve(dve, g, m):
    s = g.s
    for k in range(2):
        yield 0.9 + 0.05 * k
        dve.wait_ge(*g.at("rt_d", ("L2f", "w")))
        dve.wait_ge(*g.at("ff_a", ("L2f", k)))
        if k == 1:
            dve.wait_ge(*g.at("dn_d", ("L2f", 0)))
        for b in range(NB):
            at = 152 + 2 * b + k
            last = dve.scalar_tensor_tensor(out=m.x[s][:, b, :], in0=cut(m.big[s], 512 * k, NB, D)[:, b, :],
                                            scalar=m.small[s][:, at:at + 1], in1=m.x[s][:, b, :],
                                            op0=ALU.mult, op1=ALU.add)
        last.then_inc(*g.one("dn_d", ("L2f", k)))



class Quantised:

    def __init__(self, m):
        self.m = m
        self.col = m.cols["L3f"][1]

    def w(self, name, lo=0, hi=None):
        at, width = self.col[name]
        return self.m.W["L3f"][:, at + lo:at + (width if hi is None else hi)]

    def xq(self, s):
        return cut(self.m.big[s], 0, NB, D)

    def hp(self, s, j):
        return cut(self.m.big[s], 512 + 520 * j, NB, T + 2)

    def hs(self, s, j):
        return cut(self.m.big[s], 2592 + 512 * j, NB, T)

    def qT(self, s):
        return cut(self.m.big[s], 4640, 1024).bitcast(BF16).rearrange("p (j n) -> p j n", n=N)

    def qa(self, s, b):
        return cut(self.m.big[s], 5664 + 512 * (b % 2), HID)

    def qb(self, s, b):
        return cut(self.m.big[s], 6688 + 256 * (b % 2), 256).bitcast(BF16)

    def time(self, b, part):
        return 0.48 + 0.12 * (b + part)

    def sm(self, s, k, b=None):
        v = self.m.small[s]
        return v[:, 4 * k:4 * k + 4] if b is None else v[:, 4 * k + b:4 * k + b + 1]


def quantised_pe(pe, g, m, Q, free):
    s = g.s
    for j in range(4):
        k = j % 2
        yield 0.06 + 0.01 * j
        pe.wait_ge(*g.at("ln_xT", "L3f"))
        g.wait_free(pe, free, s, k)
        pe.matmul(m.bank[s][k][:, :], Q.w("w1", 128 * j, 128 * j + 128), m.xT[s][:, :], start=True, stop=True)\
          .then_inc(*g.one("qf_pe", ("h", j)))
        free[s, k] = ("qf_a", ("h", j))
    for b in range(NB + 1):
        if b < NB:
            yield Q.time(b, -0.8)
            if b == 0:
                pe.wait_ge(*g.at("qf_a", ("hs", 3)))
            if b >= 2:
                g.wait_free(pe, free, s, b % 2)
            for j in range(4):
                last = pe.transpose(m.bank[s][b % 2][:, 128 * j:128 * j + 128], Q.hs(s, j)[:, b, :],
                                    m.const["ident"])
            last.then_inc(*g.one("qf_pe", ("tok", b)))
            free[s, b % 2] = ("qf_d", ("q1", b))
        if b >= 1:
            yield Q.time(b - 1, 0.8)
            pe.wait_ge(*g.at("qf_d", ("q3", b - 1)))
            g.wait_free(pe, free, s, 2)
            for j in range(4):
                last = pe.transpose(m.bank[s][2][:, :].bitcast(BF16)[:, 128 * j:128 * j + 128],
                                    Q.qb(s, b - 1)[:, 128 * j:128 * j + 128], m.identb[:, :])
            last.then_inc(*g.one("qf_pe", ("back", b - 1)))
            free[s, 2] = ("qf_a", ("qT", b - 1))
    yield 0.98
    g.wait_free(pe, free, s, 3)
    pe.wait_ge(*g.at("qf_a", ("qT", NB - 1)))
    for b in range(NB):
        for j in range(4):
            last = pe.matmul(m.bank[s][3][:, b * D:(b + 1) * D], Q.qT(s)[:, j, b * T:(b + 1) * T],
                             m.w2t[:, 128 * j:128 * j + 128], start=j == 0, stop=j == 3)
    last.then_inc(*g.one("qf_pe", "out"))
    free[s, 3] = ("x_upd", "L3f")


def quantised_act(act, g, m, Q):
    s = g.s
    for j in range(4):
        yield 0.06 + 0.01 * j
        act.wait_ge(*g.at("qf_pe", ("h", j)))
        act.activation(Q.hp(s, j)[:, :, 1:T + 1], m.bank[s][j % 2][:, :].rearrange("p (b t) -> p b t", t=T),
                       ACT.Copy).then_inc(*g.one("qf_a", ("h", j)))
    for j in range(4):
        yield 0.16 + 0.06 * j
        act.wait_ge(*g.at("qf_d", ("conv", j, 2)))
        act.activation(Q.hs(s, j), Q.hs(s, j), ACT.Silu, bias=Q.w("convb", j, j + 1))\
           .then_inc(*g.one("qf_a", ("hs", j)))
    for b in range(NB):
        yield Q.time(b, 0.85)
        act.wait_ge(*g.at("qf_pe", ("back", b)))
        act.activation(Q.qT(s)[:, :, b * T:(b + 1) * T],
                       m.bank[s][2][:, :].bitcast(BF16)[:, 0:512].rearrange("p (j t) -> p j t", t=T),
                       ACT.Copy).then_inc(*g.one("qf_a", ("qT", b)))


def quantised_pool(pool, g, m, Q):
    s = g.s
    yield 0.04
    for j in range(4):
        for at in (0, T + 1):
            last = pool.memset(Q.hp(s, j)[:, :, at:at + 1], 0.0)
    last.then_inc(*g.one("qf_p", "pad"))


def quantise_tokens_dve(dve, g, m, Q):
    s = g.s

    def step(name, last):
        last.then_inc(*g.one("qf_d", name))

    def after(name):
        dve.wait_ge(*g.at("qf_d", name))

    yield 0.02
    dve.wait_ge(*g.at("ln_xn", "L3f"))
    step("abs", dve.scalar_tensor_tensor(out=Q.xq(s), in0=m.xn[s][:, :, :], scalar=-1.0, in1=m.xn[s][:, :, :],
                                            op0=ALU.mult, op1=ALU.max))
    yield 0.022
    after("abs")
    step("am", dve.tensor_reduce(Q.sm(s, 0), Q.xq(s), AX.X, ALU.max))
    yield 0.024
    after("am")
    step("clip", dve.tensor_scalar(Q.sm(s, 0), Q.sm(s, 0), 1e-5, None, ALU.max))
    yield 0.026
    after("clip")
    step("rec", dve.reciprocal(Q.sm(s, 1), Q.sm(s, 0)))
    yield 0.028
    after("rec")
    step("sc", dve.tensor_scalar(Q.sm(s, 1), Q.sm(s, 1), 127.0, None, ALU.mult))
    yield 0.030
    after("sc")
    step("inv", dve.reciprocal(Q.sm(s, 2), Q.sm(s, 1)))
    for b in range(NB):
        last = dve.tensor_scalar(Q.xq(s)[:, b, :], m.xn[s][:, b, :], Q.sm(s, 1, b), 127.0, ALU.mult, ALU.min)
    step("r1", last)
    yield 0.032
    after("r1")
    step("r2", dve.tensor_scalar(Q.xq(s), Q.xq(s), -128.0, ROUND, ALU.max, ALU.add))
    yield 0.034
    after("r2")
    after("inv")
    for b in range(NB):
        last = dve.tensor_scalar(Q.xq(s)[:, b, :], Q.xq(s)[:, b, :], ROUND, Q.sm(s, 2, b),
                                 ALU.subtract, ALU.mult)
    step("r3", last)


def quantised_dve(dve, g, m, Q):
    s = g.s
    for j in range(4):
        for tap in range(3):
            yield 0.12 + 0.06 * j + 0.01 * tap
            src, w = Q.hp(s, j)[:, :, tap:tap + T], Q.w("conv", 3 * j + tap, 3 * j + tap + 1)
            if tap == 0:
                dve.wait_ge(*g.at("qf_a", ("h", j)))
                dve.wait_ge(*g.at("qf_p", "pad"))
                ins = dve.tensor_scalar(Q.hs(s, j), src, w, None, ALU.mult)
            else:
                dve.wait_ge(*g.at("qf_d", ("conv", j, tap - 1)))
                ins = dve.scalar_tensor_tensor(out=Q.hs(s, j), in0=src, scalar=w, in1=Q.hs(s, j),
                                               op0=ALU.mult, op1=ALU.add)
            ins.then_inc(*g.one("qf_d", ("conv", j, tap)))
    for b in range(NB):
        def step(name, last):
            last.then_inc(*g.one("qf_d", (name, b)))

        def after(name):
            dve.wait_ge(*g.at("qf_d", (name, b)))

        yield Q.time(b, 0.0)
        dve.wait_ge(*g.at("qf_pe", ("tok", b)))
        step("mx", dve.tensor_reduce(Q.sm(s, 4, b), m.bank[s][b % 2][:, :], AX.X, ALU.max))
        step("mn", dve.tensor_reduce(Q.sm(s, 5, b), m.bank[s][b % 2][:, :], AX.X, ALU.min))
        yield Q.time(b, 0.1)
        after("mn")
        step("m", dve.scalar_tensor_tensor(out=Q.sm(s, 6, b), in0=Q.sm(s, 5, b), scalar=-1.0,
                                              in1=Q.sm(s, 4, b), op0=ALU.mult, op1=ALU.max))
        yield Q.time(b, 0.2)
        after("m")
        step("mc", dve.tensor_scalar(Q.sm(s, 6, b), Q.sm(s, 6, b), 1e-5, None, ALU.max))
        yield Q.time(b, 0.3)
        after("mc")
        step("mr", dve.reciprocal(Q.sm(s, 7, b), Q.sm(s, 6, b)))
        yield Q.time(b, 0.4)
        after("mr")
        step("ms", dve.tensor_scalar(Q.sm(s, 7, b), Q.sm(s, 7, b), 127.0, None, ALU.mult))
        yield Q.time(b, 0.5)
        after("ms")
        step("q1", dve.tensor_scalar(Q.qa(s, b), m.bank[s][b % 2][:, :], Q.sm(s, 7, b), 127.0,
                                        ALU.mult, ALU.min))
        yield Q.time(b, 0.6)
        after("q1")
        step("q2", dve.tensor_scalar(Q.qa(s, b), Q.qa(s, b), -128.0, ROUND, ALU.max, ALU.add))
        yield Q.time(b, 0.7)
        after("q2")
        if b >= 2:
            dve.wait_ge(*g.at("qf_pe", ("back", b - 2)))
        step("q3", dve.tensor_scalar(Q.qb(s, b), Q.qa(s, b), ROUND, None, ALU.subtract))
    yield 0.96
    dve.reciprocal(Q.sm(s, 8), Q.sm(s, 7)).then_inc(*g.one("qf_d", "inv2"))
    dve.wait_ge(*g.at("qf_d", "inv2"))
    dve.tensor_scalar(Q.sm(s, 8), Q.sm(s, 8), m.wsc[:, 3:4], None, ALU.mult).then_inc(*g.one("qf_d", "f"))
    yield 0.99
    dve.wait_ge(*g.at("qf_d", "f"))
    dve.wait_ge(*g.at("qf_pe", "out"))
    for b in range(NB):
        last = dve.scalar_tensor_tensor(out=m.x[s][:, b, :], in0=m.bank[s][3][:, b * D:(b + 1) * D],
                                        scalar=Q.sm(s, 8, b), in1=m.x[s][:, b, :], op0=ALU.mult, op1=ALU.add)
    last.then_inc(*g.one("x_upd", "L3f"))



class Gauge:

    def __init__(self, m, numbers, s):
        self.m, self.numbers, self.s = m, numbers, s
        self.i, self.ahead = None, 0
        self.before = None
        self.made = {}
        self.free = {}

    def start(self, i, ahead, before):
        self.i, self.ahead, self.before = i, ahead, before
        if before is None:
            self.made, self.free = {}, {}

    def at(self, signal, name):
        return self.m.sem[self.s][signal], self.numbers.value(signal, name, self.i, self.ahead)

    def one(self, signal, name):
        self.made[signal] = self.made.get(signal, 0) + 1
        self.numbers.count(signal, name, self.made[signal])
        return self.m.sem[self.s][signal], 1

    def loads(self):
        return self.i * 16 + (self.ahead * 16 + 16)

    def context_at(self):
        return self.m.s_ctx[self.s], self.loads()

    def mask_at(self):
        return self.m.s_mask[self.s], self.loads()

    def wait_free(self, pe, free, s, k):
        if (s, k) in free:
            pe.wait_ge(*self.at(*free[s, k]))


ORDER = ["L0a", "L0x", "L0f", "L1a", "L1x", "L1f", "L2a", "L2x", "L2f", "L3a", "L3x", "L3f"][:LAST]
SPAN = {"L0a": 94, "L0x": 32, "L0f": 90, "L1a": 151, "L1x": 107, "L1f": 135, "L2a": 345, "L2x": 160,
        "L2f": 32, "L3a": 120, "L3x": 145, "L3f": 74}
NORM_SPAN = 13
CUT0, CUT1 = 5, 7


def in_turn(first, second):
    streams = [first, second]
    due = [next(st, None) for st in streams]
    while due != [None, None]:
        s = min((t, s) for s, t in enumerate(due) if t is not None)[1]
        due[s] = next(streams[s], None)


def last_step(m, key):
    if key in ("L0f", "L1f"):
        return "dn_d", (key, E - 1)
    if key == "L2f":
        return "dn_d", (key, 1)
    if key in ("L2a", "L3f"):
        return "x_upd", key
    return "x_upd", (key, Attention(m, key).blocks - 1)


def run_sublayers(engine, m, g, keys, i, ahead, sublayer):
    start = now = 0.0
    for key in keys:
        n = ORDER.index(key)
        own = i
        if not isinstance(i, int):
            reg = engine.alloc_register()
            engine.reg_mov(reg, i)
            own = engine.snap(reg, min_val=0, max_val=PASSES - 2)
        g.start(own, ahead, last_step(m, ORDER[n - 1]) if n else None)
        for t in sublayer(g, key):
            now = max(now, start + (NORM_SPAN * t / 0.05 if t < 0.05 else
                                    NORM_SPAN + (SPAN[key] - NORM_SPAN) * (t - 0.05) / 0.95))
            yield now
        start += SPAN[key]


def run_passes(engine, m, numbers, sublayer):
    g = [Gauge(m, numbers, s) for s in range(STREAMS)]
    early, late = (ORDER[:CUT0], ORDER[CUT0:]), (ORDER[:CUT1], ORDER[CUT1:])

    def part(first, second):
        in_turn(run_sublayers(engine, m, g[0], *first, sublayer),
                run_sublayers(engine, m, g[1], *second, sublayer))

    part((early[0], 0, 0), ([], 0, 0))
    with engine.Fori(0, PASSES - 1) as i:
        part((early[1], i, 0), (late[0], i, 0))
        part((early[0], i, 1), (late[1], i, 0))
    part((early[1], PASSES - 1, 0), (late[0], PASSES - 1, 0))
    part(([], 0, 0), (late[1], PASSES - 1, 0))


def write_program(nc, m, numbers):
    A = {key: Attention(m, key) for key in ("L0a", "L0x", "L1a", "L1x", "L2x", "L3a", "L3x")}
    R = {key: Router(m, key) for key in ("L0f", "L1f", "L2f")}
    X = {key: Experts(m, key) for key in ("L0f", "L1f")}
    M = Mamba(m)
    Q = Quantised(m)
    at = m.cols["const"][1]
    m.const = {n: m.W["const"][:, a:a + width] for n, (a, width) in at.items()}
    inner = [t[:, :].rearrange("p (b d) -> p b d", d=D) for t in m.xT]
    quantised = [Q.xq(s) for s in range(STREAMS)]

    with nc.Block() as block:

        @block.tensor
        def _(pe):
            def sublayer(g, key):
                free = g.free
                pe.wait_ge(m.s_w[key], 16)
                if key in A:
                    yield from attention_early_pe(pe, g, m, A[key], free)
                yield from turn_pe(pe, g, m, key, inner if key in NESTED else quantised if key == "L3f" else m.xn,
                                   free)
                if key in R:
                    yield from router_pe(pe, g, m, R[key], free)
                if key in A:
                    yield from attention_pe(pe, g, m, A[key], free)
                if key in X:
                    yield from experts_pe(pe, g, m, X[key], free)
                if key == "L2a":
                    yield from mamba_pe(pe, g, m, M, free)
                if key == "L2f":
                    yield from maps_pe(pe, g, m, free)
                if key == "L3f":
                    yield from quantised_pe(pe, g, m, Q, free)

            setup_pe(pe, m)
            run_passes(pe, m, numbers, sublayer)

        @block.scalar
        def _(act):
            def sublayer(g, key):
                act.wait_ge(m.s_w[key], 16)
                if key in A:
                    yield from attention_early_act(act, g, m, A[key])
                if key in NESTED:
                    gain, shift = (m.W[key][:, a:a + 1] for a, _ in (m.cols[key][1]["g"], m.cols[key][1]["b"]))
                    yield from turn_act(act, g, m, key, gain, shift)
                else:
                    yield from turn_act(act, g, m, key)
                if key in A:
                    yield from attention_act(act, g, m, A[key])
                if key in R:
                    yield from router_act(act, g, m, R[key])
                if key in X:
                    yield from experts_act(act, g, m, X[key])
                if key == "L2a":
                    yield from mamba_act(act, g, m, M)
                if key == "L2f":
                    yield from maps_act(act, g, m)
                if key == "L3f":
                    yield from quantised_act(act, g, m, Q)

            setup_act(act, m)
            run_passes(act, m, numbers, sublayer)

        @block.vector
        def _(dve):
            def sublayer(g, key):
                dve.wait_ge(m.s_w[key], 16)
                base = m.xin if key == "L0a" else m.x
                yield from norm_dve(dve, g, m, key, base, m.xn)
                if key in NESTED:
                    yield from norm_dve(dve, g, m, key + "i", m.xn, inner, made=key)
                if key == "L3f":
                    yield from quantise_tokens_dve(dve, g, m, Q)
                if key == "L1x":
                    mask_dve(dve, g, m)
                if key in A:
                    yield from attention_dve(dve, g, m, A[key], base)
                if key in R:
                    yield from router_dve(dve, g, m, R[key])
                if key in X:
                    yield from experts_dve(dve, g, m, X[key])
                if key == "L2a":
                    yield from mamba_dve(dve, g, m, M)
                if key == "L2f":
                    yield from maps_dve(dve, g, m)
                if key == "L3f":
                    yield from quantised_dve(dve, g, m, Q)

            setup_dve(dve, m)
            run_passes(dve, m, numbers, sublayer)

        @block.gpsimd
        def _(pool):
            def sublayer(g, key):
                yield from norm_pool(pool, g, m, key)
                if key in NESTED:
                    yield from norm_pool(pool, g, m, key + "i")
                if key in A:
                    yield from attention_pool(pool, g, m, A[key])
                if key == "L2a":
                    yield from mamba_pool(pool, g, m, M)
                if key == "L3f":
                    yield from quantised_pool(pool, g, m, Q)

            setup_pool(pool, m)
            run_passes(pool, m, numbers, sublayer)

        @block.sync
        def _(sp):
            def load_x(i, s):
                lo = (i * STREAMS + s) * NB
                sp.dma_start(m.xin[s][:, :, :], m.ins["x"][lo:lo + NB].rearrange("b t d -> t b d"))\
                  .then_inc(m.s_xin[s], 16)

            def load_context(i, s):
                lo = (i * STREAMS + s) * NB
                sp.dma_start(m.ctxT[s][:, :], m.ins["ctxT"][:, lo * C:(lo + NB) * C]).then_inc(m.s_ctx[s], 16)
                sp.dma_start(m.mask8[:, s, :], m.ins["mask"][:, lo * C:(lo + NB) * C]).then_inc(m.s_mask[s], 16)

            sp.dma_start(m.W["const"][:, :], m.ins["w_const"]).then_inc(m.s_w["const"], 16)
            sp.dma_start(raw_bias_rows(m), m.ins["rows"]).then_inc(m.s_rows, 16)
            for key in ("L3f", "L0a", "L2a"):
                if key == "L0a":
                    for s in range(STREAMS):
                        load_x(0, s)
                        load_context(0, s)
                sp.dma_start(m.W[key][:, :], m.ins["w_" + key]).then_inc(m.s_w[key], 16)
            for key in [key for key in m.W if key not in ("const", "L3f", "L0a", "L2a")]:
                sp.dma_start(m.W[key][:, :], m.ins["w_" + key]).then_inc(m.s_w[key], 16)
            g = [Gauge(m, numbers, s) for s in range(STREAMS)]
            for i in range(PASSES):
                for s in range(STREAMS):
                    g[s].start(i, 0, None)
                    if i + 1 < PASSES:
                        sp.wait_ge(*g[s].at("x_upd", ("L0a", 0)))
                        load_x(i + 1, s)
                for s in range(STREAMS):
                    lo = (i * STREAMS + s) * NB
                    sp.wait_ge(*g[s].at(*last_step(m, ORDER[-1])))
                    sp.dma_start(m.out[lo:lo + NB].rearrange("b t d -> t b d"), m.x[s][:, :, :])\
                      .then_inc(m.s_out[s], 16)
                    sp.wait_ge(m.s_out[s], 16 * (i + 1))
                    if i + 1 < PASSES:
                        load_context(i + 1, s)


def build(nc, ins, out, cols, rows, known):
    with ExitStack() as ctx:
        m = declare(nc, ins, out, cols, rows, ctx)
        numbers = Numbers(known)
        write_program(nc, m, numbers)
    return numbers.known


def raw_bias_rows(m):
    return cut(m.big[1], 0, 128)[0:96]


def setup_pe(pe, m):
    pe.wait_ge(m.s_w["const"], 16)
    pe.wait_ge(m.s_pre_d, 5)
    pe.matmul(m.bank[0][0][:, 0:2], m.const["ones"], m.wsc[:, 0:2], start=True, stop=True).then_inc(m.s_pre_pe, 1)
    pe.wait_ge(m.s_pre_d, PRE_D)


def setup_act(act, m):
    act.wait_ge(m.s_w["const"], 16)
    act.wait_ge(m.s_w["L2a"], 16)
    at = m.cols["L2a"][1]["alog"][0]
    act.activation(m.Aneg[:, :], m.W["L2a"][:, at:at + 2 * NS], ACT.Exp).then_inc(m.s_pre_a, 1)
    act.wait_ge(m.s_pre_a, 1)
    act.activation(m.Aneg[:, :], m.Aneg[:, :], ACT.Copy, scale=-1.0).then_inc(m.s_pre_a, 1)
    act.wait_ge(m.s_pre_a, 2)


def setup_dve(dve, m):
    dve.wait_ge(m.s_w["const"], 16)
    ident = m.const["ident"]
    dve.tensor_tensor(m.sel3[0:32, :], ident[0:32, 0:32], ident[0:32, 32:64], ALU.add)
    dve.tensor_tensor(m.sel3[32:64, :], ident[32:64, 32:64], ident[32:64, 0:32], ALU.add)
    dve.tensor_tensor(m.sel3[64:96, :], ident[64:96, 64:96], ident[64:96, 0:32], ALU.add)
    dve.tensor_copy(m.causalb[:, :], m.const["causal"])
    dve.tensor_copy(m.identb[:, :], ident).then_inc(m.s_pre_d, 1)

    dve.wait_ge(m.s_w["L3f"], 16)
    col = m.cols["L3f"][1]
    w = [m.W["L3f"][:, col[n][0]:col[n][0] + HID] for n in ("w1", "w2")]
    made = 1
    for k in range(2):
        t = cut(m.big[0], 512 * k, HID)
        dve.scalar_tensor_tensor(out=t, in0=w[k], scalar=-1.0, in1=w[k], op0=ALU.mult, op1=ALU.max)\
           .then_inc(m.s_pre_d, 1)
        dve.wait_ge(m.s_pre_d, made + 1)
        dve.tensor_reduce(m.wsc[:, k:k + 1], t, AX.X, ALU.add).then_inc(m.s_pre_d, 1)
        made += 2
    dve.wait_ge(m.s_pre_pe, 1)
    dve.tensor_scalar(m.wsc[:, 2:4], m.bank[0][0][:, 0:2], 1.0 / (D * HID), 1e-5, ALU.mult, ALU.max)\
       .then_inc(m.s_pre_d, 1)
    dve.wait_ge(m.s_pre_d, made + 1)
    dve.reciprocal(m.wsc[:, 4:6], m.wsc[:, 2:4]).then_inc(m.s_pre_d, 1)
    dve.wait_ge(m.s_pre_d, made + 2)
    made += 2
    for k in range(2):
        dve.tensor_scalar(w[k], w[k], m.wsc[:, 4 + k:5 + k], ROUND, ALU.mult, ALU.add).then_inc(m.s_pre_d, 1)
        dve.wait_ge(m.s_pre_d, made + 1)
        dve.tensor_scalar(w[k], w[k], ROUND, 1.0, ALU.subtract, ALU.min).then_inc(m.s_pre_d, 1)
        dve.wait_ge(m.s_pre_d, made + 2)
        if k == 0:
            dve.tensor_scalar(w[0], w[0], -1.0, m.wsc[:, 2:3], ALU.max, ALU.mult).then_inc(m.s_pre_d, 1)
        else:
            dve.tensor_scalar(m.w2t[:, :], w[1], -1.0, None, ALU.max).then_inc(m.s_pre_d, 1)
        made += 3
    raw, parts = raw_bias_rows(m), m.brow3
    mid = cut(m.big[1], 128, 64).bitcast(BF16)[0:96]
    dve.wait_ge(m.s_rows, 16)
    dve.tensor_copy(parts[0:96, :], raw).then_inc(m.s_pre_d, 1)
    dve.wait_ge(m.s_pre_d, made + 1)
    dve.tensor_tensor(raw, raw, parts[0:96, :], ALU.subtract).then_inc(m.s_pre_d, 1)
    dve.wait_ge(m.s_pre_d, made + 2)
    dve.tensor_copy(mid, raw).then_inc(m.s_pre_d, 1)
    dve.wait_ge(m.s_pre_d, made + 3)
    dve.tensor_copy(parts[32:64, :], mid[32:64])
    dve.tensor_tensor(parts[64:96, :], raw[64:96], mid[64:96], ALU.subtract).then_inc(m.s_pre_d, 1)
    assert made + 4 == PRE_D


def setup_pool(pool, m):
    pool.wait_ge(m.s_w["const"], 16)



def kernel(**inputs):
    import concourse.bacc as bacc
    from concourse.bass_utils import run_bass_kernel_spmd

    w = {k: np.asarray(v) for k, v in inputs.items()}
    blocks = layouts(w)
    arrays, cols = {}, {}
    for st, parts in blocks.items():
        at, where = 0, {}
        for name, a in parts.items():
            assert a.shape[0] == 128, (st, name, a.shape)
            where[name] = (at, a.shape[1])
            at += a.shape[1]
        cols[st] = (at, where)
        arrays["w_" + st] = np.ascontiguousarray(np.concatenate(list(parts.values()), axis=1))
    rows, stack = {}, []
    for name, a in bias_rows(w).items():
        rows[name] = len(stack)
        stack += list(a.reshape(-1, 128))
    third = rows_below(np.stack(stack))[:32]
    arrays["rows"] = np.concatenate([third, third, third])
    arrays["x"] = np.ascontiguousarray(w["x"])
    arrays["ctxT"] = np.ascontiguousarray(w["ctx_1024"].transpose(2, 0, 1).reshape(D, B * C))
    arrays["mask"] = np.ascontiguousarray(
        np.broadcast_to(w["mask_BxS2_bk0"].reshape(1, B * C), (128, B * C)))

    known = None
    for _ in range(2):
        nc = bacc.Bacc("TRN2", target_bir_lowering=False, num_devices=1)
        ins = {n: nc.dram_tensor(n, a.shape, U8 if n == "mask" else F32, kind="ExternalInput").ap()
               for n, a in arrays.items()}
        out = nc.dram_tensor("out", (B, T, D), F32, kind="ExternalOutput").ap()
        known = build(nc, ins, out, cols, rows, known)
    r = run_bass_kernel_spmd(nc, [arrays], core_ids=[0])
    return r.results[0]["out"]
```
